# Optimizing a Trainium2 kernel written in Bass

```python
import numpy as np
import jax
import jax.numpy as jnp

def _softmax(x, axis=-1):
    return jax.nn.softmax(x, axis=axis)

def _gelu(x):
    return jax.nn.gelu(x, approximate=True)

def _silu(x):
    return jax.nn.silu(x)

def _sigmoid(x):
    return jax.nn.sigmoid(x)

def _layernorm(x, axis=-1, eps=1e-05):
    m = jnp.mean(x, axis=axis, keepdims=True)
    v = jnp.var(x, axis=axis, keepdims=True)
    return (x - m) / jnp.sqrt(v + eps)

def _scatter_add(tgt, idx, src, axis=0):
    return tgt.at[idx].add(src)

def _segment_sum(src, seg, n):
    return jax.ops.segment_sum(src, seg, n)
kernel_name = 'mk_gnn_resnorm_d4_gnn_r64_679e37'

def setup_inputs(seed: int=0):
    np.random.seed(seed)
    _w = jnp.asarray

    def _rec_inputs():
        import jax
        import jax.numpy as jnp
        _gk = jax.random.key(seed)
        x = -8.776e-05 + 1 * jax.random.normal(jax.random.fold_in(_gk, 1), (20000, 256), jnp.float32)
        src = jax.random.randint(jax.random.fold_in(_gk, 2), (5000,), 0, 20000, jnp.int32)
        dst = jnp.minimum((20000 * jax.random.uniform(jax.random.fold_in(_gk, 3), (5000,)) ** 2.0).astype(jnp.int32), 19999)
        _o = jnp.argsort(dst, stable=True)
        src = src[_o]
        dst = dst[_o]
        edge_attr_64 = 0.000189758 + 1.00013 * jax.random.normal(jax.random.fold_in(_gk, 11), (5000, 64), jnp.float32)
        return (x, src, dst, edge_attr_64)
    x, src, dst, edge_attr_64 = _rec_inputs()

    def _L0_gnn_setup():
        import jax, jax.numpy as jnp
        import numpy as np
        N = 20000
        E = 5000
        IN = 256
        H = 4
        C = 64
        D = H * C
        LN_EPS = 1e-05
        key = jax.random.key(seed)
        ks = jax.random.split(key, 8)
        w = lambda k, sh: jax.random.normal(k, sh, jnp.float32) * 0.05
        return {'x': jax.random.normal(ks[0], (N, IN), jnp.float32), 'edge_index': jax.random.randint(ks[1], (2, E), 0, N, dtype=jnp.int32), 'Wq': w(ks[2], (IN, D)), 'bq': jnp.zeros((D,), jnp.float32), 'Wk': w(ks[3], (IN, D)), 'bk': jnp.zeros((D,), jnp.float32), 'Wv': w(ks[4], (IN, D)), 'bv': jnp.zeros((D,), jnp.float32), 'Wskip': w(ks[5], (IN, D)), 'bskip': jnp.zeros((D,), jnp.float32), 'gamma': jnp.ones((D,), jnp.float32), 'beta_ln': jnp.zeros((D,), jnp.float32)}
    _L0_gnn_all = _L0_gnn_setup()
    _L0_gnn_in = {k: v for k, v in _L0_gnn_all.items() if k in ('Wq', 'bq', 'Wk', 'bk', 'Wv', 'bv', 'Wskip', 'bskip', 'gamma', 'beta_ln')}
    del _L0_gnn_all

    def _L1_gnn_setup():
        import jax, jax.numpy as jnp
        import numpy as np
        N, E = (50000, 12500)
        HID, EDIM, HEADS = (256, 64, 8)
        C = HID // HEADS
        NEG_SLOPE = 0.2
        LN_EPS = 1e-05

        def _gat_block(x, edge_index, edge_attr, W, W_e, att_src, att_dst, att_edge, bias, gamma, beta):
            n = x.shape[0]
            src, dst = (edge_index[0], edge_index[1])
            xp = (x @ W).reshape(n, HEADS, C)
            a_src = jnp.einsum('nhc,hc->nh', xp, att_src)
            a_dst = jnp.einsum('nhc,hc->nh', xp, att_dst)
            ep = (edge_attr @ W_e).reshape(-1, HEADS, C)
            a_edge = jnp.einsum('ehc,hc->eh', ep, att_edge)
            alpha = a_src[src] + a_dst[dst] + a_edge
            alpha = jax.nn.leaky_relu(alpha, NEG_SLOPE)
            m = jax.ops.segment_max(alpha, dst, num_segments=n)
            m = jnp.where(jnp.isfinite(m), m, 0.0)
            ea = jnp.exp(alpha - m[dst])
            den = jax.ops.segment_sum(ea, dst, num_segments=n)
            attn = ea / (den[dst] + 1e-16)
            msg = xp[src] * attn[:, :, None]
            out = jax.ops.segment_sum(msg, dst, num_segments=n)
            h = out.reshape(n, HEADS * C) + bias
            y = x + h
            mu = jnp.mean(y, axis=-1, keepdims=True)
            var = jnp.var(y, axis=-1, keepdims=True)
            return (y - mu) * jax.lax.rsqrt(var + LN_EPS) * gamma + beta
        key = jax.random.key(seed)
        ks = jax.random.split(key, 12)
        s = 1.0 / np.sqrt(HID)
        se = 1.0 / np.sqrt(EDIM)
        return {'x': jax.random.normal(ks[0], (N, HID), jnp.float32), 'edge_index': jax.random.randint(ks[1], (2, E), 0, N, jnp.int32), 'edge_attr': jax.random.normal(ks[2], (E, EDIM), jnp.float32), 'W': jax.random.uniform(ks[3], (HID, HEADS * C), jnp.float32, -s, s), 'W_e': jax.random.uniform(ks[4], (EDIM, HEADS * C), jnp.float32, -se, se), 'att_src': jax.random.normal(ks[5], (HEADS, C), jnp.float32) * 0.1, 'att_dst': jax.random.normal(ks[6], (HEADS, C), jnp.float32) * 0.1, 'att_edge': jax.random.normal(ks[7], (HEADS, C), jnp.float32) * 0.1, 'bias': jnp.zeros((HEADS * C,), jnp.float32), 'gamma': jnp.ones((HID,), jnp.float32), 'beta': jnp.zeros((HID,), jnp.float32)}
    _L1_gnn_all = _L1_gnn_setup()
    _L1_gnn_in = {k: v for k, v in _L1_gnn_all.items() if k in ('W', 'W_e', 'att_src', 'att_dst', 'att_edge', 'bias', 'gamma', 'beta')}
    del _L1_gnn_all

    def _L2_gnn_setup():
        import jax, jax.numpy as jnp
        import numpy as np
        N_NODES = 50000
        N_EDGES = 12500
        IN_CH = 256
        HID_CH = 256
        OUT_CH = 256
        N_LAYERS = 3
        key = jax.random.key(seed)
        ks = jax.random.split(key, 8)
        s_in = 1.0 / np.sqrt(IN_CH)
        s_h = 1.0 / np.sqrt(HID_CH)
        return {'x': jax.random.normal(ks[0], (N_NODES, IN_CH), dtype=jnp.float32), 'W_in': jax.random.normal(ks[1], (IN_CH, HID_CH), dtype=jnp.float32) * s_in, 'b_in': jnp.zeros((HID_CH,), dtype=jnp.float32), 'W_agg': jax.random.normal(ks[2], (N_LAYERS, HID_CH, HID_CH), dtype=jnp.float32) * s_h, 'W_self': jax.random.normal(ks[3], (N_LAYERS, HID_CH, HID_CH), dtype=jnp.float32) * s_h, 'b_hid': jnp.zeros((N_LAYERS, HID_CH), dtype=jnp.float32), 'W_out': jax.random.normal(ks[4], (HID_CH, OUT_CH), dtype=jnp.float32) * s_h, 'b_out': jnp.zeros((OUT_CH,), dtype=jnp.float32), 'edge_index': jax.random.randint(ks[5], (2, N_EDGES), 0, N_NODES, dtype=jnp.int64)}
    _L2_gnn_all = _L2_gnn_setup()
    _L2_gnn_in = {k: v for k, v in _L2_gnn_all.items() if k in ('W_in', 'b_in', 'W_agg', 'W_self', 'b_hid', 'W_out', 'b_out')}
    del _L2_gnn_all

    def _L3_gnn_setup():
        import jax, jax.numpy as jnp
        import numpy as np
        N_NODES = 50000

        def _gcn_layer(h_in, W, b, src, dst, norm_edge, n_nodes):
            h = h_in @ W
            msg = h[src] * norm_edge[:, None]
            agg = jax.ops.segment_sum(msg, dst, num_segments=n_nodes)
            return agg + b
        key = jax.random.key(seed)
        ks = jax.random.split(key, 8)
        n, c_in, c_out = (N_NODES, 256, 256)
        hid = 2 * c_out
        E = 12500
        x = jax.random.normal(ks[0], (n, c_in), dtype=jnp.float32)
        edge_index = jax.random.randint(ks[1], (2, E), 0, n, dtype=jnp.int64)

        def glorot(k, fan_in, fan_out):
            s = jnp.sqrt(6.0 / (fan_in + fan_out)).astype(jnp.float32)
            return jax.random.uniform(k, (fan_in, fan_out), jnp.float32, -s, s)
        return {'x': x, 'edge_index': edge_index, 'W1': glorot(ks[2], c_in, hid), 'b1': jnp.zeros((hid,), jnp.float32), 'W2': glorot(ks[3], hid, hid), 'b2': jnp.zeros((hid,), jnp.float32), 'W3': glorot(ks[4], hid, c_out), 'b3': jnp.zeros((c_out,), jnp.float32)}
    _L3_gnn_all = _L3_gnn_setup()
    _L3_gnn_in = {k: v for k, v in _L3_gnn_all.items() if k in ('W1', 'b1', 'W2', 'b2', 'W3', 'b3')}
    del _L3_gnn_all
    return {'x': x, 'src': src, 'dst': dst, 'edge_attr_64': edge_attr_64, 'L0_gnn_Wq': _L0_gnn_in['Wq'], 'L0_gnn_bq': _L0_gnn_in['bq'], 'L0_gnn_Wk': _L0_gnn_in['Wk'], 'L0_gnn_bk': _L0_gnn_in['bk'], 'L0_gnn_Wv': _L0_gnn_in['Wv'], 'L0_gnn_bv': _L0_gnn_in['bv'], 'L0_gnn_Wskip': _L0_gnn_in['Wskip'], 'L0_gnn_bskip': _L0_gnn_in['bskip'], 'L0_gnn_gamma': _L0_gnn_in['gamma'], 'L0_gnn_beta_ln': _L0_gnn_in['beta_ln'], 'L1_gnn_W': _L1_gnn_in['W'], 'L1_gnn_W_e': _L1_gnn_in['W_e'], 'L1_gnn_att_src': _L1_gnn_in['att_src'], 'L1_gnn_att_dst': _L1_gnn_in['att_dst'], 'L1_gnn_att_edge': _L1_gnn_in['att_edge'], 'L1_gnn_bias': _L1_gnn_in['bias'], 'L1_gnn_gamma': _L1_gnn_in['gamma'], 'L1_gnn_beta': _L1_gnn_in['beta'], 'L2_gnn_W_in': _L2_gnn_in['W_in'], 'L2_gnn_b_in': _L2_gnn_in['b_in'], 'L2_gnn_W_agg': _L2_gnn_in['W_agg'], 'L2_gnn_W_self': _L2_gnn_in['W_self'], 'L2_gnn_b_hid': _L2_gnn_in['b_hid'], 'L2_gnn_W_out': _L2_gnn_in['W_out'], 'L2_gnn_b_out': _L2_gnn_in['b_out'], 'L3_gnn_W1': _L3_gnn_in['W1'], 'L3_gnn_b1': _L3_gnn_in['b1'], 'L3_gnn_W2': _L3_gnn_in['W2'], 'L3_gnn_b2': _L3_gnn_in['b2'], 'L3_gnn_W3': _L3_gnn_in['W3'], 'L3_gnn_b3': _L3_gnn_in['b3']}

def reference(x, src, dst, edge_attr_64, L0_gnn_Wq, L0_gnn_bq, L0_gnn_Wk, L0_gnn_bk, L0_gnn_Wv, L0_gnn_bv, L0_gnn_Wskip, L0_gnn_bskip, L0_gnn_gamma, L0_gnn_beta_ln, L1_gnn_W, L1_gnn_W_e, L1_gnn_att_src, L1_gnn_att_dst, L1_gnn_att_edge, L1_gnn_bias, L1_gnn_gamma, L1_gnn_beta, L2_gnn_W_in, L2_gnn_b_in, L2_gnn_W_agg, L2_gnn_W_self, L2_gnn_b_hid, L2_gnn_W_out, L2_gnn_b_out, L3_gnn_W1, L3_gnn_b1, L3_gnn_W2, L3_gnn_b2, L3_gnn_W3, L3_gnn_b3):
    import jax
    import jax.numpy as jnp

    def _L0_gnn_ref(x, edge_index, Wq, bq, Wk, bk, Wv, bv, Wskip, bskip, gamma, beta_ln):
        import jax, jax.numpy as jnp
        import numpy as np
        N = 20000
        E = 5000
        IN = 256
        H = 4
        C = 64
        D = H * C
        LN_EPS = 1e-05
        src = edge_index[0]
        dst = edge_index[1]
        q = (x @ Wq + bq).reshape(N, H, C)
        k = (x @ Wk + bk).reshape(N, H, C)
        v = (x @ Wv + bv).reshape(N, H, C)
        scale = 1.0 / jnp.sqrt(jnp.float32(C))
        alpha = jnp.einsum('ehc,ehc->eh', q[dst], k[src]) * scale
        m = jax.ops.segment_max(alpha, dst, num_segments=N)
        m = jnp.where(jnp.isfinite(m), m, 0.0)
        a = jnp.exp(alpha - m[dst])
        denom = jax.ops.segment_sum(a, dst, num_segments=N)
        a = a / (denom[dst] + 1e-16)
        msg = a[:, :, None] * v[src]
        agg = jax.ops.segment_sum(msg, dst, num_segments=N)
        out = agg.reshape(N, D) + (x @ Wskip + bskip)
        out = jax.nn.gelu(out, approximate=False)
        mu = jnp.mean(out, axis=-1, keepdims=True)
        var = jnp.var(out, axis=-1, keepdims=True)
        out = (out - mu) * jax.lax.rsqrt(var + LN_EPS) * gamma + beta_ln
        return out

    def _L1_gnn_ref(x, edge_index, edge_attr, W, W_e, att_src, att_dst, att_edge, bias, gamma, beta):
        import jax, jax.numpy as jnp
        import numpy as np
        N, E = (50000, 12500)
        HID, EDIM, HEADS = (256, 64, 8)
        C = HID // HEADS
        NEG_SLOPE = 0.2
        LN_EPS = 1e-05

        def _gat_block(x, edge_index, edge_attr, W, W_e, att_src, att_dst, att_edge, bias, gamma, beta):
            n = x.shape[0]
            src, dst = (edge_index[0], edge_index[1])
            xp = (x @ W).reshape(n, HEADS, C)
            a_src = jnp.einsum('nhc,hc->nh', xp, att_src)
            a_dst = jnp.einsum('nhc,hc->nh', xp, att_dst)
            ep = (edge_attr @ W_e).reshape(-1, HEADS, C)
            a_edge = jnp.einsum('ehc,hc->eh', ep, att_edge)
            alpha = a_src[src] + a_dst[dst] + a_edge
            alpha = jax.nn.leaky_relu(alpha, NEG_SLOPE)
            m = jax.ops.segment_max(alpha, dst, num_segments=n)
            m = jnp.where(jnp.isfinite(m), m, 0.0)
            ea = jnp.exp(alpha - m[dst])
            den = jax.ops.segment_sum(ea, dst, num_segments=n)
            attn = ea / (den[dst] + 1e-16)
            msg = xp[src] * attn[:, :, None]
            out = jax.ops.segment_sum(msg, dst, num_segments=n)
            h = out.reshape(n, HEADS * C) + bias
            y = x + h
            mu = jnp.mean(y, axis=-1, keepdims=True)
            var = jnp.var(y, axis=-1, keepdims=True)
            return (y - mu) * jax.lax.rsqrt(var + LN_EPS) * gamma + beta
        return _gat_block(x, edge_index, edge_attr, W, W_e, att_src, att_dst, att_edge, bias, gamma, beta)

    def _L2_gnn_ref(x, W_in, b_in, W_agg, W_self, b_hid, W_out, b_out, edge_index):
        import jax, jax.numpy as jnp
        import numpy as np
        N_NODES = 50000
        N_EDGES = 12500
        IN_CH = 256
        HID_CH = 256
        OUT_CH = 256
        N_LAYERS = 3
        n = x.shape[0]
        dst = edge_index[0]
        src = edge_index[1]
        n_layers = W_agg.shape[0]
        h = x @ W_in + b_in
        deg = jax.ops.segment_sum(jnp.ones_like(dst, dtype=h.dtype), dst, num_segments=n)
        deg = jnp.maximum(deg, 1.0)[:, None]
        for l in range(n_layers):
            agg = jax.ops.segment_sum(h[src], dst, num_segments=n) / deg
            h = jax.nn.relu(agg @ W_agg[l] + h @ W_self[l] + b_hid[l])
        return h @ W_out + b_out

    def _L3_gnn_ref(x, edge_index, W1, b1, W2, b2, W3, b3):
        import jax, jax.numpy as jnp
        import numpy as np
        N_NODES = 50000

        def _gcn_layer(h_in, W, b, src, dst, norm_edge, n_nodes):
            h = h_in @ W
            msg = h[src] * norm_edge[:, None]
            agg = jax.ops.segment_sum(msg, dst, num_segments=n_nodes)
            return agg + b
        n = x.shape[0]
        loops = jnp.arange(n, dtype=edge_index.dtype)
        src = jnp.concatenate([edge_index[0], loops])
        dst = jnp.concatenate([edge_index[1], loops])
        deg = jax.ops.segment_sum(jnp.ones_like(dst, dtype=x.dtype), dst, num_segments=n)
        dinv = jnp.where(deg > 0, jax.lax.rsqrt(deg), 0.0)
        norm_edge = dinv[src] * dinv[dst]
        h = x
        for W, b in ((W1, b1), (W2, b2), (W3, b3)):
            h = jax.nn.relu(_gcn_layer(h, W, b, src, dst, norm_edge, n))
        return h
    edge_index = jnp.stack([src, dst])
    x = _layernorm(x + _L0_gnn_ref(x, edge_index, L0_gnn_Wq, L0_gnn_bq, L0_gnn_Wk, L0_gnn_bk, L0_gnn_Wv, L0_gnn_bv, L0_gnn_Wskip, L0_gnn_bskip, L0_gnn_gamma, L0_gnn_beta_ln), axis=-1)
    x = _layernorm(x + _L1_gnn_ref(x, edge_index, edge_attr_64, L1_gnn_W, L1_gnn_W_e, L1_gnn_att_src, L1_gnn_att_dst, L1_gnn_att_edge, L1_gnn_bias, L1_gnn_gamma, L1_gnn_beta), axis=-1)
    x = _layernorm(x + _L2_gnn_ref(x, L2_gnn_W_in, L2_gnn_b_in, L2_gnn_W_agg, L2_gnn_W_self, L2_gnn_b_hid, L2_gnn_W_out, L2_gnn_b_out, edge_index), axis=-1)
    x = _layernorm(x + _L3_gnn_ref(x, edge_index, L3_gnn_W1, L3_gnn_b1, L3_gnn_W2, L3_gnn_b2, L3_gnn_W3, L3_gnn_b3), axis=-1)
    return x

_drawn_inputs = setup_inputs


def setup_inputs(seed=0):
    import zlib

    import numpy as np

    out = dict(_drawn_inputs(seed))
    spreads = {'L0_gnn_bq': (0.0, 0.8),
     'L0_gnn_bk': (0.0, 2.0),
     'L0_gnn_bv': (0.0, 0.1),
     'L0_gnn_bskip': (0.0, 0.1),
     'L0_gnn_gamma': (1.0, 0.2),
     'L0_gnn_beta_ln': (0.0, 0.1),
     'L1_gnn_bias': (0.0, 0.1),
     'L1_gnn_gamma': (1.0, 0.2),
     'L1_gnn_beta': (0.0, 0.1),
     'L2_gnn_b_in': (0.0, 0.1),
     'L2_gnn_b_hid': (0.0, 0.1),
     'L2_gnn_b_out': (0.0, 0.1),
     'L3_gnn_b1': (0.0, 0.1),
     'L3_gnn_b2': (0.0, 0.1),
     'L3_gnn_b3': (0.0, 0.1)}
    factors = {'edge_attr_64': 8.0,
     'L1_gnn_W_e': 8.0,
     'L1_gnn_att_src': 200.0,
     'L1_gnn_att_dst': 200.0,
     'L1_gnn_att_edge': 8.0}
    for name, (base, spread) in spreads.items():
        noise = np.random.default_rng([zlib.crc32(name.encode()), seed]).standard_normal(out[name].shape)
        drawn = base * np.exp(spread * noise) if base else spread * noise
        out[name] = jnp.asarray(drawn.astype(out[name].dtype))
    for name, factor in factors.items():
        out[name] = (out[name] * factor).astype(out[name].dtype)
    return out
```

```python
from contextlib import ExitStack

import concourse.bass as bass
from concourse import mybir

F32 = mybir.dt.float32
I32 = mybir.dt.int32
U32 = mybir.dt.uint32
BF16 = mybir.dt.bfloat16
ALU = mybir.AluOpType
ACT = mybir.ActivationFunctionType
AX = mybir.AxisListType

P = 128
R = 125
J = 4
C = R * J
D = 256
DB = D // P
EPS = 1e-5
BIG = 1e30


def rows_of(table, n):
    return table[bass.ds(n * C, C), :].rearrange("(j p) d -> p j d", p=R)


def wide(row, j=J):
    return row.unsqueeze(1).broadcast_to([row.shape[0], j, row.shape[1]])



def wait(e, s, value):
    e.wait_ge(s, value)
    e.nop(nofuse=True)


def transposes(e, K, out, rows, blocks, width=P):
    for k in range(blocks):
        for j in range(J):
            last = e.transpose(out[0:width, k, j * R:(j + 1) * R],
                               rows[:, j, k * width:(k + 1) * width], K["ident"][0:R, 0:R])
    return last


def product_T(e, out, w, m, xT, blocks, first=True, last=True):
    for k in range(blocks):
        mm = e.matmul(out, w[:, k, m * P:(m + 1) * P], xT[:, k, :],
                      start=first and k == 0, stop=last and k == blocks - 1)
    return mm


def product_rows(e, out, w, xT, blocks, aggT=None, ident=None):
    for j in range(J):
        if aggT is None:
            for k in range(blocks):
                mm = e.matmul(out[0:R, j, :], xT[:, k, j * R:(j + 1) * R], w[:, k, :],
                              start=k == 0, stop=k == blocks - 1)
        else:
            for m in range(DB):
                half = out[0:R, j, m * P:(m + 1) * P]
                for k in range(blocks):
                    e.matmul(half, xT[:, k, j * R:(j + 1) * R], w[:, k, m * P:(m + 1) * P],
                             start=k == 0, stop=False)
                mm = e.matmul(half, aggT[:, m, j * R:(j + 1) * R], ident[:, :], start=False, stop=True)
    return mm


def agg_rows(e, out, aggT, ident):
    for j in range(J):
        for k in range(DB):
            mm = e.transpose(out[0:R, j, k * P:(k + 1) * P], aggT[:, k, j * R:(j + 1) * R], ident[:, :])
    return mm


def ln_vector(e, K, L, t, src, dst):
    for j in range(J):
        ins = e.bn_stats(L["stats"][:, j, :], src[:, j, :])
    ins.then_inc(L["s_stats"], 1)
    wait(e, L["s_stats"], t)
    for j in range(J):
        ins = e.bn_aggr(L["mv"][:, j, :], L["stats"][:, j, :])
    ins.then_inc(L["s_var"], 1)
    e.wait_ge(L["s_rstd"], t)
    for j in range(J):
        ins = e.tensor_scalar(dst[:, j, :], src[:, j, :], L["mv"][:, j, 0:1], L["rstd"][:, j:j + 1],
                              ALU.subtract, ALU.mult)
    return ins


def ln_pool(e, K, L, t):
    wait(e, L["s_var"], t)
    e.tensor_scalar(L["vare"][:, :], L["mv"][:, :, 1], EPS, None, ALU.add).then_inc(L["s_vare"], 1)
    e.wait_ge(L["s_vare"], t)
    e.tensor_tensor(L["rstd"][:, :], L["vare"][:, :], K["mhalf"][:, :], ALU.pow).then_inc(L["s_rstd"], 1)


def ln_buffers(sb, sem, name):
    return dict(
        stats=sb(f"{name}_stats", [R, J, 6]), mv=sb(f"{name}_mv", [R, J, 2]),
        vare=sb(f"{name}_vare", [R, J]), rstd=sb(f"{name}_rstd", [R, J]),
        s_stats=sem(f"{name}_s_stats"), s_var=sem(f"{name}_s_var"),
        s_vare=sem(f"{name}_s_vare"), s_rstd=sem(f"{name}_s_rstd"))


def scopes(nc, ctx, name):
    def sb(n, s, d=F32):
        return ctx.enter_context(nc.sbuf_tensor(f"{name}_{n}", s, d))

    def ps(n, s, d=F32):
        return ctx.enter_context(nc.psum_tensor(f"{name}_{n}", s, d))

    sems = []

    def sem(n):
        sems.append(nc.alloc_semaphore(name=f"{name}_{n}"))
        return sems[-1]

    def done():
        if sems:
            nc.clear_and_free_semaphores(sems)
            nc.all_engine_barrier()
    ctx.callback(done)
    return sb, ps, sem



def load_constants(nc, K, A):
    mats = {"Wq": A["L0_gnn_Wq"], "Wk": A["L0_gnn_Wk"], "Wv": A["L0_gnn_Wv"], "Wskip": A["L0_gnn_Wskip"],
            "W": A["L1_gnn_W"], "W_in": A["L2_gnn_W_in"], "W_out": A["L2_gnn_W_out"],
            "W1": A["L3_gnn_W1"], "W2": A["L3_gnn_W2"], "W3": A["L3_gnn_W3"]}
    for l in range(3):
        mats[f"Wagg{l}"] = A["L2_gnn_W_agg"][l]
        mats[f"Wself{l}"] = A["L2_gnn_W_self"][l]
    cols = {"bq": A["L0_gnn_bq"], "bk": A["L0_gnn_bk"], "bv": A["L0_gnn_bv"], "b_in": A["L2_gnn_b_in"],
            "b1": A["L3_gnn_b1"], "b2": A["L3_gnn_b2"]}
    for l in range(3):
        cols[f"b_hid{l}"] = A["L2_gnn_b_hid"][l]
    rows = {"bskip": A["L0_gnn_bskip"], "gamma0": A["L0_gnn_gamma"], "beta0": A["L0_gnn_beta_ln"],
            "bias1": A["L1_gnn_bias"], "gamma1": A["L1_gnn_gamma"], "beta1": A["L1_gnn_beta"],
            "b_out": A["L2_gnn_b_out"], "b3": A["L3_gnn_b3"]}
    sb = K["sb"]
    for n, m in mats.items():
        K[n] = sb(n, [P, m.shape[0] // P, m.shape[1]])
    for n, m in cols.items():
        K[n] = sb(n, [P, m.shape[0] // P])
    for n, m in rows.items():
        K[n] = sb(n, [R, m.shape[0]])
    K["ident"] = sb("ident", [P, P])
    K["mhalf"] = sb("mhalf", [R, J])
    with ExitStack() as ctx:
        sem = scopes(nc, ctx, "const")[2]
        s_w, s_i0, s_i1 = sem("s_w"), sem("s_i0"), sem("s_i1")
        block = ctx.enter_context(nc.Block())

        @block.sync
        def _(e):
            for n, m in mats.items():
                e.dma_start(K[n][:, :, :], m.rearrange("(k p) n -> p k n", p=P)).then_inc(s_w, 16)
            for n, m in cols.items():
                e.dma_start(K[n][:, :], m.rearrange("(k p) -> p k", p=P),
                            allow_slow_non_contiguous=True).then_inc(s_w, 16)
            for n, m in rows.items():
                e.dma_start(K[n][:, :], m.unsqueeze(0).broadcast_to([R, m.shape[0]])).then_inc(s_w, 16)
            e.wait_ge(s_w, 16 * (len(mats) + len(cols) + len(rows)))

        @block.gpsimd
        def _(e):
            e.memset(K["mhalf"][:, :], -0.5)
            e.memset(K["ident"][:, :], 0.0).then_inc(s_i0, 1)
            e.wait_ge(s_i0, 1)
            e.affine_select(out=K["ident"][:, :], in_=K["ident"][:, :], compare_op=ALU.not_equal, fill=1.0,
                            base=0, pattern=[[-1, P]], channel_multiplier=1).then_inc(s_i1, 1)


def dense(nc, K, A, N):
    chunks = N // C
    RING = 2
    with ExitStack() as ctx:
        sb, ps, sem = scopes(nc, ctx, "dense")
        xr, xb, u = sb("xr", [R, J, D]), sb("xb", [R, J, D]), sb("u", [R, J, D])
        v = sb("v", [R, J, D])
        x1, x2, x3 = sb("x1", [R, J, D]), sb("x2", [R, J, D]), sb("x3", [R, J, D])
        t3, o, z = sb("t3", [R, J, D]), sb("o", [R, J, D]), sb("z", [R, J, D])
        xT, x2T, x3T = sb("xT", [P, DB, C]), sb("x2T", [P, DB, C]), sb("x3T", [P, DB, C])
        h = [sb(f"h{i}", [P, DB, C]) for i in range(2)]
        g1, g2 = sb("g1", [P, 2 * DB, C]), sb("g2", [P, 2 * DB, C])
        pF = ps("pF", [P, DB, 512])
        pG = ps("pG", [P, J, D])
        pO = ps("pO", [P, J, D])
        ring = ps("ring", [P, RING, 512])
        LF, LB = ln_buffers(sb, sem, "front"), ln_buffers(sb, sem, "back")
        s_x, s_xT, s_xTc, s_skip = sem("s_x"), sem("s_xT"), sem("s_xTc"), sem("s_skip")
        s_u, s_g, s_n0, s_xb0, s_ga0, s_t0 = (sem("s_u"), sem("s_g"), sem("s_n0"), sem("s_xb0"),
                                              sem("s_ga0"), sem("s_t0"))
        s_x1, s_y, s_xb1, s_n1, s_ga1, s_t1 = (sem("s_x1"), sem("s_y"), sem("s_xb1"), sem("s_n1"),
                                               sem("s_ga1"), sem("s_t1"))
        s_x2, s_x2T, s_x2Tc = sem("s_x2"), sem("s_x2T"), sem("s_x2Tc")
        s_mm, s_ev = sem("s_mm"), sem("s_ev")
        s_o, s_oa, s_ob, s_x3, s_x3T, s_x3Tc = (sem("s_o"), sem("s_oa"), sem("s_ob"), sem("s_x3"),
                                                sem("s_x3T"), sem("s_x3Tc"))
        s_z, s_za, s_zr, s_zb, s_out, s_st = (sem("s_z"), sem("s_za"), sem("s_zr"), sem("s_zb"),
                                              sem("s_out"), sem("s_st"))
        s_out0 = sem("s_out0")
        groups = [(K["W_in"], x2T, DB, m, K["b_in"], h[0], False) for m in range(DB)]
        for l in range(3):
            groups += [(K[f"Wself{l}"], h[l % 2], DB, m, K[f"b_hid{l}"], h[(l + 1) % 2], True)
                       for m in range(DB)]
        hL = h[1]
        G2 = len(groups)
        groups += [(K["W1"], x3T, DB, m, K["b1"], g1, True) for m in range(2 * DB)]
        groups += [(K["W2"], g1, 2 * DB, m, K["b2"], g2, True) for m in range(2 * DB)]
        G = len(groups)
        block = ctx.enter_context(nc.Block())

        @block.sync
        def _(e):
            e.dma_start(xr[:], rows_of(A["x"], 0)).then_inc(s_x, 16)
            with e.Fori(0, chunks - 1) as c:
                wait(e, s_t0, c + 1)
                e.dma_start(xr[:], rows_of(A["x"], c + 1)).then_inc(s_x, 16)
                wait(e, s_out, c + 1)
                e.dma_start(rows_of(A["out"], c), o[:]).then_inc(s_st, 16)
            e.wait_ge(s_out, chunks)
            e.dma_start(rows_of(A["out"], chunks - 1), o[:]).then_inc(s_st, 16)
            e.wait_ge(s_st, 16 * chunks + 1)

        def pe_front_x(e, c):
            wait(e, s_x, 16 * c + 16)
            transposes(e, K, pF, xr, DB).then_inc(s_xT, 1)

        def pe_front_skip(e, c):
            wait(e, s_xTc, c + 1)
            product_rows(e, pG, K["Wskip"], xT, DB).then_inc(s_skip, 1)

        def pe_front_x2(e, c):
            wait(e, s_x2, c + 1)
            transposes(e, K, pF, x2, DB).then_inc(s_x2T, 1)

        def pe_group(e, c, g):
            w, xin, nb, m, _, _, _ = groups[g]
            first_of_layer = g == 0 or groups[g - 1][1] is not xin
            wait(e, s_ev, c * G + (RING + g if first_of_layer else g + 1))
            product_T(e, ring[:, g % RING, 0:C], w, m, xin, nb).then_inc(s_mm, 1)

        def pe_back_1(e, c):
            wait(e, s_x2Tc, c + 1)
            for g in range(G2):
                pe_group(e, c, g)
            wait(e, s_ev, c * G + G2 + RING)
            product_rows(e, pO, K["W_out"], hL, DB).then_inc(s_o, 1)

        def pe_back_2(e, c):
            wait(e, s_x3, c + 1)
            transposes(e, K, pF, x3, DB).then_inc(s_x3T, 1)
            wait(e, s_x3Tc, c + 1)
            for g in range(G2, G):
                pe_group(e, c, g)
            wait(e, s_ev, c * G + G + RING)
            product_rows(e, pO, K["W3"], g2, 2 * DB).then_inc(s_z, 1)

        @block.tensor
        def _(e):
            pe_front_x(e, 0)
            pe_front_skip(e, 0)
            pe_front_x2(e, 0)
            with e.Fori(0, chunks - 1) as c:
                pe_back_1(e, c)
                pe_front_x(e, c + 1)
                pe_front_skip(e, c + 1)
                pe_back_2(e, c)
                pe_front_x2(e, c + 1)
            pe_back_1(e, chunks - 1)
            pe_back_2(e, chunks - 1)

        def act_evac(e, c, g):
            _, _, _, m, bias, out, relu = groups[g]
            e.wait_ge(s_mm, c * G + g + 1)
            e.activation(out[:, m, :], ring[:, g % RING, 0:C], ACT.Relu if relu else ACT.Identity,
                         bias=bias[:, m:m + 1]).then_inc(s_ev, 1)

        def act_front_x(e, c):
            e.wait_ge(s_xT, c + 1)
            e.activation(xT[:, :, :], pF[:, :, 0:C], ACT.Copy).then_inc(s_xTc, 1)

        def act_gelu(e, c):
            e.wait_ge(s_u, c + 1)
            e.activation(v[:, :, :], u[:, :, :], ACT.Gelu).then_inc(s_g, 1)

        def act_front_x2(e, c):
            e.wait_ge(s_x2T, c + 1)
            e.activation(x2T[:, :, :], pF[:, :, 0:C], ACT.Copy).then_inc(s_x2Tc, 1)

        @block.scalar
        def _(e):
            e.sem_inc(s_ev, RING)
            act_front_x(e, 0)
            act_gelu(e, 0)
            act_front_x2(e, 0)

            def act_back_1(c):
                for g in range(G2):
                    act_evac(e, c, g)

            def act_back_2(c):
                e.wait_ge(s_x3T, c + 1)
                e.activation(x3T[:, :, :], pF[:, :, 0:C], ACT.Copy).then_inc(s_x3Tc, 1)
                for g in range(G2, G):
                    act_evac(e, c, g)

            def act_final(c):
                e.wait_ge(s_za, c + 1)
                e.activation(z[:, :, :], z[:, :, :], ACT.Relu).then_inc(s_zr, 1)

            with e.Fori(0, chunks - 1) as c:
                act_back_1(c)
                act_front_x(e, c + 1)
                act_gelu(e, c + 1)
                act_back_2(c)
                act_final(c)
                act_front_x2(e, c + 1)
            act_back_1(chunks - 1)
            act_back_2(chunks - 1)
            act_final(chunks - 1)

        def dve_front_u(e, c):
            e.drain()
            e.wait_ge(s_skip, c + 1)
            e.tensor_tensor(u[:, :, :], pG[0:R, :, :], wide(K["bskip"][:, :]), ALU.add).then_inc(s_u, 1)

        def dve_front(e, c):
            e.drain()
            e.wait_ge(s_g, c + 1)
            ln_vector(e, K, LF, 4 * c + 1, v, u).then_inc(s_n0, 1)
            e.wait_ge(s_t0, c + 1)
            ln_vector(e, K, LF, 4 * c + 2, u, x1).then_inc(s_x1, 1)
            e.wait_ge(s_y, c + 1)
            ln_vector(e, K, LF, 4 * c + 3, u, v).then_inc(s_n1, 1)
            e.wait_ge(s_t1, c + 1)
            ln_vector(e, K, LF, 4 * c + 4, v, x2).then_inc(s_x2, 1)

        def dve_back_1(e, c):
            e.drain()
            e.wait_ge(s_o, c + 1)
            e.tensor_tensor(t3[:, :, :], pO[0:R, :, :], wide(K["b_out"][:, :]), ALU.add).then_inc(s_oa, 1)
            e.wait_ge(s_oa, c + 1)
            e.tensor_tensor(t3[:, :, :], t3[:, :, :], x2[:, :, :], ALU.add).then_inc(s_ob, 1)
            e.wait_ge(s_ob, c + 1)
            ln_vector(e, K, LB, 2 * c + 1, t3, x3).then_inc(s_x3, 1)

        def dve_back_2(e, c):
            e.drain()
            e.wait_ge(s_z, c + 1)
            e.tensor_tensor(z[:, :, :], pO[0:R, :, :], wide(K["b3"][:, :]), ALU.add).then_inc(s_za, 1)
            e.wait_ge(s_zr, c + 1)
            e.tensor_tensor(t3[:, :, :], z[:, :, :], x3[:, :, :], ALU.add).then_inc(s_zb, 1)
            e.wait_ge(s_zb, c + 1)
            ln_vector(e, K, LB, 2 * c + 2, t3, z).then_inc(s_out0, 1)

        @block.vector
        def _(e):
            dve_front_u(e, 0)
            dve_front(e, 0)
            with e.Fori(0, chunks - 1) as c:
                dve_back_1(e, c)
                dve_front_u(e, c + 1)
                dve_front(e, c + 1)
                dve_back_2(e, c)
            dve_back_1(e, chunks - 1)
            dve_back_2(e, chunks - 1)

        @block.gpsimd
        def _(e):
            e.sem_inc(s_st, 1)

            def pool_front(c):
                e.drain()
                e.wait_ge(s_x, 16 * c + 16)
                e.tensor_tensor(xb[:, :, :], xr[:, :, :], wide(K["beta0"][:, :]), ALU.add).then_inc(s_xb0, 1)
                ln_pool(e, K, LF, 4 * c + 1)
                e.wait_ge(s_n0, c + 1)
                e.tensor_tensor(u[:, :, :], u[:, :, :], wide(K["gamma0"][:, :]), ALU.mult).then_inc(s_ga0, 1)
                e.wait_ge(s_ga0, c + 1)
                e.wait_ge(s_xb0, c + 1)
                e.tensor_tensor(u[:, :, :], u[:, :, :], xb[:, :, :], ALU.add).then_inc(s_t0, 1)
                ln_pool(e, K, LF, 4 * c + 2)
                e.wait_ge(s_x1, c + 1)
                e.tensor_tensor(u[:, :, :], x1[:, :, :], wide(K["bias1"][:, :]), ALU.add).then_inc(s_y, 1)
                e.tensor_tensor(xb[:, :, :], x1[:, :, :], wide(K["beta1"][:, :]), ALU.add).then_inc(s_xb1, 1)
                ln_pool(e, K, LF, 4 * c + 3)
                e.wait_ge(s_n1, c + 1)
                e.tensor_tensor(v[:, :, :], v[:, :, :], wide(K["gamma1"][:, :]), ALU.mult).then_inc(s_ga1, 1)
                e.wait_ge(s_ga1, c + 1)
                e.wait_ge(s_xb1, c + 1)
                e.tensor_tensor(v[:, :, :], v[:, :, :], xb[:, :, :], ALU.add).then_inc(s_t1, 1)
                ln_pool(e, K, LF, 4 * c + 4)

            def pool_out(c):
                e.wait_ge(s_out0, c + 1)
                wait(e, s_st, 16 * c + 1)
                e.tensor_copy(o[:, :, :], z[:, :, :]).then_inc(s_out, 1)

            pool_front(0)
            with e.Fori(0, chunks - 1) as c:
                ln_pool(e, K, LB, 2 * c + 1)
                pool_front(c + 1)
                ln_pool(e, K, LB, 2 * c + 2)
                pool_out(c)
            ln_pool(e, K, LB, 2 * (chunks - 1) + 1)
            ln_pool(e, K, LB, 2 * (chunks - 1) + 2)
            pool_out(chunks - 1)



TILES = 40
U = 8
FAR = 1 << 17


def column_loop(e, K, body):
    with e.Fori(0, TILES // U) as i:
        body(i)


def rank_edges(nc, K, A, name, key, table):
    E = key.shape[0]
    with ExitStack() as ctx:
        sb, ps, sem = scopes(nc, ctx, name)
        keyI, keyF = sb("keyI", [R, E], I32), sb("keyF", [R, E])
        count, before = sb("count", [R, 2 * E]), sb("before", [R, 2 * E], BF16)
        less = sb("less", [R, E], BF16)
        srcC, dstC, keyC = sb("srcC", [R, TILES], I32), sb("dstC", [R, TILES], I32), sb("keyC", [R, TILES])
        rank, rankU = sb("rank", [R, TILES]), sb("rankU", [R, TILES], U32)
        pay = sb("pay", [R, TILES, 4], I32)
        idx8, pay8 = sb("idx8", [R, U], U32), sb("pay8", [R, U, 4], I32)
        s_ld, s_count, s_pos, s_rank, s_c8, s_sc = (sem("s_ld"), sem("s_count"), sem("s_pos"),
                                                    sem("s_rank"), sem("s_c8"), sem("s_sc"))
        block = ctx.enter_context(nc.Block())

        @block.sync
        def _(e):
            e.dma_start(keyI[:], key.unsqueeze(0).broadcast_to([R, E])).then_inc(s_ld, 16)
            for c, a in ((srcC, A["src"]), (dstC, A["dst"])):
                e.dma_start(c[:], a.rearrange("(t p) -> p t", p=R), allow_slow_non_contiguous=True)\
                    .then_inc(s_ld, 16)

        @block.vector
        def _(e):
            e.wait_ge(s_ld, 48)
            e.tensor_copy(keyF[:], keyI[:])
            e.tensor_copy(keyC[:], (srcC if key is A["src"] else dstC)[:])
            e.wait_ge(s_pos, 1)
            e.tensor_copy(pay[:, :, 0], srcC[:])
            e.tensor_copy(pay[:, :, 1], dstC[:])
            e.wait_ge(s_count, 1)
            e.tensor_scalar(before[:], count[:], float(E), 0.5, ALU.is_lt, ALU.mult)
            e.drain()
            with e.Fori(0, TILES) as t:
                e.scalar_tensor_tensor(out=less[:], in0=keyF[:], scalar=keyC[:, bass.ds(t, 1)],
                                       in1=before[:, bass.ds(t * (-R) + E, E)], op0=ALU.subtract,
                                       op1=ALU.is_lt, accum_out=rank[:, bass.ds(t, 1)])
                e.drain()
            e.tensor_copy(rankU[:], rank[:]).then_inc(s_rank, 1)

        @block.gpsimd
        def _(e):
            e.memset(pay[:], 0)
            e.drain()
            e.iota(pay[:, :, 2], pattern=[[R, TILES]], base=0, channel_multiplier=1).then_inc(s_pos, 1)
            e.iota(count[:], pattern=[[1, 2 * E]], base=0, channel_multiplier=-1,
                   allow_small_or_imprecise_dtypes=True).then_inc(s_count, 1)
            e.wait_ge(s_rank, 1)

            def body(i):
                e.tensor_copy(idx8[:], rankU[:, bass.ds(i * U, U)])
                e.tensor_copy(pay8[:], pay[:, bass.ds(i * U, U), :]).then_inc(s_c8, 1)
                wait(e, s_c8, i + 1)
                for k in range(U):
                    e.indirect_dma_start(table, bass.IndirectOffsetOnAxis(ap=idx8[:, k:k + 1], axis=0),
                                         pay8[:, k, :], None).then_inc(s_sc, 16)
                wait(e, s_sc, i * (16 * U) + 16 * U)
            column_loop(e, K, body)


def load_sorted(nc, K, A, S):
    with ExitStack() as ctx:
        sb, ps, sem = scopes(nc, ctx, "sorted")
        rows = [sb(f"rows{i}", [R, TILES, 4], I32) for i in range(2)]
        keyT = [sb(f"keyT{i}", [TILES, R]) for i in range(2)]
        pk = ps("pk", [P, 2, 512])
        zero = sb("zero", [R, 4 * K["N"] // R])
        s_ld, s_col, s_T, s_Tc, s_st, s_z, s_ord = (sem("s_ld"), sem("s_col"), sem("s_T"), sem("s_Tc"),
                                                    sem("s_st"), sem("s_z"), sem("s_ord"))
        block = ctx.enter_context(nc.Block())

        @block.sync
        def _(e):
            for i in range(2):
                e.dma_start(rows[i][:], S["edges"][i].rearrange("(t p) w -> p t w", p=R)).then_inc(s_ld, 16)
            e.wait_ge(s_z, 1)
            e.dma_start(S["nodes"].rearrange("(p a) w -> p (a w)", p=R), zero[:]).then_inc(s_st, 16)
            e.wait_ge(s_Tc, 1)
            for i in range(2):
                e.dma_start(S["key"][i], keyT[i][:]).then_inc(s_st, 16)
            e.wait_ge(s_st, 48)

        @block.vector
        def _(e):
            e.memset(zero[:], 0.0).then_inc(s_z, 1)
            e.wait_ge(s_ld, 32)
            for i in range(2):
                e.tensor_copy(K["srcF"][i][:], rows[i][:, :, 0])
                e.tensor_copy(K["dstF"][i][:], rows[i][:, :, 1])
                e.tensor_copy(K["srcU"][i][:], rows[i][:, :, 0])
                last = e.tensor_copy(K["dstU"][i][:], rows[i][:, :, 1])
            last = e.tensor_copy(K["ordU"][:], rows[0][:, :, 2])
            last.then_inc(s_col, 1)
            e.wait_ge(s_T, 1)
            for i in range(2):
                last = e.tensor_copy(keyT[i][:], pk[0:TILES, i, 0:R])
            last.then_inc(s_Tc, 1)

        @block.tensor
        def _(e):
            e.wait_ge(s_col, 1)
            e.transpose(pk[0:TILES, 0, 0:R], K["dstF"][0][:], K["ident"][0:R, 0:R])
            e.transpose(pk[0:TILES, 1, 0:R], K["srcF"][1][:], K["ident"][0:R, 0:R]).then_inc(s_T, 1)


def load_segments(nc, K, name, S, i, seg):
    E = K["E"]
    with ExitStack() as ctx:
        sb, ps, sem = scopes(nc, ctx, name)
        keyB = sb("keyB", [P, E])
        s_ld = sem("s_ld")
        block = ctx.enter_context(nc.Block())

        @block.sync
        def _(e):
            e.dma_start(keyB[:], S["key"][i].rearrange("t p -> (t p)").unsqueeze(0).broadcast_to([P, E]))\
                .then_inc(s_ld, 16)

        @block.vector
        def _(e):
            e.memset(seg[:, 0:1], 0.0)
            e.memset(seg[:, E:E + 1], 0.0)
            e.wait_ge(s_ld, 16)
            e.tensor_tensor(seg[:, 1:E], keyB[:, 1:E], keyB[:, 0:E - 1], ALU.is_equal)


def node_maps(nc, K, A, S):
    E, N = K["E"], K["N"]
    with ExitStack() as ctx:
        sb, ps, sem = scopes(nc, ctx, "maps")
        seg = [sb(f"seg{i}", [P, E + 1]) for i in range(2)]
        for i in range(2):
            load_segments(nc, K, f"maps_seg{i}", S, i, seg[i])
        cnt = sb("cnt", [P, E])
        one = sb("one", [P, 1])
        pos = sb("pos", [R, TILES])
        same = [sb(f"same{i}", [R, TILES]) for i in range(2)]
        pay = [sb(f"pay{i}", [R, TILES, 2]) for i in range(2)]
        at = [sb(f"at{i}", [R, TILES], U32) for i in range(2)]
        atF = sb("atF", [R, TILES])
        info = {}
        tmp = [sb(f"tmp{i}", [R, TILES]) for i in range(4)]
        half = sb("half", [R, TILES])
        idx8, pay8, got8 = sb("idx8", [R, U], U32), sb("pay8", [R, U, 2]), sb("got8", [R, U, 4])
        pc = ps("pc", [P, 4, TILES])
        s_one, s_cnt, s_c, s_cc, s_at, s_pos = (sem("s_one"), sem("s_cnt"), sem("s_c"), sem("s_cc"),
                                                sem("s_at"), sem("s_pos"))
        s_c8, s_sc, s_g8, s_ga, s_gb = sem("s_c8"), sem("s_sc"), sem("s_g8"), sem("s_ga"), sem("s_gb")
        s_all, s_pw, s_pd = sem("s_all"), sem("s_pw"), sem("s_pd")
        looks = [(K["srcU"][0], "src0"), (K["dstU"][0], "dst0"), (K["srcU"][1], "src1"), (K["dstU"][1], "dst1")]
        for _, n in looks:
            info[n] = sb(f"info_{n}", [R, TILES, 4])
        block = ctx.enter_context(nc.Block())

        @block.vector
        def _(e):
            e.memset(one[:], 1.0).then_inc(s_one, 1)
            e.memset(half[:], -0.5)
            e.drain()
            for i in range(2):
                if i:
                    e.wait_ge(s_c, 1)
                e.tensor_tensor_scan(cnt[:], seg[i][:, 0:E], one[:, 0:1].broadcast_to([P, E]), 0.0,
                                     ALU.mult, ALU.add).then_inc(s_cnt, 1)
            e.wait_ge(s_c, 2)
            e.wait_ge(s_pos, 1)
            for i in range(2):
                e.tensor_copy(same[i][:], pc[0:R, 2 * i + 1, :])
                e.tensor_copy(pay[i][:, :, 1], pc[0:R, 2 * i, :])
                e.tensor_scalar(pay[i][:, :, 0], pos[:], 1.0, None, ALU.add)
                e.drain()
                e.tensor_scalar(atF[:], (K["dstF"][0] if i == 0 else K["srcF"][1])[:], 2.0, float(i),
                                ALU.mult, ALU.add)
                e.drain()
                e.scalar_tensor_tensor(out=atF[:], in0=same[i][:], scalar=float(FAR), in1=atF[:],
                                       op0=ALU.mult, op1=ALU.add)
                e.drain()
                e.tensor_copy(at[i][:], atF[:])
                e.drain()
            e.tensor_copy(atF[:], atF[:]).then_inc(s_at, 1)
            e.wait_ge(s_all, 1)

            def map1(n, out):
                a, b = info[n][:, :, 0], info[n][:, :, 2]
                e.tensor_tensor(tmp[0][:], a, b, ALU.subtract)
                e.tensor_scalar(tmp[1][:], a, 0.0, None, ALU.is_gt)
                e.drain()
                e.scalar_tensor_tensor(out=tmp[2][:], in0=tmp[0][:], scalar=-float(E), in1=tmp[1][:],
                                       op0=ALU.add, op1=ALU.mult)
                e.drain()
                e.scalar_tensor_tensor(out=tmp[3][:], in0=tmp[2][:], scalar=float(E - 1), in1=b,
                                       op0=ALU.add, op1=ALU.add)
                e.drain()
                e.tensor_copy(out[:], tmp[3][:])
                e.drain()

            def map2(n, out):
                a, b = info[n][:, :, 0], info[n][:, :, 2]
                e.tensor_tensor(tmp[0][:], b, a, ALU.subtract)
                e.tensor_scalar(tmp[1][:], b, 0.0, None, ALU.is_gt)
                e.drain()
                e.scalar_tensor_tensor(out=tmp[2][:], in0=tmp[0][:], scalar=float(E), in1=tmp[1][:],
                                       op0=ALU.add, op1=ALU.mult)
                e.drain()
                e.scalar_tensor_tensor(out=tmp[3][:], in0=tmp[2][:], scalar=-1.0, in1=a,
                                       op0=ALU.add, op1=ALU.add)
                e.drain()
                e.tensor_copy(out[:], tmp[3][:])
                e.drain()

            map1("src0", K["m1s"])
            map2("src0", K["m2s"])
            map1("dst1", K["m1d"])
            map2("dst1", K["m2d"])
            map2("dst0", K["ownA"])
            map1("src1", K["ownB"])
            e.scalar_tensor_tensor(out=tmp[0][:], in0=same[0][:], scalar=float(FAR), in1=K["dstF"][0][:],
                                   op0=ALU.mult, op1=ALU.add)
            e.tensor_scalar(tmp[1][:], info["src1"][:, :, 0], 0.0, None, ALU.is_gt)
            e.drain()
            e.tensor_copy(K["outA"][:], tmp[0][:])
            e.tensor_tensor(tmp[2][:], tmp[1][:], same[1][:], ALU.max)
            e.drain()
            e.scalar_tensor_tensor(out=tmp[3][:], in0=tmp[2][:], scalar=float(FAR), in1=K["srcF"][1][:],
                                   op0=ALU.mult, op1=ALU.add)
            e.drain()
            e.tensor_copy(K["outB"][:], tmp[3][:])
            e.reciprocal(K["inv2"][:], info["src1"][:, :, 3])
            e.tensor_scalar(tmp[0][:], info["src0"][:, :, 1], 1.0, None, ALU.add)
            e.tensor_scalar(tmp[1][:], info["dst0"][:, :, 1], 1.0, None, ALU.add).then_inc(s_pw, 1)
            e.wait_ge(s_pd, 1)
            e.tensor_tensor(K["norm3"][:], tmp[2][:], tmp[3][:], ALU.mult)
            e.tensor_tensor(K["self3"][:], tmp[3][:], tmp[3][:], ALU.mult)

        @block.tensor
        def _(e):
            e.wait_ge(s_one, 1)
            for i in range(2):
                e.wait_ge(s_cnt, i + 1)
                for t in range(TILES):
                    e.matmul(pc[0:R, 2 * i, t:t + 1], cnt[0:1, t * R:(t + 1) * R], one[0:1, 0:1],
                             start=True, stop=True)
                    mm = e.matmul(pc[0:R, 2 * i + 1, t:t + 1], seg[i][0:1, t * R + 1:(t + 1) * R + 1],
                                  one[0:1, 0:1], start=True, stop=True)
                mm.then_inc(s_c, 1)

        @block.gpsimd
        def _(e):
            e.iota(pos[:], pattern=[[R, TILES]], base=0, channel_multiplier=1,
                   allow_small_or_imprecise_dtypes=True).then_inc(s_pos, 1)
            e.wait_ge(s_at, 1)
            for i in range(2):
                def body(j):
                    turn = j + i * (TILES // U)
                    e.tensor_copy(idx8[:], at[i][:, bass.ds(j * U, U)])
                    e.tensor_copy(pay8[:], pay[i][:, bass.ds(j * U, U), :]).then_inc(s_c8, 1)
                    wait(e, s_c8, turn + 1)
                    for k in range(U):
                        e.indirect_dma_start(S["nodes"], bass.IndirectOffsetOnAxis(ap=idx8[:, k:k + 1], axis=0),
                                             pay8[:, k, :], None, bounds_check=2 * N - 1,
                                             oob_is_err=False).then_inc(s_sc, 16)
                    wait(e, s_sc, turn * (16 * U) + 16 * U)
                column_loop(e, K, body)
            wide_nodes = S["nodes"].rearrange("(n two) w -> n (two w)", two=2)
            for q, (idx, n) in enumerate(looks):
                def body(j):
                    turn = j + q * (TILES // U)
                    e.tensor_copy(idx8[:], idx[:, bass.ds(j * U, U)]).then_inc(s_g8, 1)
                    wait(e, s_g8, turn + 1)
                    for k in range(U):
                        e.indirect_dma_start(got8[:, k, :], None, wide_nodes,
                                             bass.IndirectOffsetOnAxis(ap=idx8[:, k:k + 1], axis=0))\
                            .then_inc(s_ga, 16)
                    wait(e, s_ga, turn * (16 * U) + 16 * U)
                    e.tensor_copy(info[n][:, bass.ds(j * U, U), :], got8[:]).then_inc(s_gb, 1)
                    wait(e, s_gb, turn + 1)
                column_loop(e, K, body)
            e.memset(idx8[:], 0).then_inc(s_all, 1)
            e.wait_ge(s_pw, 1)
            e.tensor_tensor(tmp[2][:], tmp[0][:], half[:], ALU.pow)
            e.tensor_tensor(tmp[3][:], tmp[1][:], half[:], ALU.pow).then_inc(s_pd, 1)


def att_weights(nc, K, A):
    with ExitStack() as ctx:
        sb, ps, sem = scopes(nc, ctx, "att")
        We = sb("We", [64, D])
        att = {n: sb(n, [P, D]) for n in ("src", "dst", "edge")}
        prod = sb("prod", [P, DB, D])
        s_ld = sem("s_ld")
        block = ctx.enter_context(nc.Block())
        drams = {"src": A["L1_gnn_att_src"], "dst": A["L1_gnn_att_dst"], "edge": A["L1_gnn_att_edge"]}

        @block.sync
        def _(e):
            e.dma_start(We[:], A["L1_gnn_W_e"]).then_inc(s_ld, 16)
            for n in att:
                e.dma_start(att[n][:], drams[n].rearrange("h c -> (h c)").unsqueeze(0).broadcast_to([P, D]))\
                    .then_inc(s_ld, 16)

        @block.vector
        def _(e):
            e.wait_ge(s_ld, 64)
            for n, out in (("src", K["WAs"]), ("dst", K["WAd"])):
                e.drain()
                e.tensor_tensor(prod[:], K["W"][:, :, :], att[n][:].unsqueeze(1).broadcast_to([P, DB, D]), ALU.mult)
                e.drain()
                e.tensor_reduce(out[:], prod[:].rearrange("p k (h c) -> p k h c", h=8), AX.X, ALU.add)
            e.drain()
            e.tensor_tensor(prod[0:64, 0, :], We[:], att["edge"][0:64, :], ALU.mult)
            e.drain()
            e.tensor_reduce(K["WAe"][:], prod[0:64, 0, :].rearrange("p (h c) -> p h c", h=8), AX.X, ALU.add)

        @block.gpsimd
        def _(e):
            def keep(t, base, pattern, cm):
                e.drain()
                e.affine_select(out=t, in_=t, compare_op=ALU.is_ge, fill=0.0, base=base, pattern=pattern,
                                channel_multiplier=cm)
            for t, w in ((K["rep0"], 64), (K["rep1"], 32)):
                e.memset(t[:], 1.0)
                keep(t[:], 0, [[1, D]], -w)
                keep(t[:], w - 1, [[-1, D]], w)
            e.memset(K["sum0"][:], 1.0)
            keep(K["sum0"][:], 0, [[P, DB], [-64, 4]], 1)
            keep(K["sum0"][:], 63, [[-P, DB], [64, 4]], -1)



def gather(e, table, idx, idxb, buf, n, s_idx, t, s_row):
    e.tensor_copy(idxb[:], idx[:, bass.ds(n * J, J)]).then_inc(s_idx, 1)
    wait(e, s_idx, t)
    for j in range(J):
        e.indirect_dma_start(buf[:, j, :], None, table, bass.IndirectOffsetOnAxis(ap=idxb[:, j:j + 1], axis=0))\
            .then_inc(s_row, 16)


def edge_scan(e, seg, n, src, agg, carry, blocks):
    for k in range(blocks):
        e.tensor_tensor_scan(agg[:, k, :], seg[:, bass.ds(n * C, C)], src[:, k, 0:C], carry[:, k:k + 1],
                             ALU.mult, ALU.add)
    e.drain()
    return e.tensor_copy(carry[:, 0:blocks], agg[:, :, C - 1])


def times_columns(e, rows, col, n, width):
    return e.tensor_tensor(rows[:], rows[:], col[:, bass.ds(n * J, J)].unsqueeze(2).broadcast_to([R, J, width]),
                           ALU.mult)


def scores0(nc, K, A, S, alpha):
    with ExitStack() as ctx:
        sb, ps, sem = scopes(nc, ctx, "sc0")
        ms, ow = sb("ms", [R, J, D]), sb("ow", [R, J, D])
        idxb = [sb(f"idxb{i}", [R, J], U32) for i in range(2)]
        msT, owT, qT, vT, prod = (sb(n, [P, DB, C]) for n in ("msT", "owT", "qT", "vT", "prod"))
        p = [ps(f"p{i}", [P, DB, 512]) for i in range(4)]
        s_go, s_idx, s_row, s_T, s_Tc, s_qk, s_q, s_v, s_pr, s_vc, s_al, s_alc, s_st = (
            sem(n) for n in ("s_go", "s_idx", "s_row", "s_T", "s_Tc", "s_qk", "s_q", "s_v", "s_pr",
                             "s_vc", "s_al", "s_alc", "s_st"))
        block = ctx.enter_context(nc.Block())
        n_chunks = K["E"] // C

        @block.sync
        def _(e):
            with e.Fori(0, n_chunks) as n:
                e.sem_inc(s_go, 1)
                wait(e, s_alc, n + 1)
                wait(e, s_vc, n + 1)
                e.dma_start(S["V"][bass.ds(n, 1)].rearrange("o p k c -> p (o k) c"), vT[:]).then_inc(s_st, 16)
                wait(e, s_st, n * 16 + 16)

        @block.gpsimd
        def _(e):
            with e.Fori(0, n_chunks) as n:
                wait(e, s_go, n + 1)
                gather(e, A["x"], K["srcU"][0], idxb[0], ms, n, s_idx, 2 * n + 1, s_row)
                gather(e, A["x"], K["dstU"][0], idxb[1], ow, n, s_idx, 2 * n + 2, s_row)

        @block.tensor
        def _(e):
            with e.Fori(0, n_chunks) as n:
                e.wait_ge(s_row, n * (32 * J) + 32 * J)
                transposes(e, K, p[0], ms, DB)
                transposes(e, K, p[1], ow, DB).then_inc(s_T, 1)
                e.wait_ge(s_Tc, n + 1)
                for m in range(DB):
                    product_T(e, p[2][:, m, 0:C], K["Wq"], m, owT, DB)
                for m in range(DB):
                    mm = product_T(e, p[3][:, m, 0:C], K["Wk"], m, msT, DB)
                mm.then_inc(s_qk, 1)
                for m in range(DB):
                    mm = product_T(e, p[0][:, m, 0:C], K["Wv"], m, msT, DB)
                mm.then_inc(s_v, 1)
                e.wait_ge(s_pr, n + 1)
                for m in range(DB):
                    mm = e.matmul(p[1][0:4, 0, 0:C], K["sum0"][:, m, :], prod[:, m, :], start=m == 0,
                                  stop=m == DB - 1)
                mm.then_inc(s_al, 1)

        @block.scalar
        def _(e):
            with e.Fori(0, n_chunks) as n:
                e.wait_ge(s_T, n + 1)
                e.activation(msT[:], p[0][:, :, 0:C], ACT.Copy)
                e.activation(owT[:], p[1][:, :, 0:C], ACT.Copy).then_inc(s_Tc, 1)
                e.wait_ge(s_qk, n + 1)
                for m in range(DB):
                    a = e.activation(qT[:, m, :], p[2][:, m, 0:C], ACT.Identity, bias=K["bq"][:, m:m + 1])
                a.then_inc(s_q, 1)
                e.wait_ge(s_v, n + 1)
                for m in range(DB):
                    a = e.activation(vT[:, m, :], p[0][:, m, 0:C], ACT.Identity, bias=K["bv"][:, m:m + 1])
                a.then_inc(s_vc, 1)

        @block.vector
        def _(e):
            with e.Fori(0, n_chunks) as n:
                e.wait_ge(s_q, n + 1)
                for m in range(DB):
                    v = e.scalar_tensor_tensor(out=prod[:, m, :], in0=p[3][:, m, 0:C], scalar=K["bk"][:, m:m + 1],
                                               in1=qT[:, m, :], op0=ALU.add, op1=ALU.mult)
                v.then_inc(s_pr, 1)
                e.wait_ge(s_al, n + 1)
                e.tensor_scalar(alpha[0:4, bass.ds(n * C, C)], p[1][0:4, 0, 0:C], 0.125, None, ALU.mult)\
                    .then_inc(s_alc, 1)


def scores1(nc, K, A, S, alpha, adst):
    with ExitStack() as ctx:
        sb, ps, sem = scopes(nc, ctx, "sc1")
        ms, ow, ea = sb("ms", [R, J, D]), sb("ow", [R, J, D]), sb("ea", [R, J, 64])
        idxb = [sb(f"idxb{i}", [R, J], U32) for i in range(2)]
        msT, owT, vT = (sb(n, [P, DB, C]) for n in ("msT", "owT", "vT"))
        eaT = sb("eaT", [64, C])
        p = [ps(f"p{i}", [P, DB, 512]) for i in range(4)]
        s_go, s_idx, s_row, s_lin, s_T, s_Tc, s_al, s_v, s_vc, s_alc, s_st = (
            sem(n) for n in ("s_go", "s_idx", "s_row", "s_lin", "s_T", "s_Tc", "s_al", "s_v", "s_vc",
                             "s_alc", "s_st"))
        block = ctx.enter_context(nc.Block())
        n_chunks = K["E"] // C

        @block.sync
        def _(e):
            with e.Fori(0, n_chunks) as n:
                e.sem_inc(s_go, 1)
                e.dma_start(ow[:], rows_of(S["X1"], n)).then_inc(s_lin, 16)
                wait(e, s_alc, n + 1)
                wait(e, s_vc, n + 1)
                e.dma_start(S["V"][bass.ds(n, 1)].rearrange("o p k c -> p (o k) c"), vT[:]).then_inc(s_st, 16)
                wait(e, s_st, n * 16 + 16)

        @block.gpsimd
        def _(e):
            with e.Fori(0, n_chunks) as n:
                wait(e, s_go, n + 1)
                gather(e, S["X1"], K["m1s"], idxb[0], ms, n, s_idx, 2 * n + 1, s_row)
                gather(e, A["edge_attr_64"], K["ordU"], idxb[1], ea, n, s_idx, 2 * n + 2, s_row)

        @block.tensor
        def _(e):
            with e.Fori(0, n_chunks) as n:
                e.wait_ge(s_lin, n * 16 + 16)
                e.wait_ge(s_row, n * (32 * J) + 32 * J)
                transposes(e, K, p[0], ms, DB)
                transposes(e, K, p[2], ea, 1, 64)
                transposes(e, K, p[1], ow, DB).then_inc(s_T, 1)
                e.wait_ge(s_Tc, n + 1)
                for k in range(DB):
                    e.matmul(p[3][0:8, 0, 0:C], K["WAs"][:, k, :], msT[:, k, :], start=k == 0, stop=False)
                e.matmul(p[3][0:8, 0, 0:C], K["WAe"][:, :], eaT[:, :], start=False, stop=True)
                for k in range(DB):
                    mm = e.matmul(p[3][0:8, 1, 0:C], K["WAd"][:, k, :], owT[:, k, :], start=k == 0, stop=k == DB - 1)
                mm.then_inc(s_al, 1)
                for m in range(DB):
                    mm = product_T(e, p[0][:, m, 0:C], K["W"], m, msT, DB)
                mm.then_inc(s_v, 1)

        @block.scalar
        def _(e):
            with e.Fori(0, n_chunks) as n:
                e.wait_ge(s_T, n + 1)
                e.activation(msT[:], p[0][:, :, 0:C], ACT.Copy)
                e.activation(eaT[:], p[2][0:64, 0, 0:C], ACT.Copy)
                e.activation(owT[:], p[1][:, :, 0:C], ACT.Copy).then_inc(s_Tc, 1)
                e.wait_ge(s_v, n + 1)
                e.activation(vT[:], p[0][:, :, 0:C], ACT.Copy).then_inc(s_vc, 1)

        @block.vector
        def _(e):
            with e.Fori(0, n_chunks) as n:
                e.wait_ge(s_al, n + 1)
                e.tensor_copy(alpha[0:8, bass.ds(n * C, C)], p[3][0:8, 0, 0:C])
                e.tensor_copy(adst[0:8, bass.ds(n * C, C)], p[3][0:8, 1, 0:C]).then_inc(s_alc, 1)


def softmax(nc, K, name, H, seg, alpha, adst):
    E = K["E"]
    with ExitStack() as ctx:
        sb, ps, sem = scopes(nc, ctx, name)
        far, m = sb("far", [8, E + 1]), sb("m", [8, E])
        s_sub, s_exp = sem("s_sub"), sem("s_exp")
        block = ctx.enter_context(nc.Block())
        al, fr, mm, sg = alpha[0:H, :], far[0:H, :], m[0:H, :], seg[0:H, :]

        def last_of_segment(e):
            e.tensor_tensor_scan(mm[:, ::-1], fr[:, E:0:-1], mm[:, ::-1], 0.0 - BIG, ALU.add, ALU.max)

        @block.vector
        def _(e):
            e.tensor_scalar(fr, sg, 1.0, BIG, ALU.subtract, ALU.mult)
            if adst is not None:
                ad = adst[0:H, :]
                e.tensor_tensor(mm, sg[:, 1:E + 1], ad, ALU.mult)
                e.drain()
                e.tensor_tensor(mm, ad, mm, ALU.subtract)
                e.drain()
                e.tensor_tensor_scan(ad[:, ::-1], sg[:, E:0:-1], mm[:, ::-1], 0.0, ALU.mult, ALU.add)
                e.drain()
                e.tensor_tensor(al, al, ad, ALU.add)
                e.drain()
                e.scalar_tensor_tensor(out=al, in0=al, scalar=0.2, in1=al, op0=ALU.mult, op1=ALU.max)
            e.drain()
            e.tensor_tensor_scan(mm, fr[:, 0:E], al, 0.0 - BIG, ALU.add, ALU.max)
            e.drain()
            last_of_segment(e)
            e.drain()
            e.tensor_tensor(al, al, mm, ALU.subtract).then_inc(s_sub, 1)
            e.wait_ge(s_exp, 1)
            e.tensor_tensor_scan(mm, sg[:, 0:E], al, 0.0, ALU.mult, ALU.add)
            e.drain()
            last_of_segment(e)
            e.drain()
            e.tensor_scalar(mm, mm, 1e-16, None, ALU.add)
            e.drain()
            e.reciprocal(mm, mm)
            e.drain()
            e.tensor_tensor(al, al, mm, ALU.mult)

        @block.scalar
        def _(e):
            e.wait_ge(s_sub, 1)
            e.activation(al, al, ACT.Exp).then_inc(s_exp, 1)


def layer0_rows(nc, K, A, S, seg, attn):
    with ExitStack() as ctx:
        sb, ps, sem = scopes(nc, ctx, "l0")
        ow, xb, u, v, x1 = (sb(n, [R, J, D]) for n in ("ow", "xb", "u", "v", "x1"))
        idxb = sb("idxb", [R, J], U32)
        owT, vT, agg = (sb(n, [P, DB, C]) for n in ("owT", "vT", "agg"))
        carry = sb("carry", [P, DB])
        pT, pE, pR = ps("pT", [P, DB, 512]), ps("pE", [P, DB, 512]), ps("pR", [P, J, D])
        L = ln_buffers(sb, sem, "l0")
        s_go, s_idx, s_row, s_lin, s_T, s_Tc, s_ex, s_ag, s_r, s_u, s_g, s_n, s_xb, s_ga, s_t, s_x1, s_st = (
            sem(n) for n in ("s_go", "s_idx", "s_row", "s_lin", "s_T", "s_Tc", "s_ex", "s_ag", "s_r", "s_u",
                             "s_g", "s_n", "s_xb", "s_ga", "s_t", "s_x1", "s_st"))
        block = ctx.enter_context(nc.Block())
        half = K["E"] // C
        parts = ((0, True), (half, False))

        @block.sync
        def _(e):
            for base, msg in parts:
                with e.Fori(base, base + half) as n:
                    e.sem_inc(s_go, 1)
                    if msg:
                        e.dma_start(vT[:], S["V"][bass.ds(n, 1)].rearrange("o p k c -> p (o k) c")).then_inc(s_lin, 16)
                    wait(e, s_x1, n + 1)
                    e.dma_start(rows_of(S["X1"], n), x1[:]).then_inc(s_st, 16)
                    wait(e, s_st, n * 16 + 16)

        @block.gpsimd
        def _(e):
            for base, msg in parts:
                with e.Fori(base, base + half) as n:
                    wait(e, s_go, n + 1)
                    gather(e, A["x"], K["dstU"][0] if msg else K["srcU"][1], idxb, ow, n - base, s_idx, n + 1, s_row)
                    wait(e, s_row, n * (16 * J) + 16 * J)
                    e.tensor_tensor(xb[:], ow[:], wide(K["beta0"][:, :]), ALU.add).then_inc(s_xb, 1)
                    ln_pool(e, K, L, 2 * n + 1)
                    e.wait_ge(s_n, n + 1)
                    e.tensor_tensor(u[:], u[:], wide(K["gamma0"][:, :]), ALU.mult).then_inc(s_ga, 1)
                    e.wait_ge(s_xb, n + 1)
                    e.wait_ge(s_ga, n + 1)
                    e.tensor_tensor(u[:], u[:], xb[:], ALU.add).then_inc(s_t, 1)
                    ln_pool(e, K, L, 2 * n + 2)

        @block.tensor
        def _(e):
            for base, msg in parts:
                with e.Fori(base, base + half) as n:
                    if msg:
                        wait(e, s_go, n + 1)
                        for m in range(DB):
                            mm = e.matmul(pE[:, m, 0:C], K["rep0"][:, m * P:(m + 1) * P],
                                          attn[0:4, bass.ds(n * C, C)], start=True, stop=True)
                        mm.then_inc(s_ex, 1)
                    e.wait_ge(s_row, n * (16 * J) + 16 * J)
                    transposes(e, K, pT, ow, DB).then_inc(s_T, 1)
                    if msg:
                        e.wait_ge(s_ag, n + 1)
                    e.wait_ge(s_Tc, n + 1)
                    product_rows(e, pR, K["Wskip"], owT, DB, agg if msg else None, K["ident"]).then_inc(s_r, 1)

        @block.scalar
        def _(e):
            with e.Fori(0, 2 * half) as n:
                e.wait_ge(s_T, n + 1)
                e.activation(owT[:], pT[:, :, 0:C], ACT.Copy).then_inc(s_Tc, 1)
                e.wait_ge(s_u, n + 1)
                e.activation(v[:], u[:], ACT.Gelu).then_inc(s_g, 1)

        @block.vector
        def _(e):
            e.memset(carry[:], 0.0)
            e.drain()
            for base, msg in parts:
                with e.Fori(base, base + half) as n:
                    if msg:
                        wait(e, s_ex, n + 1)
                        e.wait_ge(s_lin, n * 16 + 16)
                        e.tensor_tensor(vT[:], vT[:], pE[:, :, 0:C], ALU.mult)
                        e.drain()
                        edge_scan(e, seg, n, vT, agg, carry, DB).then_inc(s_ag, 1)
                    e.wait_ge(s_r, n + 1)
                    e.tensor_tensor(u[:], pR[0:R, :, :], wide(K["bskip"][:, :]), ALU.add).then_inc(s_u, 1)
                    e.wait_ge(s_g, n + 1)
                    ln_vector(e, K, L, 2 * n + 1, v, u).then_inc(s_n, 1)
                    e.wait_ge(s_t, n + 1)
                    ln_vector(e, K, L, 2 * n + 2, u, x1).then_inc(s_x1, 1)
                    e.drain()


def layer1_rows(nc, K, A, S, seg, attn):
    with ExitStack() as ctx:
        sb, ps, sem = scopes(nc, ctx, "l1")
        x1, xb, u, v, x2, h = (sb(n, [R, J, D]) for n in ("x1", "xb", "u", "v", "x2", "h"))
        b_in = sb("b_in", [R, D])
        x2T, vT, agg = (sb(n, [P, DB, C]) for n in ("x2T", "vT", "agg"))
        carry = sb("carry", [P, DB])
        pT, pE, pR = ps("pT", [P, DB, 512]), ps("pE", [P, DB, 512]), ps("pR", [P, J, D])
        L = ln_buffers(sb, sem, "l1")
        s_b, s_lin, s_ex, s_ag, s_r, s_y, s_ya, s_xb, s_n, s_ga, s_t, s_x2, s_T, s_Tc, s_h, s_hc, s_st = (
            sem(n) for n in ("s_b", "s_lin", "s_ex", "s_ag", "s_r", "s_y", "s_ya", "s_xb", "s_n", "s_ga",
                             "s_t", "s_x2", "s_T", "s_Tc", "s_h", "s_hc", "s_st"))
        s_v = sem("s_v")
        block = ctx.enter_context(nc.Block())
        half = K["E"] // C
        parts = ((0, True), (half, False))

        @block.sync
        def _(e):
            e.dma_start(b_in[:], A["L2_gnn_b_in"].unsqueeze(0).broadcast_to([R, D])).then_inc(s_b, 16)
            for base, msg in parts:
                with e.Fori(base, base + half) as n:
                    e.dma_start(x1[:], rows_of(S["X1"], n)).then_inc(s_lin, 16)
                    if msg:
                        e.dma_start(vT[:], S["V"][bass.ds(n, 1)].rearrange("o p k c -> p (o k) c")).then_inc(s_v, 16)
                    wait(e, s_x2, n + 1)
                    e.dma_start(rows_of(S["X2"], n), x2[:]).then_inc(s_st, 16)
                    wait(e, s_hc, n + 1)
                    e.dma_start(rows_of(S["H"][0], n), h[:]).then_inc(s_st, 16)
                    wait(e, s_st, n * 32 + 32)

        @block.gpsimd
        def _(e):
            for base, msg in parts:
                with e.Fori(base, base + half) as n:
                    wait(e, s_lin, n * 16 + 16)
                    e.tensor_tensor(u[:], x1[:], wide(K["bias1"][:, :]), ALU.add).then_inc(s_y, 1)
                    e.tensor_tensor(xb[:], x1[:], wide(K["beta1"][:, :]), ALU.add).then_inc(s_xb, 1)
                    ln_pool(e, K, L, 2 * n + 1)
                    e.wait_ge(s_n, n + 1)
                    e.tensor_tensor(v[:], v[:], wide(K["gamma1"][:, :]), ALU.mult).then_inc(s_ga, 1)
                    e.wait_ge(s_xb, n + 1)
                    e.wait_ge(s_ga, n + 1)
                    e.tensor_tensor(v[:], v[:], xb[:], ALU.add).then_inc(s_t, 1)
                    ln_pool(e, K, L, 2 * n + 2)

        @block.tensor
        def _(e):
            for base, msg in parts:
                with e.Fori(base, base + half) as n:
                    if msg:
                        wait(e, s_lin, n * 16 + 16)
                        for m in range(DB):
                            mm = e.matmul(pE[:, m, 0:C], K["rep1"][:, m * P:(m + 1) * P],
                                          attn[0:8, bass.ds(n * C, C)], start=True, stop=True)
                        mm.then_inc(s_ex, 1)
                        e.wait_ge(s_ag, n + 1)
                        agg_rows(e, pR, agg, K["ident"]).then_inc(s_r, 1)
                    e.wait_ge(s_x2, n + 1)
                    transposes(e, K, pT, x2, DB).then_inc(s_T, 1)
                    e.wait_ge(s_Tc, n + 1)
                    product_rows(e, pR, K["W_in"], x2T, DB).then_inc(s_h, 1)

        @block.scalar
        def _(e):
            with e.Fori(0, 2 * half) as n:
                e.wait_ge(s_T, n + 1)
                e.activation(x2T[:], pT[:, :, 0:C], ACT.Copy).then_inc(s_Tc, 1)

        @block.vector
        def _(e):
            e.memset(carry[:], 0.0)
            e.wait_ge(s_b, 16)
            e.drain()
            for base, msg in parts:
                with e.Fori(base, base + half) as n:
                    if msg:
                        wait(e, s_ex, n + 1)
                        e.wait_ge(s_v, n * 16 + 16)
                        e.tensor_tensor(vT[:], vT[:], pE[:, :, 0:C], ALU.mult)
                        e.drain()
                        edge_scan(e, seg, n, vT, agg, carry, DB).then_inc(s_ag, 1)
                        wait(e, s_r, n + 1)
                        e.wait_ge(s_y, n + 1)
                        e.tensor_tensor(u[:], u[:], pR[0:R, :, :], ALU.add)
                        e.drain()
                    else:
                        wait(e, s_y, n + 1)
                    ln_vector(e, K, L, 2 * n + 1, u, v).then_inc(s_n, 1)
                    e.wait_ge(s_t, n + 1)
                    ln_vector(e, K, L, 2 * n + 2, v, x2).then_inc(s_x2, 1)
                    e.wait_ge(s_h, n + 1)
                    e.tensor_tensor(h[:], pR[0:R, :, :], wide(b_in[:, :]), ALU.add).then_inc(s_hc, 1)
                    e.drain()


def layer2_rows(nc, K, A, S, seg, l):
    tail = l == 2
    with ExitStack() as ctx:
        sb, ps, sem = scopes(nc, ctx, f"l2{l}")
        ow, ms, h, x2, u, x3 = (sb(n, [R, J, D]) for n in ("ow", "ms", "h", "x2", "u", "x3"))
        bias = sb("bias", [R, D])
        idxb = [sb(f"idxb{i}", [R, J], U32) for i in range(3)]
        owT, agg, hT = (sb(n, [P, DB, C]) for n in ("owT", "agg", "hT"))
        carry = sb("carry", [P, DB])
        pT, pM, pR = ps("pT", [P, DB, 512]), ps("pM", [P, DB, 512]), ps("pR", [P, J, D])
        pR2 = ps("pR2", [P, J, D])
        L = ln_buffers(sb, sem, "l2")
        s_b, s_go, s_idx, s_own, s_x2, s_msg, s_w, s_T, s_M, s_Tc, s_ag, s_r, s_b1, s_h, s_hT, s_hTc, s_o, s_x3, s_st = (
            sem(n) for n in ("s_b", "s_go", "s_idx", "s_own", "s_x2", "s_msg", "s_w", "s_T", "s_M", "s_Tc",
                             "s_ag", "s_r", "s_b1", "s_h", "s_hT", "s_hTc", "s_o", "s_x3", "s_st"))
        block = ctx.enter_context(nc.Block())
        half = K["E"] // C
        parts = ((0, False), (half, True))
        Wself, Wagg = K[f"Wself{l}"], K[f"Wagg{l}"]
        s_ownG, s_x2G = sem("s_ownG"), sem("s_x2G")

        @block.sync
        def _(e):
            e.dma_start(bias[:], A["L2_gnn_b_hid"][l].unsqueeze(0).broadcast_to([R, D])).then_inc(s_b, 16)
            for base, msg in parts:
                with e.Fori(base, base + half) as n:
                    e.sem_inc(s_go, 1)
                    if not (msg and l == 0):
                        e.dma_start(ow[:], rows_of(S["H"][l], n)).then_inc(s_own, 16)
                    if tail and not msg:
                        e.dma_start(x2[:], rows_of(S["X2"], n)).then_inc(s_x2, 16)
                    if tail:
                        wait(e, s_x3, n + 1)
                        e.dma_start(rows_of(S["X3"], n), x3[:]).then_inc(s_st, 16)
                    else:
                        wait(e, s_h, n + 1)
                        e.dma_start(rows_of(S["H"][l + 1], n), h[:]).then_inc(s_st, 16)
                    wait(e, s_st, n * 16 + 16)

        @block.gpsimd
        def _(e):
            for base, msg in parts:
                with e.Fori(base, base + half) as n:
                    wait(e, s_go, n + 1)
                    if msg:
                        g = 1 + (l == 0) + tail
                        m = n - base
                        gather(e, S["H"][l], K["m1d"] if l == 0 else K["m2d"], idxb[0], ms, m, s_idx, m * g + 1, s_msg)
                        if l == 0:
                            gather(e, S["H"][l], K["ownB"], idxb[1], ow, m, s_idx, m * g + 2, s_ownG)
                        if tail:
                            gather(e, S["X2"], K["ownB"], idxb[2], x2, m, s_idx, m * g + 2, s_x2G)
                    if tail:
                        ln_pool(e, K, L, n + 1)

        def rows_there(e, n, base, gathered, s_line, s_gather):
            if gathered:
                wait(e, s_gather, (n - base) * (16 * J) + 16 * J)
            else:
                wait(e, s_line, n * 16 + 16)

        @block.tensor
        def _(e):
            for base, msg in parts:
                with e.Fori(base, base + half) as n:
                    rows_there(e, n, base, msg and l == 0, s_own, s_ownG)
                    transposes(e, K, pT, ow, DB).then_inc(s_T, 1)
                    if msg:
                        wait(e, s_w, n - base + 1)
                        transposes(e, K, pM, ms, DB).then_inc(s_M, 1)
                        wait(e, s_ag, n - base + 1)
                    e.wait_ge(s_Tc, n + 1)
                    for j in range(J):
                        terms = [(owT, Wself)] + ([(agg, Wagg)] if msg else [])
                        for a, (xT, w) in enumerate(terms):
                            for k in range(DB):
                                mm = e.matmul(pR[0:R, j, :], xT[:, k, j * R:(j + 1) * R], w[:, k, :],
                                              start=a == 0 and k == 0, stop=a == len(terms) - 1 and k == DB - 1)
                    mm.then_inc(s_r, 1)
                    if tail:
                        e.wait_ge(s_h, n + 1)
                        transposes(e, K, pT, h, DB).then_inc(s_hT, 1)
                        e.wait_ge(s_hTc, n + 1)
                        product_rows(e, pR2, K["W_out"], hT, DB).then_inc(s_o, 1)

        @block.scalar
        def _(e):
            with e.Fori(0, 2 * half) as n:
                e.wait_ge(s_T, n + 1)
                e.activation(owT[:], pT[:, :, 0:C], ACT.Copy).then_inc(s_Tc, 1)
                e.wait_ge(s_b1, n + 1)
                e.activation(h[:], u[:], ACT.Relu).then_inc(s_h, 1)
                if tail:
                    e.wait_ge(s_hT, n + 1)
                    e.activation(hT[:], pT[:, :, 0:C], ACT.Copy).then_inc(s_hTc, 1)

        @block.vector
        def _(e):
            e.memset(carry[:], 0.0)
            e.wait_ge(s_b, 16)
            e.drain()
            for base, msg in parts:
                with e.Fori(base, base + half) as n:
                    if msg:
                        m = n - base
                        wait(e, s_msg, m * (16 * J) + 16 * J)
                        times_columns(e, ms, K["inv2"], m, D).then_inc(s_w, 1)
                        wait(e, s_M, m + 1)
                        edge_scan(e, seg, m, pM, agg, carry, DB).then_inc(s_ag, 1)
                    wait(e, s_r, n + 1)
                    e.tensor_tensor(u[:], pR[0:R, :, :], wide(bias[:, :]), ALU.add).then_inc(s_b1, 1)
                    if tail:
                        wait(e, s_o, n + 1)
                        e.tensor_tensor(u[:], pR2[0:R, :, :], wide(K["b_out"][:, :]), ALU.add)
                        e.drain()
                        rows_there(e, n, base, msg, s_x2, s_x2G)
                        e.tensor_tensor(u[:], u[:], x2[:], ALU.add)
                        e.drain()
                        ln_vector(e, K, L, n + 1, u, x3).then_inc(s_x3, 1)
                    e.drain()


def layer3_rows(nc, K, A, S, seg, l):
    with ExitStack() as ctx:
        sb, ps, sem = scopes(nc, ctx, f"l3{l}")
        W_in = [D, 2 * D, D][l]
        nb = W_in // P
        ow, ms = sb("ow", [R, J, W_in]), sb("ms", [R, J, W_in])
        wideout = 2 * D
        u = sb("u", [R, J, wideout if l < 2 else D])
        g = sb("g", [R, J, wideout if l < 2 else D])
        z = sb("z", [R, J, D])
        bias = sb("bias", [R, wideout if l < 2 else D])
        x3 = sb("x3", [R, J, D])
        idxb = [sb(f"idxb{i}", [R, J], U32) for i in range(3)]
        agg, tT = sb("agg", [P, nb, C]), sb("tT", [P, nb, C])
        gT = sb("gT", [P, 2 * DB, C]) if l == 1 else None
        carry = sb("carry", [P, nb])
        pT, pM = ps("pT", [P, 4, 512]), ps("pM", [P, 4, 512])
        pRows = pT[:, 0:2, :].rearrange("p a (b d) -> p (a b) d", d=D)
        L = ln_buffers(sb, sem, "l3")
        s_b, s_go, s_idx, s_own, s_x3, s_msg, s_w, s_T, s_M, s_ag, s_tT, s_r, s_b1, s_g, s_gT, s_gTc, s_z, s_zc, s_st, s_out = (
            sem(n) for n in ("s_b", "s_go", "s_idx", "s_own", "s_x3", "s_msg", "s_w", "s_T", "s_M", "s_ag",
                             "s_tT", "s_r", "s_b1", "s_g", "s_gT", "s_gTc", "s_z", "s_zc", "s_st", "s_out"))
        block = ctx.enter_context(nc.Block())
        half = K["E"] // C
        parts = ((0, True), (half, False))
        src = [S["X3"], S["G"], S["Z"]][l]
        vec = [A["L3_gnn_b1"], A["L3_gnn_b2"], A["L3_gnn_b3"]][l]
        G = 16 * J

        s_ownG, s_x3G, s_sc = sem("s_ownG"), sem("s_x3G"), sem("s_sc")
        loaded_before = half if l == 0 else 0

        def own_there(e, n, msg):
            if l == 0 and msg:
                wait(e, s_ownG, n * G + G)
            else:
                wait(e, s_own, (n - loaded_before) * 16 + 16)

        def x3_there(e, n, msg):
            if msg:
                wait(e, s_x3G, n * G + G)
            else:
                wait(e, s_x3, (n - half) * 16 + 16)

        @block.sync
        def _(e):
            e.dma_start(bias[:], vec.unsqueeze(0).broadcast_to([R, vec.shape[0]])).then_inc(s_b, 16)
            for base, msg in parts:
                with e.Fori(base, base + half) as n:
                    e.sem_inc(s_go, 1)
                    if not (msg and l == 0):
                        e.dma_start(ow[:], rows_of(src, n)).then_inc(s_own, 16)
                    if l == 2 and not msg:
                        e.dma_start(x3[:], rows_of(S["X3"], n)).then_inc(s_x3, 16)
                    if l == 0:
                        wait(e, s_g, n + 1)
                        e.dma_start(rows_of(S["G"], n), g[:]).then_inc(s_st, 16)
                        wait(e, s_st, n * 16 + 16)
                    elif l == 1:
                        wait(e, s_zc, n + 1)
                        e.dma_start(rows_of(S["Z"], n), z[:]).then_inc(s_st, 16)
                        wait(e, s_st, n * 16 + 16)
                    else:
                        wait(e, s_sc, n * G + G)

        @block.gpsimd
        def _(e):
            for base, msg in parts:
                with e.Fori(base, base + half) as n:
                    wait(e, s_go, n + 1)
                    if l < 2 and msg:
                        g_ = 1 + (l == 0)
                        gather(e, src, K["m2s"] if l == 0 else K["m1s"], idxb[0], ms, n, s_idx, n * g_ + 1, s_msg)
                        if l == 0:
                            gather(e, src, K["ownA"], idxb[1], ow, n, s_idx, n * g_ + 2, s_ownG)
                    if l == 2:
                        if msg:
                            gather(e, src, K["m1s"], idxb[0], ms, n, s_idx, 3 * n + 1, s_msg)
                            gather(e, S["X3"], K["ownA"], idxb[1], x3, n, s_idx, 3 * n + 2, s_x3G)
                            t, col = 3 * n + 3, K["outA"]
                        else:
                            t, col = n - base + 3 * half + 1, K["outB"]
                        e.tensor_copy(idxb[2][:], col[:, bass.ds((n - base) * J, J)]).then_inc(s_idx, 1)
                        wait(e, s_idx, t)
                        ln_pool(e, K, L, n + 1)
                        wait(e, s_out, n + 1)
                        for j in range(J):
                            e.indirect_dma_start(A["out"], bass.IndirectOffsetOnAxis(ap=idxb[2][:, j:j + 1], axis=0),
                                                 z[:, j, :], None, bounds_check=K["N"] - 1, oob_is_err=False)\
                                .then_inc(s_sc, 16)

        @block.tensor
        def _(e):
            for base, msg in parts:
                with e.Fori(base, base + half) as n:
                    if l < 2:
                        if msg:
                            wait(e, s_w, 2 * n + 2)
                            transposes(e, K, pT, ow, nb)
                            transposes(e, K, pM, ms, nb).then_inc(s_M, 1)
                        else:
                            own_there(e, n, msg)
                            transposes(e, K, pT, ow, nb).then_inc(s_T, 1)
                        e.wait_ge(s_tT, n + 1)
                        w = K["W1"] if l == 0 else K["W2"]
                        for j in range(J):
                            for k in range(nb):
                                mm = e.matmul(pT[0:R, j, :], tT[:, k, j * R:(j + 1) * R], w[:, k, :],
                                              start=k == 0, stop=k == nb - 1)
                        mm.then_inc(s_r, 1)
                    elif msg:
                        wait(e, s_w, 2 * n + 2)
                        transposes(e, K, pM, ms, nb).then_inc(s_M, 1)
                        wait(e, s_ag, n + 1)
                        agg_rows(e, pRows, agg, K["ident"]).then_inc(s_r, 1)
                    if l == 1:
                        e.wait_ge(s_g, n + 1)
                        transposes(e, K, pM, g, 2 * DB).then_inc(s_gT, 1)
                        e.wait_ge(s_gTc, n + 1)
                        product_rows(e, pRows, K["W3"], gT, 2 * DB).then_inc(s_z, 1)

        @block.scalar
        def _(e):
            with e.Fori(0, 2 * half) as n:
                e.wait_ge(s_b1, n + 1)
                e.activation(g[:], u[:], ACT.Relu).then_inc(s_g, 1)
                if l == 1:
                    e.wait_ge(s_gT, n + 1)
                    e.activation(gT[:, 0:2, :], pM[:, 0:2, 0:C], ACT.Copy)
                    e.activation(gT[:, 2:4, :], pM[:, 2:4, 0:C], ACT.Copy).then_inc(s_gTc, 1)

        @block.vector
        def _(e):
            e.memset(carry[:], 0.0)
            e.wait_ge(s_b, 16)
            e.drain()
            for base, msg in parts:
                with e.Fori(base, base + half) as n:
                    if msg:
                        own_there(e, n, msg)
                        times_columns(e, ow, K["self3"], n, W_in).then_inc(s_w, 1)
                        wait(e, s_msg, n * G + G)
                        times_columns(e, ms, K["norm3"], n, W_in).then_inc(s_w, 1)
                        wait(e, s_M, n + 1)
                        edge_scan(e, seg, n, pM, agg, carry, nb).then_inc(s_ag, 1)
                    if l < 2:
                        if msg:
                            e.tensor_tensor(tT[:], pT[:, 0:nb, 0:C], agg[:], ALU.add).then_inc(s_tT, 1)
                        else:
                            wait(e, s_T, n - base + 1)
                            e.tensor_copy(tT[:], pT[:, 0:nb, 0:C]).then_inc(s_tT, 1)
                        wait(e, s_r, n + 1)
                        e.tensor_tensor(u[:], pT[0:R, :, :], bias[:, :].unsqueeze(1).broadcast_to([R, J, wideout]),
                                        ALU.add).then_inc(s_b1, 1)
                        if l == 1:
                            wait(e, s_z, n + 1)
                            e.tensor_copy(z[:], pRows[0:R, :, :]).then_inc(s_zc, 1)
                    else:
                        if msg:
                            wait(e, s_r, n + 1)
                            e.tensor_tensor(ow[:], ow[:], pRows[0:R, :, :], ALU.add)
                            e.drain()
                        else:
                            own_there(e, n, msg)
                        e.tensor_tensor(u[:], ow[:], wide(bias[:, :]), ALU.add).then_inc(s_b1, 1)
                        wait(e, s_g, n + 1)
                        x3_there(e, n, msg)
                        e.tensor_tensor(u[:], g[:], x3[:], ALU.add)
                        e.drain()
                        ln_vector(e, K, L, n + 1, u, z).then_inc(s_out, 1)
                    e.drain()


def build(nc, A):
    K = {}
    N, _ = A["x"].shape
    E = A["src"].shape[0]
    K["N"], K["E"] = N, E

    def scratch(name, shape, d=F32):
        return nc.dram_tensor(name, shape, d, kind="Internal").ap()
    S = dict(
        edges=[scratch(f"edges{i}", [E, 4], I32) for i in range(2)],
        key=[scratch(f"key{i}", [TILES, R]) for i in range(2)],
        nodes=scratch("nodes", [2 * N, 2]),
        V=scratch("V", [E // C, P, DB, C]),
        X1=scratch("X1", [2 * E, D]), X2=scratch("X2", [2 * E, D]), X3=scratch("X3", [2 * E, D]),
        H=[scratch(f"H{i}", [2 * E, D]) for i in range(3)],
        G=scratch("G", [2 * E, 2 * D]), Z=scratch("Z", [2 * E, D]))
    with ExitStack() as ctx:
        K["sb"] = scopes(nc, ctx, "k")[0]
        for n in ("srcF", "dstF"):
            K[n] = [K["sb"](f"{n}{i}", [R, TILES]) for i in range(2)]
        for n in ("srcU", "dstU"):
            K[n] = [K["sb"](f"{n}{i}", [R, TILES], U32) for i in range(2)]
        for n in ("ordU", "m1s", "m2s", "m1d", "m2d", "ownA", "ownB", "outA", "outB"):
            K[n] = K["sb"](n, [R, TILES], U32)
        for n in ("inv2", "norm3", "self3"):
            K[n] = K["sb"](n, [R, TILES])
        K["WAs"], K["WAd"], K["WAe"] = K["sb"]("WAs", [P, DB, 8]), K["sb"]("WAd", [P, DB, 8]), K["sb"]("WAe", [64, 8])
        K["rep0"], K["rep1"], K["sum0"] = K["sb"]("rep0", [4, D]), K["sb"]("rep1", [8, D]), K["sb"]("sum0", [P, DB, 4])
        load_constants(nc, K, A)
        att_weights(nc, K, A)
        rank_edges(nc, K, A, "rank0", A["dst"], S["edges"][0])
        rank_edges(nc, K, A, "rank1", A["src"], S["edges"][1])
        load_sorted(nc, K, A, S)
        node_maps(nc, K, A, S)
        dense(nc, K, A, N)
        with ExitStack() as c2:
            sb = scopes(nc, c2, "attn")[0]
            seg, alpha = sb("seg", [P, E + 1]), sb("alpha", [8, E])
            load_segments(nc, K, "seg_a", S, 0, seg)
            scores0(nc, K, A, S, alpha)
            softmax(nc, K, "sm0", 4, seg, alpha, None)
            layer0_rows(nc, K, A, S, seg, alpha)
            with ExitStack() as c3:
                adst = scopes(nc, c3, "attn1")[0]("adst", [8, E])
                scores1(nc, K, A, S, alpha, adst)
                softmax(nc, K, "sm1", 8, seg, alpha, adst)
            layer1_rows(nc, K, A, S, seg, alpha)
        with ExitStack() as c2:
            seg = scopes(nc, c2, "l2s")[0]("seg", [P, E + 1])
            load_segments(nc, K, "seg_b", S, 1, seg)
            for l in range(3):
                layer2_rows(nc, K, A, S, seg, l)
        with ExitStack() as c2:
            seg = scopes(nc, c2, "l3s")[0]("seg", [P, E + 1])
            load_segments(nc, K, "seg_c", S, 0, seg)
            for l in range(3):
                layer3_rows(nc, K, A, S, seg, l)


_INS = ['x', 'src', 'dst', 'edge_attr_64', 'L0_gnn_Wq', 'L0_gnn_bq', 'L0_gnn_Wk', 'L0_gnn_bk', 'L0_gnn_Wv',
        'L0_gnn_bv', 'L0_gnn_Wskip', 'L0_gnn_bskip', 'L0_gnn_gamma', 'L0_gnn_beta_ln', 'L1_gnn_W',
        'L1_gnn_W_e', 'L1_gnn_att_src', 'L1_gnn_att_dst', 'L1_gnn_att_edge', 'L1_gnn_bias', 'L1_gnn_gamma',
        'L1_gnn_beta', 'L2_gnn_W_in', 'L2_gnn_b_in', 'L2_gnn_W_agg', 'L2_gnn_W_self', 'L2_gnn_b_hid',
        'L2_gnn_W_out', 'L2_gnn_b_out', 'L3_gnn_W1', 'L3_gnn_b1', 'L3_gnn_W2', 'L3_gnn_b2', 'L3_gnn_W3',
        'L3_gnn_b3']


def kernel(**inputs):
    import numpy as _np
    import concourse.bacc as _bacc
    from concourse import mybir as _mybir
    from concourse.bass_utils import run_bass_kernel_spmd as _run

    nc = _bacc.Bacc("TRN2", target_bir_lowering=False, num_devices=1)
    arrays, args = {}, {}
    for name in _INS:
        a = _np.ascontiguousarray(inputs[name])
        arrays[f"in_{name}_dram"] = a
        args[name] = nc.dram_tensor(f"in_{name}_dram", a.shape, _mybir.dt.from_np(a.dtype), kind="ExternalInput").ap()
    out_shape = inputs['x'].shape
    args["out"] = nc.dram_tensor("out_0_dram", out_shape, _mybir.dt.float32, kind="ExternalOutput").ap()
    build(nc, args)
    r = _run(nc, [arrays], core_ids=[0])
    return r.results[0]["out_0_dram"]
```

```python
from contextlib import ExitStack

import concourse.bass as bass
from concourse import mybir

F32 = mybir.dt.float32
I32 = mybir.dt.int32
U32 = mybir.dt.uint32
BF16 = mybir.dt.bfloat16
ALU = mybir.AluOpType
ACT = mybir.ActivationFunctionType
AX = mybir.AxisListType

P = 128
R = 125
J = 4
C = R * J
D = 256
DB = D // P
EPS = 1e-5
BIG = 1e30


def rows_of(table, n):
    return table[bass.ds(n * C, C), :].rearrange("(j p) d -> p j d", p=R)


def wide(row, j=J):
    return row.unsqueeze(1).broadcast_to([row.shape[0], j, row.shape[1]])



def wait(e, s, value):
    e.wait_ge(s, value)
    e.nop(nofuse=True)


def transposes(e, K, out, rows, blocks, width=P):
    for k in range(blocks):
        for j in range(J):
            last = e.transpose(out[0:width, k, j * R:(j + 1) * R],
                               rows[:, j, k * width:(k + 1) * width], K["ident"][0:R, 0:R])
    return last


def product_T(e, out, w, m, xT, blocks, first=True, last=True):
    for k in range(blocks):
        mm = e.matmul(out, w[:, k, m * P:(m + 1) * P], xT[:, k, :],
                      start=first and k == 0, stop=last and k == blocks - 1)
    return mm


def product_rows(e, out, w, xT, blocks, aggT=None, ident=None):
    for j in range(J):
        if aggT is None:
            for k in range(blocks):
                mm = e.matmul(out[0:R, j, :], xT[:, k, j * R:(j + 1) * R], w[:, k, :],
                              start=k == 0, stop=k == blocks - 1)
        else:
            for m in range(DB):
                half = out[0:R, j, m * P:(m + 1) * P]
                for k in range(blocks):
                    e.matmul(half, xT[:, k, j * R:(j + 1) * R], w[:, k, m * P:(m + 1) * P],
                             start=k == 0, stop=False)
                mm = e.matmul(half, aggT[:, m, j * R:(j + 1) * R], ident[:, :], start=False, stop=True)
    return mm


def agg_rows(e, out, aggT, ident):
    for j in range(J):
        for k in range(DB):
            mm = e.transpose(out[0:R, j, k * P:(k + 1) * P], aggT[:, k, j * R:(j + 1) * R], ident[:, :])
    return mm


def ln_stats(e, L, t, src):
    for j in range(J):
        ins = e.bn_stats(L["stats"][:, j, :], src[:, j, :])
    ins.then_inc(L["s_stats"], 1)
    wait(e, L["s_stats"], t)
    for j in range(J):
        ins = e.bn_aggr(L["mv"][:, j, :], L["stats"][:, j, :])
    ins.then_inc(L["s_var"], 1)


def ln_scale(e, L, t, src, dst):
    e.wait_ge(L["s_rstd"], t)
    for j in range(J):
        ins = e.tensor_scalar(dst[:, j, :], src[:, j, :], L["mv"][:, j, 0:1], L["rstd"][:, j:j + 1],
                              ALU.subtract, ALU.mult)
    return ins


def ln_affine(e, L, t, src, gamma, plus, dst):
    wait(e, L["s_var"], t)
    for j in range(J):
        e.scalar_tensor_tensor(out=dst[:, j, :], in0=src[:, j, :], scalar=L["mv"][:, j, 0:1], in1=gamma[:, :],
                               op0=ALU.subtract, op1=ALU.mult)
    e.drain()
    e.wait_ge(L["s_rstd"], t)
    for j in range(J):
        ins = e.scalar_tensor_tensor(out=dst[:, j, :], in0=dst[:, j, :], scalar=L["rstd"][:, j:j + 1],
                                     in1=plus[:, j, :], op0=ALU.mult, op1=ALU.add)
    return ins


def ln_vector(e, K, L, t, src, dst):
    ln_stats(e, L, t, src)
    return ln_scale(e, L, t, src, dst)


def ln_pool(e, K, L, t):
    wait(e, L["s_var"], t)
    e.tensor_scalar(L["vare"][:, :], L["mv"][:, :, 1], EPS, None, ALU.add).then_inc(L["s_vare"], 1)
    e.wait_ge(L["s_vare"], t)
    e.tensor_tensor(L["rstd"][:, :], L["vare"][:, :], K["mhalf"][:, :], ALU.pow).then_inc(L["s_rstd"], 1)


def ln_buffers(sb, sem, name):
    return dict(
        stats=sb(f"{name}_stats", [R, J, 6]), mv=sb(f"{name}_mv", [R, J, 2]),
        vare=sb(f"{name}_vare", [R, J]), rstd=sb(f"{name}_rstd", [R, J]),
        s_stats=sem(f"{name}_s_stats"), s_var=sem(f"{name}_s_var"),
        s_vare=sem(f"{name}_s_vare"), s_rstd=sem(f"{name}_s_rstd"))


def scopes(nc, ctx, name):
    def sb(n, s, d=F32):
        return ctx.enter_context(nc.sbuf_tensor(f"{name}_{n}", s, d))

    def ps(n, s, d=F32):
        return ctx.enter_context(nc.psum_tensor(f"{name}_{n}", s, d))

    sems = []

    def sem(n):
        sems.append(nc.alloc_semaphore(name=f"{name}_{n}"))
        return sems[-1]

    def done():
        if sems:
            nc.clear_and_free_semaphores(sems)
            nc.all_engine_barrier()
    ctx.callback(done)
    return sb, ps, sem



def load_constants(nc, K, A):
    mats = {"Wq": A["L0_gnn_Wq"], "Wk": A["L0_gnn_Wk"], "Wv": A["L0_gnn_Wv"], "Wskip": A["L0_gnn_Wskip"],
            "W": A["L1_gnn_W"], "W_in": A["L2_gnn_W_in"], "W_out": A["L2_gnn_W_out"],
            "W1": A["L3_gnn_W1"], "W2": A["L3_gnn_W2"], "W3": A["L3_gnn_W3"]}
    for l in range(3):
        mats[f"Wagg{l}"] = A["L2_gnn_W_agg"][l]
        mats[f"Wself{l}"] = A["L2_gnn_W_self"][l]
    cols = {"bq": A["L0_gnn_bq"], "bk": A["L0_gnn_bk"], "bv": A["L0_gnn_bv"], "b_in": A["L2_gnn_b_in"],
            "b1": A["L3_gnn_b1"], "b2": A["L3_gnn_b2"]}
    for l in range(3):
        cols[f"b_hid{l}"] = A["L2_gnn_b_hid"][l]
    rows = {"bskip": A["L0_gnn_bskip"], "gamma0": A["L0_gnn_gamma"], "beta0": A["L0_gnn_beta_ln"],
            "bias1": A["L1_gnn_bias"], "gamma1": A["L1_gnn_gamma"], "beta1": A["L1_gnn_beta"],
            "b_out": A["L2_gnn_b_out"], "b3": A["L3_gnn_b3"]}
    sb = K["sb"]
    for n, m in mats.items():
        K[n] = sb(n, [P, m.shape[0] // P, m.shape[1]])
    for n, m in cols.items():
        K[n] = sb(n, [P, m.shape[0] // P])
    for n, m in rows.items():
        K[n] = sb(n, [R, m.shape[0]])
    K["ident"] = sb("ident", [P, P])
    K["mhalf"] = sb("mhalf", [R, J])
    with ExitStack() as ctx:
        sem = scopes(nc, ctx, "const")[2]
        s_w, s_i0, s_i1 = sem("s_w"), sem("s_i0"), sem("s_i1")
        block = ctx.enter_context(nc.Block())

        @block.sync
        def _(e):
            for n, m in mats.items():
                e.dma_start(K[n][:, :, :], m.rearrange("(k p) n -> p k n", p=P)).then_inc(s_w, 16)
            for n, m in cols.items():
                e.dma_start(K[n][:, :], m.rearrange("(k p) -> p k", p=P),
                            allow_slow_non_contiguous=True).then_inc(s_w, 16)
            for n, m in rows.items():
                e.dma_start(K[n][:, :], m.unsqueeze(0).broadcast_to([R, m.shape[0]])).then_inc(s_w, 16)
            e.wait_ge(s_w, 16 * (len(mats) + len(cols) + len(rows)))

        @block.gpsimd
        def _(e):
            e.memset(K["mhalf"][:, :], -0.5)
            e.memset(K["ident"][:, :], 0.0).then_inc(s_i0, 1)
            e.wait_ge(s_i0, 1)
            e.affine_select(out=K["ident"][:, :], in_=K["ident"][:, :], compare_op=ALU.not_equal, fill=1.0,
                            base=0, pattern=[[-1, P]], channel_multiplier=1).then_inc(s_i1, 1)


def dense(nc, K, A, N, jobs=()):
    chunks = N // C
    RING = 2
    with ExitStack() as ctx:
        sb, ps, sem = scopes(nc, ctx, "dense")
        xr, xb, u, v = (sb(n, [R, J, D]) for n in ("xr", "xb", "u", "v"))
        x1, x2, x3, xres = (sb(n, [R, J, D]) for n in ("x1", "x2", "x3", "xres"))
        t3, o, z = (sb(n, [R, J, D]) for n in ("t3", "o", "z"))
        xT, x2T, x3T = (sb(n, [P, DB, C]) for n in ("xT", "x2T", "x3T"))
        h = [sb(f"h{i}", [P, DB, C]) for i in range(2)]
        g1, g2 = sb("g1", [P, 2 * DB, C]), sb("g2", [P, 2 * DB, C])
        pF = ps("pF", [P, DB, 512])
        pG = ps("pG", [P, DB, 512])
        pGr = pG[:, :, :].rearrange("p a (b d) -> p (a b) d", d=D)
        pO = ps("pO", [P, J, D])
        ring = ps("ring", [P, RING, 512])
        LF, LB, LO = (ln_buffers(sb, sem, n) for n in ("front", "back", "last"))
        s_x, s_xT, s_xTc, s_skip = sem("s_x"), sem("s_xT"), sem("s_xTc"), sem("s_skip")
        s_u, s_g, s_xb0, s_t0 = sem("s_u"), sem("s_g"), sem("s_xb0"), sem("s_t0")
        s_x1, s_y, s_xb1, s_t1 = sem("s_x1"), sem("s_y"), sem("s_xb1"), sem("s_t1")
        s_x2, s_x2T, s_x2Tc = sem("s_x2"), sem("s_x2T"), sem("s_x2Tc")
        s_mm, s_ev = sem("s_mm"), sem("s_ev")
        s_o, s_oa, s_ob, s_x3, s_x3T, s_x3Tc, s_xres = (
            sem(n) for n in ("s_o", "s_oa", "s_ob", "s_x3", "s_x3T", "s_x3Tc", "s_xres"))
        s_z, s_za, s_zr, s_zb, s_out, s_st = (sem(n) for n in ("s_z", "s_za", "s_zr", "s_zb", "s_out", "s_st"))

        back1 = [(K["W_in"], x2T, DB, m, K["b_in"], h[0], False) for m in range(DB)]
        for l in range(3):
            back1 += [(K[f"Wself{l}"], h[l % 2], DB, m, K[f"b_hid{l}"], h[(l + 1) % 2], True)
                      for m in range(DB)]
        hL = h[1]
        back2 = [(K["W1"], x3T, DB, m, K["b1"], g1, True) for m in range(2 * DB)]
        back2 += [(K["W2"], g1, 2 * DB, m, K["b2"], g2, True) for m in range(2 * DB)]
        G1, G2 = len(back1), len(back2)

        def ring_at(c, part, g):
            if part == 1:
                return c * (G1 + G2) - (G2 if not isinstance(c, int) or c > 0 else 0) + g
            return (c + 1) * G1 + c * G2 + (G1 if not isinstance(c, int) or c < chunks - 1 else 0) + g

        block = ctx.enter_context(nc.Block())

        def turns(e, turn, engine):
            turn(0, True, False)
            c = 1
            for count, each, after in jobs + ((chunks - 3 - sum(j[0] for j in jobs), {}, {}),):
                with e.Fori(c, c + count) as i:
                    turn(i, True, True)
                    if engine in each:
                        each[engine](e, i - c)
                if engine in after:
                    after[engine](e)
                c += count
            turn(chunks - 2, True, True)
            turn(chunks - 1, False, True)

        @block.sync
        def _(e):
            e.dma_start(xr[:], rows_of(A["x"], 0)).then_inc(s_x, 16)
            e.wait_ge(s_t0, 1)
            e.dma_start(xr[:], rows_of(A["x"], 1)).then_inc(s_x, 16)

            def turn(c, front, back):
                if not isinstance(c, int) or c < chunks - 2:
                    if front:
                        wait(e, s_t0, c + 2)
                        e.dma_start(xr[:], rows_of(A["x"], c + 2)).then_inc(s_x, 16)
                if back:
                    wait(e, s_out, c)
                    e.dma_start(rows_of(A["out"], c - 1), o[:]).then_inc(s_st, 16)
            turns(e, turn, "sync")
            e.wait_ge(s_out, chunks)
            e.dma_start(rows_of(A["out"], chunks - 1), o[:]).then_inc(s_st, 16)
            e.wait_ge(s_st, 16 * chunks + 1)

        def pe_group(e, c, part, g):
            groups = back1 if part == 1 else back2
            w, xin, nb, m, _, _, _ = groups[g]
            at = ring_at(c, part, g)
            first = g > 0 and groups[g - 1][1] is not xin
            e.wait_ge(s_ev, at + 1)
            for k in range(nb):
                if first:
                    e.wait_ge(s_ev, at - nb + k + 1 + RING)
                mm = e.matmul(ring[:, g % RING, 0:C], w[:, k, m * P:(m + 1) * P], xin[:, k, :],
                              start=k == 0, stop=k == nb - 1)
            mm.then_inc(s_mm, 1)

        def pe_x(e, c):
            e.wait_ge(s_x, 16 * c + 16)
            if not isinstance(c, int) or c > 0:
                e.wait_ge(s_u, c)
            transposes(e, K, pG, xr, DB).then_inc(s_xT, 1)

        def pe_skip(e, c):
            e.wait_ge(s_xTc, c + 1)
            product_rows(e, pGr, K["Wskip"], xT, DB).then_inc(s_skip, 1)

        def pe_x2(e, c):
            e.wait_ge(s_x2, c + 1)
            transposes(e, K, pF, x2, DB).then_inc(s_x2T, 1)

        def pe_back2(e, c):
            e.wait_ge(s_x3Tc, c + 1)
            for g in range(G2):
                pe_group(e, c, 2, g)
            e.wait_ge(s_ev, ring_at(c, 2, G2) + RING)
            e.wait_ge(s_oa, c + 3 if not isinstance(c, int) or c < chunks - 1 else c + 2)
            product_rows(e, pO, K["W3"], g2, 2 * DB).then_inc(s_z, 1)

        @block.tensor
        def _(e):
            pe_x(e, 0)
            pe_skip(e, 0)
            pe_x2(e, 0)

            def turn(c, front, back):
                if front:
                    pe_x(e, c + 1)
                e.wait_ge(s_x2Tc, c + 1)
                pe_group(e, c, 1, 0)
                pe_group(e, c, 1, 1)
                if back:
                    e.wait_ge(s_x3, c)
                    transposes(e, K, pF, x3, DB).then_inc(s_x3T, 1)
                if front:
                    pe_skip(e, c + 1)
                for g in range(2, G1):
                    pe_group(e, c, 1, g)
                e.wait_ge(s_ev, ring_at(c, 1, G1) + RING)
                if back:
                    e.wait_ge(s_za, c)
                product_rows(e, pO, K["W_out"], hL, DB).then_inc(s_o, 1)
                if back:
                    pe_back2(e, c - 1)
                if front:
                    pe_x2(e, c + 1)
            turns(e, turn, "tensor")
            e.wait_ge(s_x3, chunks)
            transposes(e, K, pF, x3, DB).then_inc(s_x3T, 1)
            pe_back2(e, chunks - 1)

        @block.scalar
        def _(e):
            e.sem_inc(s_ev, RING)

            def evac(c, part, g):
                _, _, _, m, bias, out, relu = (back1 if part == 1 else back2)[g]
                e.wait_ge(s_mm, ring_at(c, part, g) + 1)
                e.activation(out[:, m, :], ring[:, g % RING, 0:C], ACT.Relu if relu else ACT.Identity,
                             bias=bias[:, m:m + 1]).then_inc(s_ev, 1)

            def x_copy(c):
                e.wait_ge(s_xT, c + 1)
                e.activation(xT[:, :, :], pG[:, :, 0:C], ACT.Copy).then_inc(s_xTc, 1)

            def gelu(c):
                e.wait_ge(s_u, c + 1)
                e.activation(v[:, :, :], u[:, :, :], ACT.Gelu).then_inc(s_g, 1)

            def x2_copy(c):
                e.wait_ge(s_x2T, c + 1)
                e.activation(x2T[:, :, :], pF[:, :, 0:C], ACT.Copy).then_inc(s_x2Tc, 1)

            def x3_copy(c):
                e.wait_ge(s_x3T, c + 1)
                e.activation(x3T[:, :, :], pF[:, :, 0:C], ACT.Copy).then_inc(s_x3Tc, 1)

            def x3_keep(c):
                if not isinstance(c, int) or c > 0:
                    e.wait_ge(s_zb, c)
                e.activation(xres[:, :, :], x3[:, :, :], ACT.Copy).then_inc(s_xres, 1)

            def relu_out(c):
                e.wait_ge(s_za, c + 2)
                e.activation(z[:, :, :], z[:, :, :], ACT.Relu).then_inc(s_zr, 1)

            x_copy(0)
            gelu(0)
            x2_copy(0)

            def turn(c, front, back):
                if front:
                    x_copy(c + 1)
                for g in range(G1):
                    evac(c, 1, g)
                    if back and g == 1:
                        x3_copy(c - 1)
                    if front and g == 3:
                        gelu(c + 1)
                    if back and g == 5:
                        x3_keep(c - 1)
                if back:
                    for g in range(G2):
                        evac(c - 1, 2, g)
                    relu_out(c - 1)
                if front:
                    x2_copy(c + 1)
            turns(e, turn, "scalar")
            x3_copy(chunks - 1)
            x3_keep(chunks - 1)
            for g in range(G2):
                evac(chunks - 1, 2, g)
            relu_out(chunks - 1)

        @block.vector
        def _(e):
            def front_0(c):
                e.drain()
                e.wait_ge(s_skip, c + 1)
                e.tensor_tensor(u[:, :, :], pGr[0:R, :, :], wide(K["bskip"][:, :]), ALU.add).then_inc(s_u, 1)
                e.wait_ge(s_g, c + 1)
                ln_stats(e, LF, 4 * c + 1, v)
                wait(e, s_xb0, c + 1)
                ln_affine(e, LF, 4 * c + 1, v, K["gamma0"], xb, u).then_inc(s_t0, 1)
                e.wait_ge(s_t0, c + 1)
                ln_vector(e, K, LF, 4 * c + 2, u, x1).then_inc(s_x1, 1)

            def front_1(c):
                e.wait_ge(s_x1, c + 1)
                e.tensor_tensor(v[:, :, :], x1[:, :, :], wide(K["bias1"][:, :]), ALU.add).then_inc(s_y, 1)
                e.wait_ge(s_y, c + 1)
                ln_stats(e, LF, 4 * c + 3, v)
                wait(e, s_xb1, c + 1)
                ln_affine(e, LF, 4 * c + 3, v, K["gamma1"], xb, u).then_inc(s_t1, 1)
                e.wait_ge(s_t1, c + 1)
                ln_stats(e, LF, 4 * c + 4, u)
                wait(e, s_oa, c + 1)
                ln_scale(e, LF, 4 * c + 4, u, x2).then_inc(s_x2, 1)

            def back_1(c):
                e.drain()
                e.wait_ge(s_o, c + 1)
                e.tensor_tensor(t3[:, :, :], pO[0:R, :, :], x2[:, :, :], ALU.add).then_inc(s_oa, 1)
                wait(e, s_oa, c + 2)
                e.tensor_tensor(t3[:, :, :], t3[:, :, :], wide(K["b_out"][:, :]), ALU.add).then_inc(s_ob, 1)
                e.wait_ge(s_ob, c + 1)
                ln_stats(e, LB, c + 1, t3)
                if not isinstance(c, int) or c > 0:
                    wait(e, s_xres, c)
                ln_scale(e, LB, c + 1, t3, x3).then_inc(s_x3, 1)

            def back_2(c):
                e.drain()
                e.wait_ge(s_z, c + 1)
                e.tensor_tensor(z[:, :, :], pO[0:R, :, :], wide(K["b3"][:, :]), ALU.add).then_inc(s_za, 1)
                e.wait_ge(s_zr, c + 1)
                wait(e, s_xres, c + 1)
                e.tensor_tensor(t3[:, :, :], z[:, :, :], xres[:, :, :], ALU.add).then_inc(s_zb, 1)
                e.wait_ge(s_zb, c + 1)
                ln_stats(e, LO, c + 1, t3)
                wait(e, s_st, 16 * c + 1)
                ln_scale(e, LO, c + 1, t3, o).then_inc(s_out, 1)

            e.sem_inc(s_oa, 1)
            e.sem_inc(s_za, 1)
            front_0(0)
            front_1(0)

            def turn(c, front, back):
                if front:
                    front_0(c + 1)
                back_1(c)
                if front:
                    front_1(c + 1)
                if back:
                    back_2(c - 1)
            turns(e, turn, "vector")
            back_2(chunks - 1)

        @block.gpsimd
        def _(e):
            e.sem_inc(s_st, 1)

            def front_0(c):
                e.drain()
                e.wait_ge(s_x, 16 * c + 16)
                e.tensor_tensor(xb[:, :, :], xr[:, :, :], wide(K["beta0"][:, :]), ALU.add).then_inc(s_xb0, 1)
                ln_pool(e, K, LF, 4 * c + 1)
                ln_pool(e, K, LF, 4 * c + 2)

            def front_1(c):
                e.wait_ge(s_x1, c + 1)
                e.tensor_tensor(xb[:, :, :], x1[:, :, :], wide(K["beta1"][:, :]), ALU.add).then_inc(s_xb1, 1)
                ln_pool(e, K, LF, 4 * c + 3)
                ln_pool(e, K, LF, 4 * c + 4)

            front_0(0)
            front_1(0)

            def turn(c, front, back):
                if front:
                    front_0(c + 1)
                ln_pool(e, K, LB, c + 1)
                if front:
                    front_1(c + 1)
                if back:
                    ln_pool(e, K, LO, c)
            turns(e, turn, "gpsimd")
            ln_pool(e, K, LO, chunks)



TILES = 40
U = 8
FAR = 1 << 17


def column_loop(e, K, body):
    with e.Fori(0, TILES // U) as i:
        body(i)


def rank_edges(nc, K, A, name, key, table):
    E = key.shape[0]
    with ExitStack() as ctx:
        sb, ps, sem = scopes(nc, ctx, name)
        keyI, keyF = sb("keyI", [R, E], I32), sb("keyF", [R, E])
        count, before = sb("count", [R, 2 * E]), sb("before", [R, 2 * E], BF16)
        less = sb("less", [R, E], BF16)
        srcC, dstC, keyC = sb("srcC", [R, TILES], I32), sb("dstC", [R, TILES], I32), sb("keyC", [R, TILES])
        rank, rankU = sb("rank", [R, TILES]), sb("rankU", [R, TILES], U32)
        pay = sb("pay", [R, TILES, 4], I32)
        idx8, pay8 = sb("idx8", [R, U], U32), sb("pay8", [R, U, 4], I32)
        s_ld, s_count, s_pos, s_rank, s_c8, s_sc = (sem("s_ld"), sem("s_count"), sem("s_pos"),
                                                    sem("s_rank"), sem("s_c8"), sem("s_sc"))
        block = ctx.enter_context(nc.Block())

        @block.sync
        def _(e):
            e.dma_start(keyI[:], key.unsqueeze(0).broadcast_to([R, E])).then_inc(s_ld, 16)
            for c, a in ((srcC, A["src"]), (dstC, A["dst"])):
                e.dma_start(c[:], a.rearrange("(t p) -> p t", p=R), allow_slow_non_contiguous=True)\
                    .then_inc(s_ld, 16)

        @block.vector
        def _(e):
            e.wait_ge(s_ld, 48)
            e.tensor_copy(keyF[:], keyI[:])
            e.tensor_copy(keyC[:], (srcC if key is A["src"] else dstC)[:])
            e.wait_ge(s_pos, 1)
            e.tensor_copy(pay[:, :, 0], srcC[:])
            e.tensor_copy(pay[:, :, 1], dstC[:])
            e.wait_ge(s_count, 1)
            e.tensor_scalar(before[:], count[:], float(E), 0.5, ALU.is_lt, ALU.mult)
            e.drain()
            with e.Fori(0, TILES) as t:
                e.scalar_tensor_tensor(out=less[:], in0=keyF[:], scalar=keyC[:, bass.ds(t, 1)],
                                       in1=before[:, bass.ds(t * (-R) + E, E)], op0=ALU.subtract,
                                       op1=ALU.is_lt, accum_out=rank[:, bass.ds(t, 1)])
                e.drain()
            e.tensor_copy(rankU[:], rank[:]).then_inc(s_rank, 1)

        @block.gpsimd
        def _(e):
            e.memset(pay[:], 0)
            e.drain()
            e.iota(pay[:, :, 2], pattern=[[R, TILES]], base=0, channel_multiplier=1).then_inc(s_pos, 1)
            e.iota(count[:], pattern=[[1, 2 * E]], base=0, channel_multiplier=-1,
                   allow_small_or_imprecise_dtypes=True).then_inc(s_count, 1)
            e.wait_ge(s_rank, 1)

            def body(i):
                e.tensor_copy(idx8[:], rankU[:, bass.ds(i * U, U)])
                e.tensor_copy(pay8[:], pay[:, bass.ds(i * U, U), :]).then_inc(s_c8, 1)
                wait(e, s_c8, i + 1)
                for k in range(U):
                    e.indirect_dma_start(table, bass.IndirectOffsetOnAxis(ap=idx8[:, k:k + 1], axis=0),
                                         pay8[:, k, :], None).then_inc(s_sc, 16)
                wait(e, s_sc, i * (16 * U) + 16 * U)
            column_loop(e, K, body)


def load_sorted(nc, K, A, S):
    with ExitStack() as ctx:
        sb, ps, sem = scopes(nc, ctx, "sorted")
        rows = [sb(f"rows{i}", [R, TILES, 4], I32) for i in range(2)]
        keyT = [sb(f"keyT{i}", [TILES, R]) for i in range(2)]
        pk = ps("pk", [P, 2, 512])
        zero = sb("zero", [R, 4 * K["N"] // R])
        s_ld, s_col, s_T, s_Tc, s_st, s_z, s_ord = (sem("s_ld"), sem("s_col"), sem("s_T"), sem("s_Tc"),
                                                    sem("s_st"), sem("s_z"), sem("s_ord"))
        block = ctx.enter_context(nc.Block())

        @block.sync
        def _(e):
            for i in range(2):
                e.dma_start(rows[i][:], S["edges"][i].rearrange("(t p) w -> p t w", p=R)).then_inc(s_ld, 16)
            e.wait_ge(s_z, 1)
            e.dma_start(S["nodes"].rearrange("(p a) w -> p (a w)", p=R), zero[:]).then_inc(s_st, 16)
            e.wait_ge(s_Tc, 1)
            for i in range(2):
                e.dma_start(S["key"][i], keyT[i][:]).then_inc(s_st, 16)
            e.wait_ge(s_st, 48)

        @block.vector
        def _(e):
            e.memset(zero[:], 0.0).then_inc(s_z, 1)
            e.wait_ge(s_ld, 32)
            for i in range(2):
                e.tensor_copy(K["srcF"][i][:], rows[i][:, :, 0])
                e.tensor_copy(K["dstF"][i][:], rows[i][:, :, 1])
                e.tensor_copy(K["srcU"][i][:], rows[i][:, :, 0])
                last = e.tensor_copy(K["dstU"][i][:], rows[i][:, :, 1])
            last = e.tensor_copy(K["ordU"][:], rows[0][:, :, 2])
            last.then_inc(s_col, 1)
            e.wait_ge(s_T, 1)
            for i in range(2):
                last = e.tensor_copy(keyT[i][:], pk[0:TILES, i, 0:R])
            last.then_inc(s_Tc, 1)

        @block.tensor
        def _(e):
            e.wait_ge(s_col, 1)
            e.transpose(pk[0:TILES, 0, 0:R], K["dstF"][0][:], K["ident"][0:R, 0:R])
            e.transpose(pk[0:TILES, 1, 0:R], K["srcF"][1][:], K["ident"][0:R, 0:R]).then_inc(s_T, 1)


def load_segments(nc, K, name, S, i, seg):
    E = K["E"]
    with ExitStack() as ctx:
        sb, ps, sem = scopes(nc, ctx, name)
        keyB = sb("keyB", [P, E])
        s_ld = sem("s_ld")
        block = ctx.enter_context(nc.Block())

        @block.sync
        def _(e):
            e.dma_start(keyB[:], S["key"][i].rearrange("t p -> (t p)").unsqueeze(0).broadcast_to([P, E]))\
                .then_inc(s_ld, 16)

        @block.vector
        def _(e):
            e.memset(seg[:, 0:1], 0.0)
            e.memset(seg[:, E:E + 1], 0.0)
            e.wait_ge(s_ld, 16)
            e.tensor_tensor(seg[:, 1:E], keyB[:, 1:E], keyB[:, 0:E - 1], ALU.is_equal)


def node_maps(nc, K, A, S):
    E, N = K["E"], K["N"]
    with ExitStack() as ctx:
        sb, ps, sem = scopes(nc, ctx, "maps")
        seg = [sb(f"seg{i}", [P, E + 1]) for i in range(2)]
        for i in range(2):
            load_segments(nc, K, f"maps_seg{i}", S, i, seg[i])
        cnt = sb("cnt", [P, E])
        one = sb("one", [P, 1])
        pos = sb("pos", [R, TILES])
        same = [sb(f"same{i}", [R, TILES]) for i in range(2)]
        pay = [sb(f"pay{i}", [R, TILES, 2]) for i in range(2)]
        at = [sb(f"at{i}", [R, TILES], U32) for i in range(2)]
        atF = sb("atF", [R, TILES])
        info = {}
        tmp = [sb(f"tmp{i}", [R, TILES]) for i in range(4)]
        half = sb("half", [R, TILES])
        idx8, pay8, got8 = sb("idx8", [R, U], U32), sb("pay8", [R, U, 2]), sb("got8", [R, U, 4])
        pc = ps("pc", [P, 4, TILES])
        s_one, s_cnt, s_c, s_cc, s_at, s_pos = (sem("s_one"), sem("s_cnt"), sem("s_c"), sem("s_cc"),
                                                sem("s_at"), sem("s_pos"))
        s_c8, s_sc, s_g8, s_ga, s_gb = sem("s_c8"), sem("s_sc"), sem("s_g8"), sem("s_ga"), sem("s_gb")
        s_all, s_pw, s_pd = sem("s_all"), sem("s_pw"), sem("s_pd")
        looks = [(K["srcU"][0], "src0"), (K["dstU"][0], "dst0"), (K["srcU"][1], "src1"), (K["dstU"][1], "dst1")]
        for _, n in looks:
            info[n] = sb(f"info_{n}", [R, TILES, 4])
        block = ctx.enter_context(nc.Block())

        @block.vector
        def _(e):
            e.memset(one[:], 1.0).then_inc(s_one, 1)
            e.memset(half[:], -0.5)
            e.drain()
            for i in range(2):
                if i:
                    e.wait_ge(s_c, 1)
                e.tensor_tensor_scan(cnt[:], seg[i][:, 0:E], one[:, 0:1].broadcast_to([P, E]), 0.0,
                                     ALU.mult, ALU.add).then_inc(s_cnt, 1)
            e.wait_ge(s_c, 2)
            e.wait_ge(s_pos, 1)
            for i in range(2):
                e.tensor_copy(same[i][:], pc[0:R, 2 * i + 1, :])
                e.tensor_copy(pay[i][:, :, 1], pc[0:R, 2 * i, :])
                e.tensor_scalar(pay[i][:, :, 0], pos[:], 1.0, None, ALU.add)
                e.drain()
                e.tensor_scalar(atF[:], (K["dstF"][0] if i == 0 else K["srcF"][1])[:], 2.0, float(i),
                                ALU.mult, ALU.add)
                e.drain()
                e.scalar_tensor_tensor(out=atF[:], in0=same[i][:], scalar=float(FAR), in1=atF[:],
                                       op0=ALU.mult, op1=ALU.add)
                e.drain()
                e.tensor_copy(at[i][:], atF[:])
                e.drain()
            e.tensor_copy(atF[:], atF[:]).then_inc(s_at, 1)
            e.wait_ge(s_all, 1)

            def map1(n, out):
                a, b = info[n][:, :, 0], info[n][:, :, 2]
                e.tensor_tensor(tmp[0][:], a, b, ALU.subtract)
                e.tensor_scalar(tmp[1][:], a, 0.0, None, ALU.is_gt)
                e.drain()
                e.scalar_tensor_tensor(out=tmp[2][:], in0=tmp[0][:], scalar=-float(E), in1=tmp[1][:],
                                       op0=ALU.add, op1=ALU.mult)
                e.drain()
                e.scalar_tensor_tensor(out=tmp[3][:], in0=tmp[2][:], scalar=float(E - 1), in1=b,
                                       op0=ALU.add, op1=ALU.add)
                e.drain()
                e.tensor_copy(out[:], tmp[3][:])
                e.drain()

            def map2(n, out):
                a, b = info[n][:, :, 0], info[n][:, :, 2]
                e.tensor_tensor(tmp[0][:], b, a, ALU.subtract)
                e.tensor_scalar(tmp[1][:], b, 0.0, None, ALU.is_gt)
                e.drain()
                e.scalar_tensor_tensor(out=tmp[2][:], in0=tmp[0][:], scalar=float(E), in1=tmp[1][:],
                                       op0=ALU.add, op1=ALU.mult)
                e.drain()
                e.scalar_tensor_tensor(out=tmp[3][:], in0=tmp[2][:], scalar=-1.0, in1=a,
                                       op0=ALU.add, op1=ALU.add)
                e.drain()
                e.tensor_copy(out[:], tmp[3][:])
                e.drain()

            map1("src0", K["m1s"])
            map2("src0", K["m2s"])
            map1("dst1", K["m1d"])
            map2("dst1", K["m2d"])
            map2("dst0", K["ownA"])
            map1("src1", K["ownB"])
            e.scalar_tensor_tensor(out=tmp[0][:], in0=same[0][:], scalar=float(FAR), in1=K["dstF"][0][:],
                                   op0=ALU.mult, op1=ALU.add)
            e.tensor_scalar(tmp[1][:], info["src1"][:, :, 0], 0.0, None, ALU.is_gt)
            e.drain()
            e.tensor_copy(K["outA"][:], tmp[0][:])
            e.tensor_tensor(tmp[2][:], tmp[1][:], same[1][:], ALU.max)
            e.drain()
            e.scalar_tensor_tensor(out=tmp[3][:], in0=tmp[2][:], scalar=float(FAR), in1=K["srcF"][1][:],
                                   op0=ALU.mult, op1=ALU.add)
            e.drain()
            e.tensor_copy(K["outB"][:], tmp[3][:])
            e.reciprocal(K["inv2"][:], info["src1"][:, :, 3])
            e.tensor_scalar(tmp[0][:], info["src0"][:, :, 1], 1.0, None, ALU.add)
            e.tensor_scalar(tmp[1][:], info["dst0"][:, :, 1], 1.0, None, ALU.add).then_inc(s_pw, 1)
            e.wait_ge(s_pd, 1)
            e.tensor_tensor(K["norm3"][:], tmp[2][:], tmp[3][:], ALU.mult)
            e.tensor_tensor(K["self3"][:], tmp[3][:], tmp[3][:], ALU.mult)

        @block.tensor
        def _(e):
            e.wait_ge(s_one, 1)
            for i in range(2):
                e.wait_ge(s_cnt, i + 1)
                for t in range(TILES):
                    e.matmul(pc[0:R, 2 * i, t:t + 1], cnt[0:1, t * R:(t + 1) * R], one[0:1, 0:1],
                             start=True, stop=True)
                    mm = e.matmul(pc[0:R, 2 * i + 1, t:t + 1], seg[i][0:1, t * R + 1:(t + 1) * R + 1],
                                  one[0:1, 0:1], start=True, stop=True)
                mm.then_inc(s_c, 1)

        @block.gpsimd
        def _(e):
            e.iota(pos[:], pattern=[[R, TILES]], base=0, channel_multiplier=1,
                   allow_small_or_imprecise_dtypes=True).then_inc(s_pos, 1)
            e.wait_ge(s_at, 1)
            for i in range(2):
                def body(j):
                    turn = j + i * (TILES // U)
                    e.tensor_copy(idx8[:], at[i][:, bass.ds(j * U, U)])
                    e.tensor_copy(pay8[:], pay[i][:, bass.ds(j * U, U), :]).then_inc(s_c8, 1)
                    wait(e, s_c8, turn + 1)
                    for k in range(U):
                        e.indirect_dma_start(S["nodes"], bass.IndirectOffsetOnAxis(ap=idx8[:, k:k + 1], axis=0),
                                             pay8[:, k, :], None, bounds_check=2 * N - 1,
                                             oob_is_err=False).then_inc(s_sc, 16)
                    wait(e, s_sc, turn * (16 * U) + 16 * U)
                column_loop(e, K, body)
            wide_nodes = S["nodes"].rearrange("(n two) w -> n (two w)", two=2)
            for q, (idx, n) in enumerate(looks):
                def body(j):
                    turn = j + q * (TILES // U)
                    e.tensor_copy(idx8[:], idx[:, bass.ds(j * U, U)]).then_inc(s_g8, 1)
                    wait(e, s_g8, turn + 1)
                    for k in range(U):
                        e.indirect_dma_start(got8[:, k, :], None, wide_nodes,
                                             bass.IndirectOffsetOnAxis(ap=idx8[:, k:k + 1], axis=0))\
                            .then_inc(s_ga, 16)
                    wait(e, s_ga, turn * (16 * U) + 16 * U)
                    e.tensor_copy(info[n][:, bass.ds(j * U, U), :], got8[:]).then_inc(s_gb, 1)
                    wait(e, s_gb, turn + 1)
                column_loop(e, K, body)
            e.memset(idx8[:], 0).then_inc(s_all, 1)
            e.wait_ge(s_pw, 1)
            e.tensor_tensor(tmp[2][:], tmp[0][:], half[:], ALU.pow)
            e.tensor_tensor(tmp[3][:], tmp[1][:], half[:], ALU.pow).then_inc(s_pd, 1)


def att_weights(nc, K, A):
    with ExitStack() as ctx:
        sb, ps, sem = scopes(nc, ctx, "att")
        We = sb("We", [64, D])
        att = {n: sb(n, [P, D]) for n in ("src", "dst", "edge")}
        prod = sb("prod", [P, DB, D])
        s_ld = sem("s_ld")
        block = ctx.enter_context(nc.Block())
        drams = {"src": A["L1_gnn_att_src"], "dst": A["L1_gnn_att_dst"], "edge": A["L1_gnn_att_edge"]}

        @block.sync
        def _(e):
            e.dma_start(We[:], A["L1_gnn_W_e"]).then_inc(s_ld, 16)
            for n in att:
                e.dma_start(att[n][:], drams[n].rearrange("h c -> (h c)").unsqueeze(0).broadcast_to([P, D]))\
                    .then_inc(s_ld, 16)

        @block.vector
        def _(e):
            e.wait_ge(s_ld, 64)
            for n, out in (("src", K["WAs"]), ("dst", K["WAd"])):
                e.drain()
                e.tensor_tensor(prod[:], K["W"][:, :, :], att[n][:].unsqueeze(1).broadcast_to([P, DB, D]), ALU.mult)
                e.drain()
                e.tensor_reduce(out[:], prod[:].rearrange("p k (h c) -> p k h c", h=8), AX.X, ALU.add)
            e.drain()
            e.tensor_tensor(prod[0:64, 0, :], We[:], att["edge"][0:64, :], ALU.mult)
            e.drain()
            e.tensor_reduce(K["WAe"][:], prod[0:64, 0, :].rearrange("p (h c) -> p h c", h=8), AX.X, ALU.add)

        @block.gpsimd
        def _(e):
            def keep(t, base, pattern, cm):
                e.drain()
                e.affine_select(out=t, in_=t, compare_op=ALU.is_ge, fill=0.0, base=base, pattern=pattern,
                                channel_multiplier=cm)
            for t, w in ((K["rep0"], 64), (K["rep1"], 32)):
                e.memset(t[:], 1.0)
                keep(t[:], 0, [[1, D]], -w)
                keep(t[:], w - 1, [[-1, D]], w)
            e.memset(K["sum0"][:], 1.0)
            keep(K["sum0"][:], 0, [[P, DB], [-64, 4]], 1)
            keep(K["sum0"][:], 63, [[-P, DB], [64, 4]], -1)



LANES = 2


def pipeline(e, base, pairs, load, rest, head=None):
    load(base)
    with e.Fori(base, base + pairs - 1) as i:
        if head:
            head(i)
        load(i + 1)
        rest(i)
    if head:
        head(base + pairs - 1)
    rest(base + pairs - 1)


def before(e, s, i):
    if not isinstance(i, int) or i > 0:
        wait(e, s, i)


def gather(e, table, idx, idxb, buf, n, s_idx, t, s_row):
    e.tensor_copy(idxb[:], idx[:, bass.ds(n * J, J)]).then_inc(s_idx, 1)
    wait(e, s_idx, t)
    for j in range(J):
        e.indirect_dma_start(buf[:, j, :], None, table, bass.IndirectOffsetOnAxis(ap=idxb[:, j:j + 1], axis=0))\
            .then_inc(s_row, 16)


def edge_scan(e, seg, n, src, agg, carry, blocks):
    for k in range(blocks):
        e.tensor_tensor_scan(agg[:, k, :], seg[:, bass.ds(n * C, C)], src[:, k, 0:C], carry[:, k:k + 1],
                             ALU.mult, ALU.add)
    e.drain()
    return e.tensor_copy(carry[:, 0:blocks], agg[:, :, C - 1])


def times_columns(e, rows, col, n, width):
    return e.tensor_tensor(rows[:], rows[:], col[:, bass.ds(n * J, J)].unsqueeze(2).broadcast_to([R, J, width]),
                           ALU.mult)


def value_chunk(S, n):
    return S["V"][bass.ds(n, 1)].rearrange("o p k c -> p (o k) c")


def lane_scopes(nc, ctx, name):
    sb, ps, sem = scopes(nc, ctx, name)
    lanes = range(LANES)
    return ((lambda n, s, d=F32: [sb(f"{n}{u}", s, d) for u in lanes]),
            (lambda n, s, d=F32: [ps(f"{n}{u}", s, d) for u in lanes]),
            (lambda n: [sem(f"{n}{u}") for u in lanes]), sb, sem)


def scores0(nc, K, A, S, alpha):
    with ExitStack() as ctx:
        sb, ps, sem, _, _ = lane_scopes(nc, ctx, "sc0")
        ms, ow = sb("ms", [R, J, D]), sb("ow", [R, J, D])
        idxm, idxo = sb("idxm", [R, J], U32), sb("idxo", [R, J], U32)
        msT, owT, qT, vT, prod = (sb(n, [P, DB, C]) for n in ("msT", "owT", "qT", "vT", "prod"))
        pA, pB = ps("pA", [P, DB, 512]), ps("pB", [P, DB, 512])
        s_im, s_io, s_rm, s_ro, s_T, s_Tc, s_q, s_qc, s_k, s_v, s_pr, s_vc, s_al, s_alc, s_st = (
            sem(n) for n in ("s_im", "s_io", "s_rm", "s_ro", "s_T", "s_Tc", "s_q", "s_qc", "s_k", "s_v",
                             "s_pr", "s_vc", "s_al", "s_alc", "s_st"))
        block = ctx.enter_context(nc.Block())
        pairs = K["E"] // C // LANES
        lanes = range(LANES)

        @block.sync
        def _(e):
            with e.Fori(0, pairs) as i:
                for u in lanes:
                    wait(e, s_vc[u], i + 1)
                    e.dma_start(value_chunk(S, i * LANES + u), vT[u][:]).then_inc(s_st[u], 16)
            for u in lanes:
                e.wait_ge(s_st[u], 16 * pairs + 1)

        @block.gpsimd
        def _(e):
            for u in lanes:
                e.sem_inc(s_st[u], 1)

            def load(i):
                for u in lanes:
                    before(e, s_T[u], i)
                    n = i * LANES + u
                    gather(e, A["x"], K["srcU"][0], idxm[u], ms[u], n, s_im[u], i + 1, s_rm[u])
                    gather(e, A["x"], K["dstU"][0], idxo[u], ow[u], n, s_io[u], i + 1, s_ro[u])
            pipeline(e, 0, pairs, load, lambda i: None)

        @block.tensor
        def _(e):
            for u in lanes:
                e.sem_inc(s_alc[u], 1)
            with e.Fori(0, pairs) as i:
                for u in lanes:
                    e.wait_ge(s_rm[u], i * (16 * J) + 16 * J)
                    e.wait_ge(s_ro[u], i * (16 * J) + 16 * J)
                    e.wait_ge(s_alc[u], i + 1)
                    transposes(e, K, pA[u], ms[u], DB)
                    transposes(e, K, pB[u], ow[u], DB).then_inc(s_T[u], 1)
                for u in lanes:
                    e.wait_ge(s_Tc[u], i + 1)
                    for m in range(DB):
                        mm = product_T(e, pA[u][:, m, 0:C], K["Wq"], m, owT[u], DB)
                    mm.then_inc(s_q[u], 1)
                    for m in range(DB):
                        mm = product_T(e, pB[u][:, m, 0:C], K["Wk"], m, msT[u], DB)
                    mm.then_inc(s_k[u], 1)
                for u in lanes:
                    e.wait_ge(s_qc[u], i + 1)
                    for m in range(DB):
                        mm = product_T(e, pA[u][:, m, 0:C], K["Wv"], m, msT[u], DB)
                    mm.then_inc(s_v[u], 1)
                for u in lanes:
                    e.wait_ge(s_pr[u], i + 1)
                    for m in range(DB):
                        mm = e.matmul(pB[u][0:4, 0, 0:C], K["sum0"][:, m, :], prod[u][:, m, :], start=m == 0,
                                      stop=m == DB - 1)
                    mm.then_inc(s_al[u], 1)
                    e.wait_ge(s_vc[u], i + 1)

        @block.scalar
        def _(e):
            with e.Fori(0, pairs) as i:
                for u in lanes:
                    e.wait_ge(s_T[u], i + 1)
                    e.activation(msT[u][:], pA[u][:, :, 0:C], ACT.Copy)
                    e.activation(owT[u][:], pB[u][:, :, 0:C], ACT.Copy).then_inc(s_Tc[u], 1)
                for u in lanes:
                    e.wait_ge(s_q[u], i + 1)
                    for m in range(DB):
                        a = e.activation(qT[u][:, m, :], pA[u][:, m, 0:C], ACT.Identity, bias=K["bq"][:, m:m + 1])
                    a.then_inc(s_qc[u], 1)
                for u in lanes:
                    e.wait_ge(s_v[u], i + 1)
                    e.wait_ge(s_st[u], i * 16 + 1)
                    for m in range(DB):
                        a = e.activation(vT[u][:, m, :], pA[u][:, m, 0:C], ACT.Identity, bias=K["bv"][:, m:m + 1])
                    a.then_inc(s_vc[u], 1)

        @block.vector
        def _(e):
            with e.Fori(0, pairs) as i:
                for u in lanes:
                    wait(e, s_qc[u], i + 1)
                    e.wait_ge(s_k[u], i + 1)
                    for m in range(DB):
                        v = e.scalar_tensor_tensor(out=prod[u][:, m, :], in0=pB[u][:, m, 0:C],
                                                   scalar=K["bk"][:, m:m + 1], in1=qT[u][:, m, :],
                                                   op0=ALU.add, op1=ALU.mult)
                    v.then_inc(s_pr[u], 1)
                for u in lanes:
                    wait(e, s_al[u], i + 1)
                    e.tensor_scalar(alpha[0:4, bass.ds((i * LANES + u) * C, C)], pB[u][0:4, 0, 0:C], 0.125, None,
                                    ALU.mult).then_inc(s_alc[u], 1)


def scores1(nc, K, A, S, alpha, adst):
    with ExitStack() as ctx:
        sb, ps, sem, _, _ = lane_scopes(nc, ctx, "sc1")
        ms, ow, ea = sb("ms", [R, J, D]), sb("ow", [R, J, D]), sb("ea", [R, J, 64])
        idxm, idxe = sb("idxm", [R, J], U32), sb("idxe", [R, J], U32)
        msT, owT, vT = (sb(n, [P, DB, C]) for n in ("msT", "owT", "vT"))
        eaT = sb("eaT", [64, C])
        pA, pB = ps("pA", [P, DB, 512]), ps("pB", [P, DB, 512])
        s_im, s_ie, s_rm, s_re, s_lin, s_T, s_Tc, s_To, s_Toc, s_al, s_v, s_vc, s_alc, s_st = (
            sem(n) for n in ("s_im", "s_ie", "s_rm", "s_re", "s_lin", "s_T", "s_Tc", "s_To", "s_Toc", "s_al",
                             "s_v", "s_vc", "s_alc", "s_st"))
        block = ctx.enter_context(nc.Block())
        pairs = K["E"] // C // LANES
        lanes = range(LANES)

        @block.sync
        def _(e):
            def load(i):
                for u in lanes:
                    before(e, s_To[u], i)
                    e.dma_start(ow[u][:], rows_of(S["X1"], i * LANES + u)).then_inc(s_lin[u], 16)

            def store(i):
                for u in lanes:
                    wait(e, s_vc[u], i + 1)
                    e.dma_start(value_chunk(S, i * LANES + u), vT[u][:]).then_inc(s_st[u], 16)
            pipeline(e, 0, pairs, load, store)
            for u in lanes:
                e.wait_ge(s_st[u], 16 * pairs + 1)

        @block.gpsimd
        def _(e):
            for u in lanes:
                e.sem_inc(s_st[u], 1)

            def load(i):
                for u in lanes:
                    before(e, s_T[u], i)
                    n = i * LANES + u
                    gather(e, S["X1"], K["m1s"], idxm[u], ms[u], n, s_im[u], i + 1, s_rm[u])
                    gather(e, A["edge_attr_64"], K["ordU"], idxe[u], ea[u], n, s_ie[u], i + 1, s_re[u])
            pipeline(e, 0, pairs, load, lambda i: None)

        @block.tensor
        def _(e):
            for u in lanes:
                e.sem_inc(s_alc[u], 1)
            with e.Fori(0, pairs) as i:
                for u in lanes:
                    e.wait_ge(s_rm[u], i * (16 * J) + 16 * J)
                    e.wait_ge(s_re[u], i * (16 * J) + 16 * J)
                    e.wait_ge(s_alc[u], i + 1)
                    transposes(e, K, pA[u], ms[u], DB)
                    transposes(e, K, pB[u], ea[u], 1, 64).then_inc(s_T[u], 1)
                for u in lanes:
                    e.wait_ge(s_lin[u], i * 16 + 16)
                    e.wait_ge(s_Tc[u], i + 1)
                    transposes(e, K, pB[u], ow[u], DB).then_inc(s_To[u], 1)
                    for m in range(DB):
                        mm = product_T(e, pA[u][:, m, 0:C], K["W"], m, msT[u], DB)
                    mm.then_inc(s_v[u], 1)
                for u in lanes:
                    e.wait_ge(s_Toc[u], i + 1)
                    for k in range(DB):
                        e.matmul(pB[u][0:8, 0, 0:C], K["WAs"][:, k, :], msT[u][:, k, :], start=k == 0, stop=False)
                    e.matmul(pB[u][0:8, 0, 0:C], K["WAe"][:, :], eaT[u][:, :], start=False, stop=True)
                    for k in range(DB):
                        mm = e.matmul(pB[u][0:8, 1, 0:C], K["WAd"][:, k, :], owT[u][:, k, :], start=k == 0,
                                      stop=k == DB - 1)
                    mm.then_inc(s_al[u], 1)
                    e.wait_ge(s_vc[u], i + 1)

        @block.scalar
        def _(e):
            with e.Fori(0, pairs) as i:
                for u in lanes:
                    e.wait_ge(s_T[u], i + 1)
                    e.activation(msT[u][:], pA[u][:, :, 0:C], ACT.Copy)
                    e.activation(eaT[u][:], pB[u][0:64, 0, 0:C], ACT.Copy).then_inc(s_Tc[u], 1)
                for u in lanes:
                    e.wait_ge(s_To[u], i + 1)
                    e.activation(owT[u][:], pB[u][:, :, 0:C], ACT.Copy).then_inc(s_Toc[u], 1)
                for u in lanes:
                    e.wait_ge(s_v[u], i + 1)
                    e.wait_ge(s_st[u], i * 16 + 1)
                    e.activation(vT[u][:], pA[u][:, :, 0:C], ACT.Copy).then_inc(s_vc[u], 1)

        @block.vector
        def _(e):
            with e.Fori(0, pairs) as i:
                for u in lanes:
                    wait(e, s_al[u], i + 1)
                    here = bass.ds((i * LANES + u) * C, C)
                    e.tensor_copy(alpha[0:8, here], pB[u][0:8, 0, 0:C])
                    e.tensor_copy(adst[0:8, here], pB[u][0:8, 1, 0:C]).then_inc(s_alc[u], 1)


def softmax(nc, K, name, H, seg, alpha, adst):
    E = K["E"]
    with ExitStack() as ctx:
        sb, ps, sem = scopes(nc, ctx, name)
        far, m = sb("far", [8, E + 1]), sb("m", [8, E])
        s_sub, s_exp = sem("s_sub"), sem("s_exp")
        block = ctx.enter_context(nc.Block())
        al, fr, mm, sg = alpha[0:H, :], far[0:H, :], m[0:H, :], seg[0:H, :]

        def last_of_segment(e):
            e.tensor_tensor_scan(mm[:, ::-1], fr[:, E:0:-1], mm[:, ::-1], 0.0 - BIG, ALU.add, ALU.max)

        @block.vector
        def _(e):
            e.tensor_scalar(fr, sg, 1.0, BIG, ALU.subtract, ALU.mult)
            if adst is not None:
                ad = adst[0:H, :]
                e.tensor_tensor(mm, sg[:, 1:E + 1], ad, ALU.mult)
                e.drain()
                e.tensor_tensor(mm, ad, mm, ALU.subtract)
                e.drain()
                e.tensor_tensor_scan(ad[:, ::-1], sg[:, E:0:-1], mm[:, ::-1], 0.0, ALU.mult, ALU.add)
                e.drain()
                e.tensor_tensor(al, al, ad, ALU.add)
                e.drain()
                e.scalar_tensor_tensor(out=al, in0=al, scalar=0.2, in1=al, op0=ALU.mult, op1=ALU.max)
            e.drain()
            e.tensor_tensor_scan(mm, fr[:, 0:E], al, 0.0 - BIG, ALU.add, ALU.max)
            e.drain()
            last_of_segment(e)
            e.drain()
            e.tensor_tensor(al, al, mm, ALU.subtract).then_inc(s_sub, 1)
            e.wait_ge(s_exp, 1)
            e.tensor_tensor_scan(mm, sg[:, 0:E], al, 0.0, ALU.mult, ALU.add)
            e.drain()
            last_of_segment(e)
            e.drain()
            e.tensor_scalar(mm, mm, 1e-16, None, ALU.add)
            e.drain()
            e.reciprocal(mm, mm)
            e.drain()
            e.tensor_tensor(al, al, mm, ALU.mult)

        @block.scalar
        def _(e):
            e.wait_ge(s_sub, 1)
            e.activation(al, al, ACT.Exp).then_inc(s_exp, 1)


def layer0_rows(nc, K, A, S, seg, attn):
    with ExitStack() as ctx:
        sb, ps, sem, sb1, sem1 = lane_scopes(nc, ctx, "l0")
        ow, xb, y, v, x1 = (sb(n, [R, J, D]) for n in ("ow", "xb", "y", "v", "x1"))
        idxb = sb("idxb", [R, J], U32)
        owT, vT, agg = (sb(n, [P, DB, C]) for n in ("owT", "vT", "agg"))
        carry = sb1("carry", [P, DB])
        pT, pE = ps("pT", [P, DB, 512]), ps("pE", [P, DB, 512])
        pR = [p[:, :, :].rearrange("p a (b d) -> p (a b) d", d=D) for p in pE]
        L = [ln_buffers(lambda n, s, u=u: sb1(f"{n}{u}", s), lambda n, u=u: sem1(f"{n}{u}"), "l0")
             for u in range(LANES)]
        s_idx, s_row, s_lin, s_T, s_Tc, s_ex, s_ag, s_r, s_u, s_g, s_xb, s_t, s_x1, s_st = (
            sem(n) for n in ("s_idx", "s_row", "s_lin", "s_T", "s_Tc", "s_ex", "s_ag", "s_r", "s_u",
                             "s_g", "s_xb", "s_t", "s_x1", "s_st"))
        block = ctx.enter_context(nc.Block())
        pairs = K["E"] // C // LANES
        lanes = range(LANES)
        parts = ((0, True), (pairs, False))

        @block.sync
        def _(e):
            def store(i):
                for u in lanes:
                    wait(e, s_x1[u], i + 1)
                    e.dma_start(rows_of(S["X1"], i * LANES + u), x1[u][:]).then_inc(s_st[u], 16)

            def load(i):
                for u in lanes:
                    before(e, s_ag[u], i)
                    e.dma_start(vT[u][:], value_chunk(S, i * LANES + u)).then_inc(s_lin[u], 16)
            for base, msg in parts:
                pipeline(e, base, pairs, load if msg else (lambda i: None), store)
            for u in lanes:
                e.wait_ge(s_st[u], 32 * pairs + 1)

        @block.gpsimd
        def _(e):
            for u in lanes:
                e.sem_inc(s_st[u], 1)
            for base, msg in parts:
                def load(i):
                    for u in lanes:
                        before(e, s_T[u], i)
                        before(e, s_xb[u], i)
                        gather(e, A["x"], K["dstU"][0] if msg else K["srcU"][1], idxb[u], ow[u],
                               (i - base) * LANES + u, s_idx[u], i + 1, s_row[u])

                def head(i):
                    for u in lanes:
                        wait(e, s_row[u], i * (16 * J) + 16 * J)
                        e.tensor_tensor(xb[u][:], ow[u][:], wide(K["beta0"][:, :]), ALU.add).then_inc(s_xb[u], 1)

                def rest(i):
                    for half in (1, 2):
                        for u in lanes:
                            ln_pool(e, K, L[u], 2 * i + half)
                pipeline(e, base, pairs, load, rest, head)

        @block.tensor
        def _(e):
            for base, msg in parts:
                with e.Fori(base, base + pairs) as i:
                    for u in lanes:
                        wait(e, s_u[u], i + 1)
                        if msg:
                            for m in range(DB):
                                mm = e.matmul(pE[u][:, m, 0:C], K["rep0"][:, m * P:(m + 1) * P],
                                              attn[0:4, bass.ds((i * LANES + u) * C, C)], start=True, stop=True)
                            mm.then_inc(s_ex[u], 1)
                        e.wait_ge(s_row[u], i * (16 * J) + 16 * J)
                        transposes(e, K, pT[u], ow[u], DB).then_inc(s_T[u], 1)
                    for u in lanes:
                        if msg:
                            e.wait_ge(s_ag[u], i + 1)
                        e.wait_ge(s_Tc[u], i + 1)
                        product_rows(e, pR[u], K["Wskip"], owT[u], DB, agg[u] if msg else None, K["ident"])\
                            .then_inc(s_r[u], 1)

        @block.scalar
        def _(e):
            with e.Fori(0, 2 * pairs) as i:
                for u in lanes:
                    e.wait_ge(s_T[u], i + 1)
                    e.activation(owT[u][:], pT[u][:, :, 0:C], ACT.Copy).then_inc(s_Tc[u], 1)
                for u in lanes:
                    e.wait_ge(s_u[u], i + 2)
                    e.activation(v[u][:], y[u][:], ACT.Gelu).then_inc(s_g[u], 1)

        @block.vector
        def _(e):
            e.memset(carry[:], 0.0)
            for u in lanes:
                e.sem_inc(s_u[u], 1)
            for base, msg in parts:
                with e.Fori(base, base + pairs) as i:
                    e.drain()
                    if msg:
                        for u in lanes:
                            wait(e, s_ex[u], i + 1)
                            e.wait_ge(s_lin[u], i * 16 + 16)
                            e.tensor_tensor(vT[u][:], vT[u][:], pE[u][:, :, 0:C], ALU.mult)
                            e.drain()
                            edge_scan(e, seg, i * LANES + u, vT[u], agg[u], carry, DB).then_inc(s_ag[u], 1)
                            e.drain()
                    for u in lanes:
                        e.wait_ge(s_r[u], i + 1)
                        e.tensor_tensor(y[u][:], pR[u][0:R, :, :], wide(K["bskip"][:, :]), ALU.add)\
                            .then_inc(s_u[u], 1)
                    for u in lanes:
                        e.wait_ge(s_g[u], i + 1)
                        ln_stats(e, L[u], 2 * i + 1, v[u])
                    for u in lanes:
                        wait(e, s_xb[u], i + 1)
                        ln_affine(e, L[u], 2 * i + 1, v[u], K["gamma0"], xb[u], y[u]).then_inc(s_t[u], 1)
                    for u in lanes:
                        e.wait_ge(s_t[u], i + 1)
                        ln_stats(e, L[u], 2 * i + 2, y[u])
                    for u in lanes:
                        wait(e, s_st[u], i * 16 + 1)
                        ln_scale(e, L[u], 2 * i + 2, y[u], x1[u]).then_inc(s_x1[u], 1)


def layer1_rows(nc, K, A, S, seg, attn):
    with ExitStack() as ctx:
        sb, ps, sem, sb1, sem1 = lane_scopes(nc, ctx, "l1")
        x1, xb, y, v, x2, h = (sb(n, [R, J, D]) for n in ("x1", "xb", "y", "v", "x2", "h"))
        b_in = sb1("b_in", [R, D])
        x2T, vT, agg = (sb(n, [P, DB, C]) for n in ("x2T", "vT", "agg"))
        carry = sb1("carry", [P, DB])
        pT, pE = ps("pT", [P, DB, 512]), ps("pE", [P, DB, 512])
        pR = [p[:, :, :].rearrange("p a (b d) -> p (a b) d", d=D) for p in pE]
        L = [ln_buffers(lambda n, s, u=u: sb1(f"{n}{u}", s), lambda n, u=u: sem1(f"{n}{u}"), "l1")
             for u in range(LANES)]
        s_b = sem1("s_b")
        s_lin, s_v, s_ex, s_ag, s_r, s_y, s_xb, s_ya, s_t, s_x2, s_T, s_Tc, s_h, s_hc, s_st, s_sth = (
            sem(n) for n in ("s_lin", "s_v", "s_ex", "s_ag", "s_r", "s_y", "s_xb", "s_ya", "s_t", "s_x2",
                             "s_T", "s_Tc", "s_h", "s_hc", "s_st", "s_sth"))
        block = ctx.enter_context(nc.Block())
        pairs = K["E"] // C // LANES
        lanes = range(LANES)
        parts = ((0, True), (pairs, False))

        @block.sync
        def _(e):
            e.dma_start(b_in[:], A["L2_gnn_b_in"].unsqueeze(0).broadcast_to([R, D])).then_inc(s_b, 16)
            for base, msg in parts:
                def load(i):
                    for u in lanes:
                        before(e, s_xb[u], i)
                        e.dma_start(x1[u][:], rows_of(S["X1"], i * LANES + u)).then_inc(s_lin[u], 16)
                        if msg:
                            before(e, s_ag[u], i)
                            e.dma_start(vT[u][:], value_chunk(S, i * LANES + u)).then_inc(s_v[u], 16)

                def store(i):
                    for u in lanes:
                        wait(e, s_x2[u], i + 1)
                        e.dma_start(rows_of(S["X2"], i * LANES + u), x2[u][:]).then_inc(s_st[u], 16)
                    for u in lanes:
                        wait(e, s_hc[u], i + 2)
                        e.dma_start(rows_of(S["H"][0], i * LANES + u), h[u][:]).then_inc(s_sth[u], 16)
                pipeline(e, base, pairs, load, store)
            for u in lanes:
                e.wait_ge(s_st[u], 32 * pairs + 1)
                e.wait_ge(s_sth[u], 32 * pairs + 1)

        @block.gpsimd
        def _(e):
            for u in lanes:
                e.sem_inc(s_st[u], 1)
                e.sem_inc(s_sth[u], 1)
            with e.Fori(0, 2 * pairs) as i:
                e.drain()
                for u in lanes:
                    wait(e, s_lin[u], i * 16 + 16)
                    e.tensor_tensor(y[u][:], x1[u][:], wide(K["bias1"][:, :]), ALU.add).then_inc(s_y[u], 1)
                for u in lanes:
                    e.tensor_tensor(xb[u][:], x1[u][:], wide(K["beta1"][:, :]), ALU.add).then_inc(s_xb[u], 1)
                for half in (1, 2):
                    for u in lanes:
                        ln_pool(e, K, L[u], 2 * i + half)

        @block.tensor
        def _(e):
            for base, msg in parts:
                with e.Fori(base, base + pairs) as i:
                    for u in lanes:
                        wait(e, s_hc[u], i + 1)
                        if msg:
                            for m in range(DB):
                                mm = e.matmul(pE[u][:, m, 0:C], K["rep1"][:, m * P:(m + 1) * P],
                                              attn[0:8, bass.ds((i * LANES + u) * C, C)], start=True, stop=True)
                            mm.then_inc(s_ex[u], 1)
                    if msg:
                        for u in lanes:
                            wait(e, s_ag[u], i + 1)
                            agg_rows(e, pR[u], agg[u], K["ident"]).then_inc(s_r[u], 1)
                    for u in lanes:
                        e.wait_ge(s_x2[u], i + 1)
                        transposes(e, K, pT[u], x2[u], DB).then_inc(s_T[u], 1)
                    for u in lanes:
                        e.wait_ge(s_Tc[u], i + 1)
                        product_rows(e, pR[u], K["W_in"], x2T[u], DB).then_inc(s_h[u], 1)

        @block.scalar
        def _(e):
            with e.Fori(0, 2 * pairs) as i:
                for u in lanes:
                    e.wait_ge(s_T[u], i + 1)
                    e.activation(x2T[u][:], pT[u][:, :, 0:C], ACT.Copy).then_inc(s_Tc[u], 1)

        @block.vector
        def _(e):
            e.memset(carry[:], 0.0)
            for u in lanes:
                e.sem_inc(s_hc[u], 1)
            e.wait_ge(s_b, 16)
            for base, msg in parts:
                with e.Fori(base, base + pairs) as i:
                    e.drain()
                    if msg:
                        for u in lanes:
                            wait(e, s_ex[u], i + 1)
                            e.wait_ge(s_v[u], i * 16 + 16)
                            e.tensor_tensor(vT[u][:], vT[u][:], pE[u][:, :, 0:C], ALU.mult)
                            e.drain()
                            edge_scan(e, seg, i * LANES + u, vT[u], agg[u], carry, DB).then_inc(s_ag[u], 1)
                            e.drain()
                        for u in lanes:
                            wait(e, s_r[u], i + 1)
                            e.wait_ge(s_y[u], i + 1)
                            e.tensor_tensor(y[u][:], y[u][:], pR[u][0:R, :, :], ALU.add)
                        e.drain()
                    for u in lanes:
                        wait(e, s_y[u], i + 1)
                        ln_stats(e, L[u], 2 * i + 1, y[u])
                    for u in lanes:
                        wait(e, s_xb[u], i + 1)
                        ln_affine(e, L[u], 2 * i + 1, y[u], K["gamma1"], xb[u], v[u]).then_inc(s_t[u], 1)
                    for u in lanes:
                        e.wait_ge(s_t[u], i + 1)
                        ln_stats(e, L[u], 2 * i + 2, v[u])
                    for u in lanes:
                        wait(e, s_st[u], i * 16 + 1)
                        ln_scale(e, L[u], 2 * i + 2, v[u], x2[u]).then_inc(s_x2[u], 1)
                    for u in lanes:
                        wait(e, s_sth[u], i * 16 + 1)
                        e.wait_ge(s_h[u], i + 1)
                        e.tensor_tensor(h[u][:], pR[u][0:R, :, :], wide(b_in[:, :]), ALU.add).then_inc(s_hc[u], 1)


def layer2_rows(nc, K, A, S, seg, l):
    tail = l == 2
    with ExitStack() as ctx:
        sb, ps, sem, sb1, sem1 = lane_scopes(nc, ctx, f"l2{l}")
        ow, ms, h, x2, y, x3 = (sb(n, [R, J, D]) for n in ("ow", "ms", "h", "x2", "y", "x3"))
        bias = sb1("bias", [R, D])
        idxm, idxo = sb("idxm", [R, J], U32), sb("idxo", [R, J], U32)
        owT, agg, hT = (sb(n, [P, DB, C]) for n in ("owT", "agg", "hT"))
        carry = sb1("carry", [P, DB])
        pT, pM = ps("pT", [P, DB, 512]), ps("pM", [P, DB, 512])
        pR = [p[:, :, :].rearrange("p a (b d) -> p (a b) d", d=D) for p in pM]
        L = [ln_buffers(lambda n, s, u=u: sb1(f"{n}{u}", s), lambda n, u=u: sem1(f"{n}{u}"), "l2")
             for u in range(LANES)]
        s_b = sem1("s_b")
        s_im, s_io, s_own, s_ownG, s_x2, s_x2G, s_msg, s_w, s_T, s_M, s_Tc, s_ag, s_r = (
            sem(n) for n in ("s_im", "s_io", "s_own", "s_ownG", "s_x2", "s_x2G", "s_msg", "s_w", "s_T", "s_M",
                             "s_Tc", "s_ag", "s_r"))
        s_b1, s_h, s_hT, s_hTc, s_o, s_ob, s_xa, s_x3, s_st = (
            sem(n) for n in ("s_b1", "s_h", "s_hT", "s_hTc", "s_o", "s_ob", "s_xa", "s_x3", "s_st"))
        block = ctx.enter_context(nc.Block())
        pairs = K["E"] // C // LANES
        lanes = range(LANES)
        parts = ((0, False), (pairs, True))
        Wself, Wagg = K[f"Wself{l}"], K[f"Wagg{l}"]
        s_free = s_ob if tail else s_b1

        def there(e, i, gathered, s_line, s_gather):
            if gathered:
                wait(e, s_gather, (i - pairs) * (16 * J) + 16 * J)
            else:
                wait(e, s_line, i * 16 + 16)

        @block.sync
        def _(e):
            e.dma_start(bias[:], A["L2_gnn_b_hid"][l].unsqueeze(0).broadcast_to([R, D])).then_inc(s_b, 16)
            for base, msg in parts:
                def load(i):
                    for u in lanes:
                        n = i * LANES + u
                        if not (msg and l == 0):
                            before(e, s_T[u], i)
                            e.dma_start(ow[u][:], rows_of(S["H"][l], n)).then_inc(s_own[u], 16)
                        if tail and not msg:
                            before(e, s_xa[u], i)
                            e.dma_start(x2[u][:], rows_of(S["X2"], n)).then_inc(s_x2[u], 16)

                def store(i):
                    for u in lanes:
                        n = i * LANES + u
                        if tail:
                            wait(e, s_x3[u], i + 1)
                            e.dma_start(rows_of(S["X3"], n), x3[u][:]).then_inc(s_st[u], 16)
                        else:
                            wait(e, s_h[u], i + 1)
                            e.dma_start(rows_of(S["H"][l + 1], n), h[u][:]).then_inc(s_st[u], 16)
                pipeline(e, base, pairs, load, store)
            for u in lanes:
                e.wait_ge(s_st[u], 32 * pairs + 1)

        @block.gpsimd
        def _(e):
            for u in lanes:
                e.sem_inc(s_st[u], 1)
            for base, msg in parts:
                def load(i):
                    for u in lanes:
                        if not msg:
                            continue
                        n = (i - base) * LANES + u
                        before(e, s_M[u], i - base)
                        gather(e, S["H"][l], K["m1d"] if l == 0 else K["m2d"], idxm[u], ms[u], n, s_im[u],
                               i - base + 1, s_msg[u])
                        if l == 0:
                            before(e, s_T[u], i)
                            gather(e, S["H"][l], K["ownB"], idxo[u], ow[u], n, s_io[u], i - base + 1, s_ownG[u])
                        if tail:
                            before(e, s_xa[u], i)
                            gather(e, S["X2"], K["ownB"], idxo[u], x2[u], n, s_io[u], i - base + 1, s_x2G[u])

                def rest(i):
                    if tail:
                        for u in lanes:
                            ln_pool(e, K, L[u], i + 1)
                pipeline(e, base, pairs, load, rest)

        @block.tensor
        def _(e):
            for base, msg in parts:
                with e.Fori(base, base + pairs) as i:
                    for u in lanes:
                        there(e, i, msg and l == 0, s_own[u], s_ownG[u])
                        transposes(e, K, pT[u], ow[u], DB).then_inc(s_T[u], 1)
                    if msg:
                        for u in lanes:
                            wait(e, s_w[u], i - base + 1)
                            wait(e, s_free[u], i + 1)
                            transposes(e, K, pM[u], ms[u], DB).then_inc(s_M[u], 1)
                    for u in lanes:
                        if msg:
                            wait(e, s_ag[u], i - base + 1)
                        else:
                            wait(e, s_free[u], i + 1)
                        e.wait_ge(s_Tc[u], i + 1)
                        terms = [(owT[u], Wself)] + ([(agg[u], Wagg)] if msg else [])
                        for j in range(J):
                            for a, (xT, w) in enumerate(terms):
                                for k in range(DB):
                                    mm = e.matmul(pR[u][0:R, j, :], xT[:, k, j * R:(j + 1) * R], w[:, k, :],
                                                  start=a == 0 and k == 0,
                                                  stop=a == len(terms) - 1 and k == DB - 1)
                        mm.then_inc(s_r[u], 1)
                    if tail:
                        for u in lanes:
                            e.wait_ge(s_h[u], i + 1)
                            transposes(e, K, pT[u], h[u], DB).then_inc(s_hT[u], 1)
                        for u in lanes:
                            e.wait_ge(s_hTc[u], i + 1)
                            product_rows(e, pR[u], K["W_out"], hT[u], DB).then_inc(s_o[u], 1)

        @block.scalar
        def _(e):
            with e.Fori(0, 2 * pairs) as i:
                for u in lanes:
                    e.wait_ge(s_T[u], i + 1)
                    e.activation(owT[u][:], pT[u][:, :, 0:C], ACT.Copy).then_inc(s_Tc[u], 1)
                for u in lanes:
                    if not tail:
                        e.wait_ge(s_st[u], i * 16 + 1)
                    e.wait_ge(s_b1[u], i + 2)
                    e.activation(h[u][:], y[u][:], ACT.Relu).then_inc(s_h[u], 1)
                if tail:
                    for u in lanes:
                        e.wait_ge(s_hT[u], i + 1)
                        e.activation(hT[u][:], pT[u][:, :, 0:C], ACT.Copy).then_inc(s_hTc[u], 1)

        @block.vector
        def _(e):
            e.memset(carry[:], 0.0)
            for u in lanes:
                e.sem_inc(s_b1[u], 1)
                e.sem_inc(s_ob[u], 1)
            e.wait_ge(s_b, 16)
            for base, msg in parts:
                with e.Fori(base, base + pairs) as i:
                    e.drain()
                    if msg:
                        for u in lanes:
                            wait(e, s_msg[u], (i - base) * (16 * J) + 16 * J)
                            times_columns(e, ms[u], K["inv2"], (i - base) * LANES + u, D).then_inc(s_w[u], 1)
                        for u in lanes:
                            wait(e, s_M[u], i - base + 1)
                            edge_scan(e, seg, (i - base) * LANES + u, pM[u], agg[u], carry, DB)\
                                .then_inc(s_ag[u], 1)
                            e.drain()
                    for u in lanes:
                        wait(e, s_r[u], i + 1)
                        e.tensor_tensor(y[u][:], pR[u][0:R, :, :], wide(bias[:, :]), ALU.add).then_inc(s_b1[u], 1)
                    if tail:
                        for u in lanes:
                            wait(e, s_o[u], i + 1)
                            e.tensor_tensor(y[u][:], pR[u][0:R, :, :], wide(K["b_out"][:, :]), ALU.add)\
                                .then_inc(s_ob[u], 1)
                        e.drain()
                        for u in lanes:
                            there(e, i, msg, s_x2[u], s_x2G[u])
                            e.tensor_tensor(y[u][:], y[u][:], x2[u][:], ALU.add).then_inc(s_xa[u], 1)
                        for u in lanes:
                            wait(e, s_xa[u], i + 1)
                            ln_stats(e, L[u], i + 1, y[u])
                        for u in lanes:
                            wait(e, s_st[u], i * 16 + 1)
                            ln_scale(e, L[u], i + 1, y[u], x3[u]).then_inc(s_x3[u], 1)
                    else:
                        for u in lanes:
                            wait(e, s_h[u], i + 1)


def layer3_rows(nc, K, A, S, seg, l):
    with ExitStack() as ctx:
        sb, ps, sem, sb1, sem1 = lane_scopes(nc, ctx, f"l3{l}")
        w_in = [D, 2 * D, D][l]
        w_out = [2 * D, 2 * D, D][l]
        nb = w_in // P
        ow, ms = sb("ow", [R, J, w_in]), sb("ms", [R, J, w_in])
        y = sb("y", [R, J, w_out])
        z = sb("z", [R, J, D]) if l else None
        x3 = sb("x3", [R, J, D]) if l == 2 else None
        bias = sb1("bias", [R, w_out])
        idxm, idxo, idxr = (sb(n, [R, J], U32) for n in ("idxm", "idxo", "idxr"))
        agg, tT = sb("agg", [P, nb, C]), sb("tT", [P, nb, C])
        gT = tT
        carry = sb1("carry", [P, nb])
        pQ = ps("pQ", [P, 4, 512])
        pZ = [p[:, 2:4, :].rearrange("p a (b d) -> p (a b) d", d=D) for p in pQ]
        L = [ln_buffers(lambda n, s, u=u: sb1(f"{n}{u}", s), lambda n, u=u: sem1(f"{n}{u}"), "l3")
             for u in range(LANES)]
        s_b = sem1("s_b")
        s_im, s_io, s_ir, s_own, s_ownG, s_x3, s_x3G, s_msg, s_wo, s_wm, s_M, s_To, s_ag, s_tT = (
            sem(n) for n in ("s_im", "s_io", "s_ir", "s_own", "s_ownG", "s_x3", "s_x3G", "s_msg", "s_wo",
                             "s_wm", "s_M", "s_To", "s_ag", "s_tT"))
        s_r, s_b1, s_g, s_gT, s_gTc, s_z, s_zc, s_xa, s_st, s_sc, s_out = (
            sem(n) for n in ("s_r", "s_b1", "s_g", "s_gT", "s_gTc", "s_z", "s_zc", "s_xa", "s_st", "s_sc",
                             "s_out"))
        block = ctx.enter_context(nc.Block())
        pairs = K["E"] // C // LANES
        lanes = range(LANES)
        parts = ((0, True), (pairs, False))
        src = [S["X3"], S["G"], S["Z"]][l]
        vec = [A["L3_gnn_b1"], A["L3_gnn_b2"], A["L3_gnn_b3"]][l]
        G = 16 * J
        s_free = s_zc if l == 1 else s_b1

        def there(e, i, gathered, s_line, s_gather, skipped):
            if gathered:
                wait(e, s_gather, i * G + G)
            else:
                wait(e, s_line, (i - skipped) * 16 + 16)

        def own_there(e, i, u, msg):
            there(e, i, l == 0 and msg, s_own[u], s_ownG[u], pairs if l == 0 else 0)

        @block.sync
        def _(e):
            e.dma_start(bias[:], vec.unsqueeze(0).broadcast_to([R, w_out])).then_inc(s_b, 16)
            for base, msg in parts:
                def load(i):
                    for u in lanes:
                        n = i * LANES + u
                        if not (msg and l == 0):
                            if l == 2:
                                before(e, s_b1[u], i + 1)
                            else:
                                before(e, s_To[u], i)
                            e.dma_start(ow[u][:], rows_of(src, n)).then_inc(s_own[u], 16)
                        if l == 2 and not msg:
                            before(e, s_xa[u], i)
                            e.dma_start(x3[u][:], rows_of(S["X3"], n)).then_inc(s_x3[u], 16)

                def store(i):
                    for u in lanes:
                        n = i * LANES + u
                        if l == 0:
                            wait(e, s_g[u], i + 1)
                            e.dma_start(rows_of(S["G"], n), y[u][:]).then_inc(s_st[u], 16)
                        if l == 1:
                            wait(e, s_zc[u], i + 2)
                            e.dma_start(rows_of(S["Z"], n), z[u][:]).then_inc(s_st[u], 16)
                pipeline(e, base, pairs, load, store)
            for u in lanes:
                if l < 2:
                    e.wait_ge(s_st[u], 32 * pairs + 1)
                else:
                    e.wait_ge(s_sc[u], 2 * pairs * G)

        @block.gpsimd
        def _(e):
            for u in lanes:
                e.sem_inc(s_st[u], 1)
            for base, msg in parts:
                def load(i):
                    for u in lanes:
                        if not msg:
                            continue
                        n = i * LANES + u
                        before(e, s_M[u], i)
                        gather(e, src, K["m2s"] if l == 0 else K["m1s"], idxm[u], ms[u], n, s_im[u], i + 1,
                               s_msg[u])
                        if l == 0:
                            before(e, s_To[u], i)
                            gather(e, src, K["ownA"], idxo[u], ow[u], n, s_io[u], i + 1, s_ownG[u])
                        if l == 2:
                            before(e, s_xa[u], i)
                            gather(e, S["X3"], K["ownA"], idxo[u], x3[u], n, s_io[u], i + 1, s_x3G[u])

                def rest(i):
                    if l < 2:
                        return
                    for u in lanes:
                        col = K["outA"] if msg else K["outB"]
                        e.tensor_copy(idxr[u][:], col[:, bass.ds(((i - base) * LANES + u) * J, J)])\
                            .then_inc(s_ir[u], 1)
                        ln_pool(e, K, L[u], i + 1)
                    for u in lanes:
                        wait(e, s_ir[u], i + 1)
                        wait(e, s_out[u], i + 1)
                        for j in range(J):
                            e.indirect_dma_start(A["out"],
                                                 bass.IndirectOffsetOnAxis(ap=idxr[u][:, j:j + 1], axis=0),
                                                 z[u][:, j, :], None, bounds_check=K["N"] - 1, oob_is_err=False)\
                                .then_inc(s_sc[u], 16)
                    for u in lanes:
                        wait(e, s_sc[u], i * G + G)
                pipeline(e, base, pairs, load, rest)

        @block.tensor
        def _(e):
            for base, msg in parts:
                with e.Fori(base, base + pairs) as i:
                    if msg:
                        for u in lanes:
                            wait(e, s_free[u], i + 1)
                            wait(e, s_wm[u], i + 1)
                            transposes(e, K, pQ[u], ms[u], nb).then_inc(s_M[u], 1)
                    if l == 2:
                        if msg:
                            for u in lanes:
                                wait(e, s_ag[u], i + 1)
                                agg_rows(e, pZ[u], agg[u], K["ident"]).then_inc(s_r[u], 1)
                    else:
                        for u in lanes:
                            if msg:
                                wait(e, s_ag[u], i + 1)
                                wait(e, s_wo[u], i + 1)
                            else:
                                wait(e, s_free[u], i + 1)
                                own_there(e, i, u, msg)
                            transposes(e, K, pQ[u], ow[u], nb).then_inc(s_To[u], 1)
                        w = K["W1"] if l == 0 else K["W2"]
                        for u in lanes:
                            e.wait_ge(s_tT[u], i + 1)
                            for j in range(J):
                                for k in range(nb):
                                    mm = e.matmul(pQ[u][0:R, j, :], tT[u][:, k, j * R:(j + 1) * R], w[:, k, :],
                                                  start=k == 0, stop=k == nb - 1)
                            mm.then_inc(s_r[u], 1)
                    if l == 1:
                        for u in lanes:
                            e.wait_ge(s_g[u], i + 1)
                            transposes(e, K, pQ[u], y[u], 2 * DB).then_inc(s_gT[u], 1)
                        for u in lanes:
                            e.wait_ge(s_gTc[u], i + 1)
                            product_rows(e, pZ[u], K["W3"], gT[u], 2 * DB).then_inc(s_z[u], 1)

        @block.scalar
        def _(e):
            with e.Fori(0, 2 * pairs) as i:
                for u in lanes:
                    e.wait_ge(s_b1[u], i + 2)
                    e.activation(y[u][:], y[u][:], ACT.Relu).then_inc(s_g[u], 1)
                if l == 1:
                    for u in lanes:
                        e.wait_ge(s_gT[u], i + 1)
                        for b in range(2):
                            a = e.activation(gT[u][:, 2 * b:2 * b + 2, :], pQ[u][:, 2 * b:2 * b + 2, 0:C], ACT.Copy)
                        a.then_inc(s_gTc[u], 1)

        @block.vector
        def _(e):
            e.memset(carry[:], 0.0)
            for u in lanes:
                e.sem_inc(s_b1[u], 1)
                e.sem_inc(s_zc[u], 1)
            e.wait_ge(s_b, 16)
            for base, msg in parts:
                with e.Fori(base, base + pairs) as i:
                    e.drain()
                    if msg:
                        for u in lanes:
                            wait(e, s_msg[u], i * G + G)
                            times_columns(e, ms[u], K["norm3"], i * LANES + u, w_in).then_inc(s_wm[u], 1)
                            own_there(e, i, u, msg)
                            times_columns(e, ow[u], K["self3"], i * LANES + u, w_in).then_inc(s_wo[u], 1)
                        for u in lanes:
                            wait(e, s_M[u], i + 1)
                            edge_scan(e, seg, i * LANES + u, pQ[u], agg[u], carry, nb).then_inc(s_ag[u], 1)
                            e.drain()
                    if l < 2:
                        for u in lanes:
                            wait(e, s_To[u], i + 1)
                            if msg:
                                e.tensor_tensor(tT[u][:], pQ[u][:, 0:nb, 0:C], agg[u][:], ALU.add)\
                                    .then_inc(s_tT[u], 1)
                            else:
                                e.tensor_copy(tT[u][:], pQ[u][:, 0:nb, 0:C]).then_inc(s_tT[u], 1)
                        for u in lanes:
                            if l == 0:
                                wait(e, s_st[u], i * 16 + 1)
                            wait(e, s_r[u], i + 1)
                            e.tensor_tensor(y[u][:], pQ[u][0:R, :, :],
                                            bias[:, :].unsqueeze(1).broadcast_to([R, J, w_out]), ALU.add)\
                                .then_inc(s_b1[u], 1)
                        if l == 1:
                            for u in lanes:
                                wait(e, s_st[u], i * 16 + 1)
                                wait(e, s_z[u], i + 1)
                                e.tensor_copy(z[u][:], pZ[u][0:R, :, :]).then_inc(s_zc[u], 1)
                    else:
                        for u in lanes:
                            if msg:
                                wait(e, s_r[u], i + 1)
                                e.tensor_tensor(ow[u][:], ow[u][:], pZ[u][0:R, :, :], ALU.add)
                                e.drain()
                            else:
                                own_there(e, i, u, msg)
                            e.tensor_tensor(y[u][:], ow[u][:], wide(bias[:, :]), ALU.add).then_inc(s_b1[u], 1)
                        for u in lanes:
                            wait(e, s_g[u], i + 1)
                            there(e, i, msg, s_x3[u], s_x3G[u], pairs)
                            e.tensor_tensor(y[u][:], y[u][:], x3[u][:], ALU.add).then_inc(s_xa[u], 1)
                        for u in lanes:
                            wait(e, s_xa[u], i + 1)
                            ln_stats(e, L[u], i + 1, y[u])
                        for u in lanes:
                            ln_scale(e, L[u], i + 1, y[u], z[u]).then_inc(s_out[u], 1)


def build(nc, A):
    K = {}
    N, _ = A["x"].shape
    E = A["src"].shape[0]
    K["N"], K["E"] = N, E

    def scratch(name, shape, d=F32):
        return nc.dram_tensor(name, shape, d, kind="Internal").ap()
    S = dict(
        edges=[scratch(f"edges{i}", [E, 4], I32) for i in range(2)],
        key=[scratch(f"key{i}", [TILES, R]) for i in range(2)],
        nodes=scratch("nodes", [2 * N, 2]),
        V=scratch("V", [E // C, P, DB, C]),
        X1=scratch("X1", [2 * E, D]), X2=scratch("X2", [2 * E, D]), X3=scratch("X3", [2 * E, D]),
        H=[scratch(f"H{i}", [2 * E, D]) for i in range(3)],
        G=scratch("G", [2 * E, 2 * D]), Z=scratch("Z", [2 * E, D]))
    with ExitStack() as ctx:
        K["sb"] = scopes(nc, ctx, "k")[0]
        for n in ("srcF", "dstF"):
            K[n] = [K["sb"](f"{n}{i}", [R, TILES]) for i in range(2)]
        for n in ("srcU", "dstU"):
            K[n] = [K["sb"](f"{n}{i}", [R, TILES], U32) for i in range(2)]
        for n in ("ordU", "m1s", "m2s", "m1d", "m2d", "ownA", "ownB", "outA", "outB"):
            K[n] = K["sb"](n, [R, TILES], U32)
        for n in ("inv2", "norm3", "self3"):
            K[n] = K["sb"](n, [R, TILES])
        K["WAs"], K["WAd"], K["WAe"] = K["sb"]("WAs", [P, DB, 8]), K["sb"]("WAd", [P, DB, 8]), K["sb"]("WAe", [64, 8])
        K["rep0"], K["rep1"], K["sum0"] = K["sb"]("rep0", [4, D]), K["sb"]("rep1", [8, D]), K["sb"]("sum0", [P, DB, 4])
        load_constants(nc, K, A)
        att_weights(nc, K, A)
        rank_edges(nc, K, A, "rank0", A["dst"], S["edges"][0])
        rank_edges(nc, K, A, "rank1", A["src"], S["edges"][1])
        load_sorted(nc, K, A, S)
        node_maps(nc, K, A, S)
        dense(nc, K, A, N)
        with ExitStack() as c2:
            sb = scopes(nc, c2, "attn")[0]
            seg, alpha = sb("seg", [P, E + 1]), sb("alpha", [8, E])
            load_segments(nc, K, "seg_a", S, 0, seg)
            scores0(nc, K, A, S, alpha)
            softmax(nc, K, "sm0", 4, seg, alpha, None)
            layer0_rows(nc, K, A, S, seg, alpha)
            with ExitStack() as c3:
                adst = scopes(nc, c3, "attn1")[0]("adst", [8, E])
                scores1(nc, K, A, S, alpha, adst)
                softmax(nc, K, "sm1", 8, seg, alpha, adst)
            layer1_rows(nc, K, A, S, seg, alpha)
        with ExitStack() as c2:
            seg = scopes(nc, c2, "l2s")[0]("seg", [P, E + 1])
            load_segments(nc, K, "seg_b", S, 1, seg)
            for l in range(3):
                layer2_rows(nc, K, A, S, seg, l)
        with ExitStack() as c2:
            seg = scopes(nc, c2, "l3s")[0]("seg", [P, E + 1])
            load_segments(nc, K, "seg_c", S, 0, seg)
            for l in range(3):
                layer3_rows(nc, K, A, S, seg, l)


_INS = ['x', 'src', 'dst', 'edge_attr_64', 'L0_gnn_Wq', 'L0_gnn_bq', 'L0_gnn_Wk', 'L0_gnn_bk', 'L0_gnn_Wv',
        'L0_gnn_bv', 'L0_gnn_Wskip', 'L0_gnn_bskip', 'L0_gnn_gamma', 'L0_gnn_beta_ln', 'L1_gnn_W',
        'L1_gnn_W_e', 'L1_gnn_att_src', 'L1_gnn_att_dst', 'L1_gnn_att_edge', 'L1_gnn_bias', 'L1_gnn_gamma',
        'L1_gnn_beta', 'L2_gnn_W_in', 'L2_gnn_b_in', 'L2_gnn_W_agg', 'L2_gnn_W_self', 'L2_gnn_b_hid',
        'L2_gnn_W_out', 'L2_gnn_b_out', 'L3_gnn_W1', 'L3_gnn_b1', 'L3_gnn_W2', 'L3_gnn_b2', 'L3_gnn_W3',
        'L3_gnn_b3']


def kernel(**inputs):
    import numpy as _np
    import concourse.bacc as _bacc
    from concourse import mybir as _mybir
    from concourse.bass_utils import run_bass_kernel_spmd as _run

    nc = _bacc.Bacc("TRN2", target_bir_lowering=False, num_devices=1)
    arrays, args = {}, {}
    for name in _INS:
        a = _np.ascontiguousarray(inputs[name])
        arrays[f"in_{name}_dram"] = a
        args[name] = nc.dram_tensor(f"in_{name}_dram", a.shape, _mybir.dt.from_np(a.dtype), kind="ExternalInput").ap()
    out_shape = inputs['x'].shape
    args["out"] = nc.dram_tensor("out_0_dram", out_shape, _mybir.dt.float32, kind="ExternalOutput").ap()
    build(nc, args)
    r = _run(nc, [arrays], core_ids=[0])
    return r.results[0]["out_0_dram"]
```

```python
from contextlib import ExitStack

import concourse.bass as bass
from concourse import mybir

F32 = mybir.dt.float32
I32 = mybir.dt.int32
U32 = mybir.dt.uint32
BF16 = mybir.dt.bfloat16
ALU = mybir.AluOpType
ACT = mybir.ActivationFunctionType
AX = mybir.AxisListType

P = 128
R = 125
J = 4
C = R * J
D = 256
DB = D // P
EPS = 1e-5
BIG = 1e30


def rows_of(table, n):
    return table[bass.ds(n * C, C), :].rearrange("(j p) d -> p j d", p=R)


def wide(row, j=J):
    return row.unsqueeze(1).broadcast_to([row.shape[0], j, row.shape[1]])



def wait(e, s, value):
    e.wait_ge(s, value)
    e.nop(nofuse=True)


def transposes(e, K, out, rows, blocks, width=P):
    for k in range(blocks):
        for j in range(J):
            last = e.transpose(out[0:width, k, j * R:(j + 1) * R],
                               rows[:, j, k * width:(k + 1) * width], K["ident"][0:R, 0:R])
    return last


def product_T(e, out, w, m, xT, blocks, first=True, last=True):
    for k in range(blocks):
        mm = e.matmul(out, w[:, k, m * P:(m + 1) * P], xT[:, k, :],
                      start=first and k == 0, stop=last and k == blocks - 1)
    return mm


def product_rows(e, out, w, xT, blocks, aggT=None, ident=None):
    for j in range(J):
        if aggT is None:
            for k in range(blocks):
                mm = e.matmul(out[0:R, j, :], xT[:, k, j * R:(j + 1) * R], w[:, k, :],
                              start=k == 0, stop=k == blocks - 1)
        else:
            for m in range(DB):
                half = out[0:R, j, m * P:(m + 1) * P]
                for k in range(blocks):
                    e.matmul(half, xT[:, k, j * R:(j + 1) * R], w[:, k, m * P:(m + 1) * P],
                             start=k == 0, stop=False)
                mm = e.matmul(half, aggT[:, m, j * R:(j + 1) * R], ident[:, :], start=False, stop=True)
    return mm


def agg_rows(e, out, aggT, ident):
    for j in range(J):
        for k in range(DB):
            mm = e.transpose(out[0:R, j, k * P:(k + 1) * P], aggT[:, k, j * R:(j + 1) * R], ident[:, :])
    return mm


def ln_stats(e, L, t, src):
    for j in range(J):
        ins = e.bn_stats(L["stats"][:, j, :], src[:, j, :])
    ins.then_inc(L["s_stats"], 1)
    wait(e, L["s_stats"], t)
    for j in range(J):
        ins = e.bn_aggr(L["mv"][:, j, :], L["stats"][:, j, :])
    ins.then_inc(L["s_var"], 1)


def ln_scale(e, L, t, src, dst):
    e.wait_ge(L["s_rstd"], t)
    for j in range(J):
        ins = e.tensor_scalar(dst[:, j, :], src[:, j, :], L["mv"][:, j, 0:1], L["rstd"][:, j:j + 1],
                              ALU.subtract, ALU.mult)
    return ins


def ln_affine(e, L, t, src, gamma, plus, dst):
    wait(e, L["s_var"], t)
    for j in range(J):
        e.scalar_tensor_tensor(out=dst[:, j, :], in0=src[:, j, :], scalar=L["mv"][:, j, 0:1], in1=gamma[:, :],
                               op0=ALU.subtract, op1=ALU.mult)
    e.drain()
    e.wait_ge(L["s_rstd"], t)
    for j in range(J):
        ins = e.scalar_tensor_tensor(out=dst[:, j, :], in0=dst[:, j, :], scalar=L["rstd"][:, j:j + 1],
                                     in1=plus[:, j, :], op0=ALU.mult, op1=ALU.add)
    return ins


def ln_vector(e, K, L, t, src, dst):
    ln_stats(e, L, t, src)
    return ln_scale(e, L, t, src, dst)


def ln_pool(e, K, L, t):
    wait(e, L["s_var"], t)
    e.tensor_scalar(L["vare"][:, :], L["mv"][:, :, 1], EPS, None, ALU.add).then_inc(L["s_vare"], 1)
    e.wait_ge(L["s_vare"], t)
    e.tensor_tensor(L["rstd"][:, :], L["vare"][:, :], K["mhalf"][:, :], ALU.pow).then_inc(L["s_rstd"], 1)


def ln_buffers(sb, sem, name):
    return dict(
        stats=sb(f"{name}_stats", [R, J, 6]), mv=sb(f"{name}_mv", [R, J, 2]),
        vare=sb(f"{name}_vare", [R, J]), rstd=sb(f"{name}_rstd", [R, J]),
        s_stats=sem(f"{name}_s_stats"), s_var=sem(f"{name}_s_var"),
        s_vare=sem(f"{name}_s_vare"), s_rstd=sem(f"{name}_s_rstd"))


def scopes(nc, ctx, name):
    def sb(n, s, d=F32):
        return ctx.enter_context(nc.sbuf_tensor(f"{name}_{n}", s, d))

    def ps(n, s, d=F32):
        return ctx.enter_context(nc.psum_tensor(f"{name}_{n}", s, d))

    sems = []

    def sem(n):
        sems.append(nc.alloc_semaphore(name=f"{name}_{n}"))
        return sems[-1]

    def done():
        if sems:
            nc.clear_and_free_semaphores(sems)
            nc.all_engine_barrier()
    ctx.callback(done)
    return sb, ps, sem



def load_constants(nc, K, A):
    mats = {"Wq": A["L0_gnn_Wq"], "Wk": A["L0_gnn_Wk"], "Wv": A["L0_gnn_Wv"], "Wskip": A["L0_gnn_Wskip"],
            "W": A["L1_gnn_W"], "W_in": A["L2_gnn_W_in"], "W_out": A["L2_gnn_W_out"],
            "W1": A["L3_gnn_W1"], "W2": A["L3_gnn_W2"], "W3": A["L3_gnn_W3"]}
    for l in range(3):
        mats[f"Wagg{l}"] = A["L2_gnn_W_agg"][l]
        mats[f"Wself{l}"] = A["L2_gnn_W_self"][l]
    cols = {"bq": A["L0_gnn_bq"], "bk": A["L0_gnn_bk"], "bv": A["L0_gnn_bv"], "b_in": A["L2_gnn_b_in"],
            "b1": A["L3_gnn_b1"], "b2": A["L3_gnn_b2"]}
    for l in range(3):
        cols[f"b_hid{l}"] = A["L2_gnn_b_hid"][l]
    rows = {"bskip": A["L0_gnn_bskip"], "gamma0": A["L0_gnn_gamma"], "beta0": A["L0_gnn_beta_ln"],
            "bias1": A["L1_gnn_bias"], "gamma1": A["L1_gnn_gamma"], "beta1": A["L1_gnn_beta"],
            "b_out": A["L2_gnn_b_out"], "b3": A["L3_gnn_b3"]}
    sb = K["sb"]
    for n, m in mats.items():
        K[n] = sb(n, [P, m.shape[0] // P, m.shape[1]])
    for n, m in cols.items():
        K[n] = sb(n, [P, m.shape[0] // P])
    for n, m in rows.items():
        K[n] = sb(n, [R, m.shape[0]])
    K["ident"] = sb("ident", [P, P])
    K["mhalf"] = sb("mhalf", [R, J])
    with ExitStack() as ctx:
        sem = scopes(nc, ctx, "const")[2]
        s_w, s_i0, s_i1 = sem("s_w"), sem("s_i0"), sem("s_i1")
        block = ctx.enter_context(nc.Block())

        @block.sync
        def _(e):
            for n, m in mats.items():
                e.dma_start(K[n][:, :, :], m.rearrange("(k p) n -> p k n", p=P)).then_inc(s_w, 16)
            for n, m in cols.items():
                e.dma_start(K[n][:, :], m.rearrange("(k p) -> p k", p=P),
                            allow_slow_non_contiguous=True).then_inc(s_w, 16)
            for n, m in rows.items():
                e.dma_start(K[n][:, :], m.unsqueeze(0).broadcast_to([R, m.shape[0]])).then_inc(s_w, 16)
            e.wait_ge(s_w, 16 * (len(mats) + len(cols) + len(rows)))

        @block.gpsimd
        def _(e):
            e.memset(K["mhalf"][:, :], -0.5)
            e.memset(K["ident"][:, :], 0.0).then_inc(s_i0, 1)
            e.wait_ge(s_i0, 1)
            e.affine_select(out=K["ident"][:, :], in_=K["ident"][:, :], compare_op=ALU.not_equal, fill=1.0,
                            base=0, pattern=[[-1, P]], channel_multiplier=1).then_inc(s_i1, 1)


def dense(nc, K, A, N, riding):
    chunks = N // C
    RING = 2
    with ExitStack() as ctx:
        sb, ps, sem = scopes(nc, ctx, "dense")
        xr, xb, u, v = (sb(n, [R, J, D]) for n in ("xr", "xb", "u", "v"))
        x1, x2, x3, xres = (sb(n, [R, J, D]) for n in ("x1", "x2", "x3", "xres"))
        t3, o, z = (sb(n, [R, J, D]) for n in ("t3", "o", "z"))
        xT, x2T, x3T = (sb(n, [P, DB, C]) for n in ("xT", "x2T", "x3T"))
        h = [sb(f"h{i}", [P, DB, C]) for i in range(2)]
        g1, g2 = sb("g1", [P, 2 * DB, C]), sb("g2", [P, 2 * DB, C])
        pF = ps("pF", [P, DB, 512])
        pG = ps("pG", [P, DB, 512])
        pGr = pG[:, :, :].rearrange("p a (b d) -> p (a b) d", d=D)
        pO = ps("pO", [P, J, D])
        ring = ps("ring", [P, RING, 512])
        LF, LB, LO = (ln_buffers(sb, sem, n) for n in ("front", "back", "last"))
        s_x, s_xT, s_xTc, s_skip = sem("s_x"), sem("s_xT"), sem("s_xTc"), sem("s_skip")
        s_u, s_g, s_xb0, s_t0 = sem("s_u"), sem("s_g"), sem("s_xb0"), sem("s_t0")
        s_x1, s_y, s_xb1, s_t1 = sem("s_x1"), sem("s_y"), sem("s_xb1"), sem("s_t1")
        s_x2, s_x2T, s_x2Tc = sem("s_x2"), sem("s_x2T"), sem("s_x2Tc")
        s_mm, s_ev = sem("s_mm"), sem("s_ev")
        s_o, s_oa, s_tb, s_x3, s_x3T, s_x3Tc, s_xres = (
            sem(n) for n in ("s_o", "s_oa", "s_tb", "s_x3", "s_x3T", "s_x3Tc", "s_xres"))
        s_z, s_za, s_zr, s_zb, s_out, s_st = (sem(n) for n in ("s_z", "s_za", "s_zr", "s_zb", "s_out", "s_st"))

        back1 = [(K["W_in"], x2T, DB, m, K["b_in"], h[0], False) for m in range(DB)]
        for l in range(3):
            back1 += [(K[f"Wself{l}"], h[l % 2], DB, m, K[f"b_hid{l}"], h[(l + 1) % 2], True)
                      for m in range(DB)]
        hL = h[1]
        back2 = [(K["W1"], x3T, DB, m, K["b1"], g1, True) for m in range(2 * DB)]
        back2 += [(K["W2"], g1, 2 * DB, m, K["b2"], g2, True) for m in range(2 * DB)]
        G1, G2 = len(back1), len(back2)

        def ring_at(c, part, g):
            if part == 1:
                return c * (G1 + G2) - (G2 if not isinstance(c, int) or c > 0 else 0) + g
            return (c + 1) * G1 + c * G2 + (G1 if not isinstance(c, int) or c < chunks - 1 else 0) + g

        stages = riding(ctx)
        stages += ((chunks - 3 - sum(s[0] for s in stages), {}, {}),)
        block = ctx.enter_context(nc.Block())

        def turns(e, turn, engine):
            def alone(part):
                pass
            turn(0, True, False, alone)
            c = 1
            for count, each, after in stages:
                with e.Fori(c, c + count) as i:
                    def ride(part):
                        if engine in each:
                            each[engine](e, i - c, part)
                    turn(i, True, True, ride)
                if engine in after:
                    after[engine](e)
                c += count
            turn(chunks - 2, True, True, alone)
            turn(chunks - 1, False, True, alone)

        @block.sync
        def _(e):
            e.dma_start(xr[:], rows_of(A["x"], 0)).then_inc(s_x, 16)
            e.wait_ge(s_t0, 1)
            e.dma_start(xr[:], rows_of(A["x"], 1)).then_inc(s_x, 16)

            def turn(c, front, back, ride):
                if not isinstance(c, int) or c < chunks - 2:
                    if front:
                        wait(e, s_t0, c + 2)
                        e.dma_start(xr[:], rows_of(A["x"], c + 2)).then_inc(s_x, 16)
                ride(0)
                if back:
                    wait(e, s_out, c)
                    e.dma_start(rows_of(A["out"], c - 1), o[:]).then_inc(s_st, 16)
            turns(e, turn, "sync")
            e.wait_ge(s_out, chunks)
            e.dma_start(rows_of(A["out"], chunks - 1), o[:]).then_inc(s_st, 16)
            e.wait_ge(s_st, 16 * chunks + 1)

        def pe_group(e, c, part, g):
            groups = back1 if part == 1 else back2
            w, xin, nb, m, _, _, _ = groups[g]
            at = ring_at(c, part, g)
            first = g > 0 and groups[g - 1][1] is not xin
            e.wait_ge(s_ev, at + 1)
            for k in range(nb):
                if first:
                    e.wait_ge(s_ev, at - nb + k + 1 + RING)
                mm = e.matmul(ring[:, g % RING, 0:C], w[:, k, m * P:(m + 1) * P], xin[:, k, :],
                              start=k == 0, stop=k == nb - 1)
            mm.then_inc(s_mm, 1)

        def pe_x(e, c):
            e.wait_ge(s_x, 16 * c + 16)
            if not isinstance(c, int) or c > 0:
                e.wait_ge(s_u, c)
            transposes(e, K, pG, xr, DB).then_inc(s_xT, 1)

        def pe_skip(e, c):
            e.wait_ge(s_xTc, c + 1)
            product_rows(e, pGr, K["Wskip"], xT, DB).then_inc(s_skip, 1)

        def pe_x2(e, c):
            e.wait_ge(s_x2, c + 1)
            transposes(e, K, pF, x2, DB).then_inc(s_x2T, 1)

        def pe_back2(e, c):
            e.wait_ge(s_x3Tc, c + 1)
            for g in range(G2):
                pe_group(e, c, 2, g)
            e.wait_ge(s_ev, ring_at(c, 2, G2) + RING)
            e.wait_ge(s_oa, c + 3 if not isinstance(c, int) or c < chunks - 1 else c + 2)
            product_rows(e, pO, K["W3"], g2, 2 * DB).then_inc(s_z, 1)

        @block.tensor
        def _(e):
            pe_x(e, 0)
            pe_skip(e, 0)
            pe_x2(e, 0)

            def turn(c, front, back, ride):
                if front:
                    pe_x(e, c + 1)
                e.wait_ge(s_x2Tc, c + 1)
                pe_group(e, c, 1, 0)
                pe_group(e, c, 1, 1)
                if back:
                    e.wait_ge(s_x3, c)
                    transposes(e, K, pF, x3, DB).then_inc(s_x3T, 1)
                if front:
                    pe_skip(e, c + 1)
                for g in range(2, G1):
                    pe_group(e, c, 1, g)
                e.wait_ge(s_ev, ring_at(c, 1, G1) + RING)
                if back:
                    e.wait_ge(s_za, c)
                product_rows(e, pO, K["W_out"], hL, DB).then_inc(s_o, 1)
                if back:
                    pe_back2(e, c - 1)
                if front:
                    pe_x2(e, c + 1)
            turns(e, turn, "tensor")
            e.wait_ge(s_x3, chunks)
            transposes(e, K, pF, x3, DB).then_inc(s_x3T, 1)
            pe_back2(e, chunks - 1)

        @block.scalar
        def _(e):
            e.sem_inc(s_ev, RING)

            def evac(c, part, g):
                _, _, _, m, bias, out, relu = (back1 if part == 1 else back2)[g]
                e.wait_ge(s_mm, ring_at(c, part, g) + 1)
                e.activation(out[:, m, :], ring[:, g % RING, 0:C], ACT.Relu if relu else ACT.Identity,
                             bias=bias[:, m:m + 1]).then_inc(s_ev, 1)

            def x_copy(c):
                e.wait_ge(s_xT, c + 1)
                e.activation(xT[:, :, :], pG[:, :, 0:C], ACT.Copy).then_inc(s_xTc, 1)

            def gelu(c):
                e.wait_ge(s_u, c + 1)
                e.activation(v[:, :, :], u[:, :, :], ACT.Gelu).then_inc(s_g, 1)

            def x2_copy(c):
                e.wait_ge(s_x2T, c + 1)
                e.activation(x2T[:, :, :], pF[:, :, 0:C], ACT.Copy).then_inc(s_x2Tc, 1)

            def x3_copy(c):
                e.wait_ge(s_x3T, c + 1)
                e.activation(x3T[:, :, :], pF[:, :, 0:C], ACT.Copy).then_inc(s_x3Tc, 1)

            def x3_keep(c):
                if not isinstance(c, int) or c > 0:
                    e.wait_ge(s_zb, c)
                e.activation(xres[:, :, :], x3[:, :, :], ACT.Copy).then_inc(s_xres, 1)

            def relu_out(c):
                e.wait_ge(s_za, c + 2)
                e.activation(z[:, :, :], z[:, :, :], ACT.Relu).then_inc(s_zr, 1)

            x_copy(0)
            gelu(0)
            x2_copy(0)

            def turn(c, front, back, ride):
                if front:
                    x_copy(c + 1)
                for g in range(G1):
                    evac(c, 1, g)
                    if back and g == 1:
                        x3_copy(c - 1)
                    if front and g == 3:
                        gelu(c + 1)
                    if back and g == 5:
                        x3_keep(c - 1)
                if back:
                    for g in range(G2):
                        evac(c - 1, 2, g)
                if front:
                    x2_copy(c + 1)
                if back:
                    relu_out(c - 1)
            turns(e, turn, "scalar")
            x3_copy(chunks - 1)
            x3_keep(chunks - 1)
            for g in range(G2):
                evac(chunks - 1, 2, g)
            relu_out(chunks - 1)

        @block.vector
        def _(e):
            def front_0(c):
                e.drain()
                e.wait_ge(s_skip, c + 1)
                e.tensor_tensor(u[:, :, :], pGr[0:R, :, :], wide(K["bskip"][:, :]), ALU.add).then_inc(s_u, 1)
                e.wait_ge(s_g, c + 1)
                ln_stats(e, LF, 4 * c + 1, v)
                wait(e, s_xb0, c + 1)
                ln_affine(e, LF, 4 * c + 1, v, K["gamma0"], xb, u).then_inc(s_t0, 1)
                e.wait_ge(s_t0, c + 1)
                ln_vector(e, K, LF, 4 * c + 2, u, x1).then_inc(s_x1, 1)

            def front_1(c):
                e.wait_ge(s_y, c + 1)
                ln_stats(e, LF, 4 * c + 3, v)
                wait(e, s_xb1, c + 1)
                ln_affine(e, LF, 4 * c + 3, v, K["gamma1"], xb, u).then_inc(s_t1, 1)
                e.wait_ge(s_t1, c + 1)
                ln_stats(e, LF, 4 * c + 4, u)
                if not isinstance(c, int) or c > 0:
                    wait(e, s_tb, c)
                ln_scale(e, LF, 4 * c + 4, u, x2).then_inc(s_x2, 1)

            def back_1(c):
                e.drain()
                e.wait_ge(s_o, c + 1)
                wait(e, s_tb, c + 1)
                e.tensor_tensor(t3[:, :, :], pO[0:R, :, :], t3[:, :, :], ALU.add).then_inc(s_oa, 1)
                wait(e, s_oa, c + 2)
                ln_stats(e, LB, c + 1, t3)
                if not isinstance(c, int) or c > 0:
                    wait(e, s_xres, c)
                ln_scale(e, LB, c + 1, t3, x3).then_inc(s_x3, 1)

            def back_2_bias(c):
                e.drain()
                e.wait_ge(s_z, c + 1)
                e.tensor_tensor(z[:, :, :], pO[0:R, :, :], wide(K["b3"][:, :]), ALU.add).then_inc(s_za, 1)

            def back_2_stats(c):
                e.wait_ge(s_zr, c + 1)
                wait(e, s_xres, c + 1)
                e.tensor_tensor(z[:, :, :], z[:, :, :], xres[:, :, :], ALU.add).then_inc(s_zb, 1)
                e.wait_ge(s_zb, c + 1)
                ln_stats(e, LO, c + 1, z)
                wait(e, s_st, 16 * c + 1)
                ln_scale(e, LO, c + 1, z, o).then_inc(s_out, 1)

            e.sem_inc(s_oa, 1)
            e.sem_inc(s_za, 1)
            front_0(0)
            front_1(0)

            def turn(c, front, back, ride):
                if front:
                    front_0(c + 1)
                ride(0)
                back_1(c)
                if front:
                    front_1(c + 1)
                ride(1)
                if back:
                    back_2_bias(c - 1)
                ride(2)
                if back:
                    back_2_stats(c - 1)
            turns(e, turn, "vector")
            back_2_bias(chunks - 1)
            back_2_stats(chunks - 1)

        @block.gpsimd
        def _(e):
            e.sem_inc(s_st, 1)

            def front_0(c):
                e.drain()
                e.wait_ge(s_x, 16 * c + 16)
                e.tensor_tensor(xb[:, :, :], xr[:, :, :], wide(K["beta0"][:, :]), ALU.add).then_inc(s_xb0, 1)
                ln_pool(e, K, LF, 4 * c + 1)
                ln_pool(e, K, LF, 4 * c + 2)
                wait(e, s_x1, c + 1)
                e.tensor_tensor(v[:, :, :], x1[:, :, :], wide(K["bias1"][:, :]), ALU.add).then_inc(s_y, 1)
                e.tensor_tensor(xb[:, :, :], x1[:, :, :], wide(K["beta1"][:, :]), ALU.add).then_inc(s_xb1, 1)

            def front_1(c):
                ln_pool(e, K, LF, 4 * c + 3)
                ln_pool(e, K, LF, 4 * c + 4)
                wait(e, s_x2, c + 1)
                if not isinstance(c, int) or c > 0:
                    wait(e, s_x3, c)
                e.tensor_tensor(t3[:, :, :], x2[:, :, :], wide(K["b_out"][:, :]), ALU.add).then_inc(s_tb, 1)

            def back_1(c):
                ln_pool(e, K, LB, c + 1)

            def back_2(c):
                ln_pool(e, K, LO, c + 1)

            front_0(0)
            front_1(0)

            def turn(c, front, back, ride):
                if front:
                    front_0(c + 1)
                back_1(c)
                if front:
                    front_1(c + 1)
                ride(0)
                if back:
                    back_2(c - 1)
                ride(1)
            turns(e, turn, "gpsimd")
            back_2(chunks - 1)



TILES = 40
FAR = 1 << 17


def load_segments(nc, K, name, S, i, seg):
    with ExitStack() as ctx:
        sem = scopes(nc, ctx, name)[2]
        s_ld = sem("s_ld")
        block = ctx.enter_context(nc.Block())

        @block.sync
        def _(e):
            e.dma_start(seg[:], S["seg"][i:i + 1, :].broadcast_to([P, K["E"] + 1])).then_inc(s_ld, 16)
            e.wait_ge(s_ld, 16)


def prepare(nc, K, A, S):
    E, N = K["E"], K["N"]
    TR = 5
    W, POINTS = 10, 2
    SCATTER_TURNS = TILES // (POINTS * W)
    GROUPS_0 = TILES // TR

    def stages(ctx):
        sb, ps, sem = scopes(nc, ctx, "prep")
        keyI = sb("keyI", [R, E], I32)
        first = sb("first", [R, E + 1])
        less = sb("less", [R, E], BF16)
        weight = first[:, 0:E].bitcast(BF16)
        srcC, dstC, keyC = sb("srcC", [R, TILES], I32), sb("dstC", [R, TILES], I32), sb("keyC", [R, TILES])
        rank, rankU = sb("rank", [R, TILES]), [sb(f"rankU{i}", [R, TILES], U32) for i in range(2)]
        pay = sb("pay", [R, TILES, 4], I32)
        idxE, payE = sb("idxE", [R, W], U32), sb("payE", [R, W, 4], I32)
        rows = [sb(f"rows{i}", [R, TILES, 4], I32) for i in range(2)]
        zero = sb("zero", [R, 4 * N // R])
        same = [sb(f"same{i}", [R, TILES]) for i in range(2)]
        cntC = [sb(f"cntC{i}", [R, TILES]) for i in range(2)]
        payN = [sb(f"payN{i}", [R, TILES, 2]) for i in range(2)]
        at = [sb(f"at{i}", [R, TILES], U32) for i in range(2)]
        pos, atF, half = sb("pos", [R, TILES]), sb("atF", [R, TILES]), sb("half", [R, TILES])
        tmp = [sb(f"tmp{i}", [R, TILES]) for i in range(4)]
        deg = [sb(f"deg{i}", [R, TILES]) for i in range(2)]
        dinv = [sb(f"dinv{i}", [R, TILES]) for i in range(2)]
        one = sb("one", [2, 1])
        payB, gotB = sb("payB", [R, W, 2]), sb("gotB", [R, W, 4])
        looks = [(K["srcU"][0], "src0"), (K["dstU"][0], "dst0"), (K["srcU"][1], "src1"), (K["dstU"][1], "dst1")]
        info = {n: sb(f"info_{n}", [R, TILES, 4]) for _, n in looks}
        s_col, s_key, s_zero, s_pos, s_weight = (sem(n) for n in ("s_col", "s_key", "s_zero", "s_pos", "s_weight"))
        s_pay, s_rank, s_cE, s_scE, s_rows, s_krow = (sem(n) for n in ("s_pay", "s_rank", "s_cE", "s_scE",
                                                                      "s_rows", "s_krow"))
        s_z, s_cnt, s_line, s_seg, s_at, s_cN, s_scN = (sem(n) for n in ("s_z", "s_cnt", "s_line", "s_seg", "s_at",
                                                                        "s_cN", "s_scN"))
        s_cG, s_got, s_copied, s_pw, s_pd = (sem(n) for n in ("s_cG", "s_got", "s_copied", "s_pw", "s_pd"))
        keys = [A["dst"], A["src"]]

        def sync_first(e, t, part):
            if part == 0:
                for c, a in ((srcC, A["src"]), (dstC, A["dst"])):
                    e.dma_start(c[:], a.rearrange("(t p) -> p t", p=R), allow_slow_non_contiguous=True)\
                        .then_inc(s_col, 16)
                e.dma_start(keyI[:], keys[0].unsqueeze(0).broadcast_to([R, E])).then_inc(s_key, 16)
                e.wait_ge(s_z, 1)
                e.dma_start(S["nodes"].rearrange("(p a) w -> p (a w)", p=R), zero[:]).then_inc(s_zero, 16)

        def pool_first(e, t, part):
            if part == 0:
                e.memset(zero[:], 0.0).then_inc(s_z, 1)
                e.memset(half[:], -0.5)
                e.memset(one[:], 1.0)
                e.memset(pay[:], 0)
                e.memset(weight[:, :], 0.5)
            if part == 1:
                e.drain()
                e.iota(pay[:, :, 2], pattern=[[R, TILES]], base=0, channel_multiplier=1)
                e.iota(pos[:], pattern=[[R, TILES]], base=0, channel_multiplier=1,
                       allow_small_or_imprecise_dtypes=True).then_inc(s_pos, 1)
                e.affine_select(out=weight[:, :], in_=weight[:, :], compare_op=ALU.is_gt, fill=0.0,
                                base=E, pattern=[[-1, 2 * E]], channel_multiplier=1).then_inc(s_weight, 1)

        def rank_keys(i):
            def keys_of_rows(e):
                e.wait_ge(s_col, 32)
                e.tensor_copy(keyC[:], (dstC, srcC)[i][:])
                if i == 0:
                    e.wait_ge(s_pos, 1)
                    e.tensor_copy(pay[:, :, 0], srcC[:])
                    e.tensor_copy(pay[:, :, 1], dstC[:]).then_inc(s_pay, 1)
                    e.wait_ge(s_weight, 1)
                e.wait_ge(s_key, 16 * i + 16)
                e.drain()
            return keys_of_rows

        def rank_turn(e, t, part):
            for k in {0: (0, 1), 1: (), 2: (2, 3, 4)}[part]:
                e.drain()
                n = t * TR + k
                e.scalar_tensor_tensor(out=less[:], in0=keyI[:], scalar=keyC[:, bass.ds(n, 1)],
                                       in1=weight[:, bass.ds(n * (-R) + E, E)], op0=ALU.subtract,
                                       op1=ALU.is_lt, accum_out=rank[:, bass.ds(n, 1)])
            e.drain()

        def rank_done(i):
            def last(e):
                e.tensor_copy(rankU[i][:], rank[:]).then_inc(s_rank, 1)
                e.drain()
            return last

        def next_keys(e):
            e.wait_ge(s_rank, 1)
            e.dma_start(keyI[:], keys[1].unsqueeze(0).broadcast_to([R, E])).then_inc(s_key, 16)

        def scatter_edges(i, width, points):
            def at_point(e, t, part):
                if part not in points:
                    return
                g = t * len(points) + points.index(part)
                use = g + i * GROUPS_0
                wait(e, s_rank, i + 1)
                e.wait_ge(s_pay, 1)
                e.tensor_copy(idxE[:, 0:width], rankU[i][:, bass.ds(g * width, width)])
                e.tensor_copy(payE[:, 0:width, :], pay[:, bass.ds(g * width, width), :]).then_inc(s_cE, 1)
                wait(e, s_cE, use + 1)
                for k in range(width):
                    e.indirect_dma_start(S["edges"][i], bass.IndirectOffsetOnAxis(ap=idxE[:, k:k + 1], axis=0),
                                         payE[:, k, :], None).then_inc(s_scE, 16)
                wait(e, s_scE, g * (16 * width) + 16 * width + i * 16 * TILES)
            return at_point

        def load_tables(e, t, part):
            if part == 0:
                e.wait_ge(s_scE, 2 * 16 * TILES)
                for i in range(2):
                    e.dma_start(rows[i][:], S["edges"][i].rearrange("(t p) w -> p t w", p=R)).then_inc(s_rows, 16)
                    e.dma_start(keyI[i:i + 1, :], S["edges"][i][:, 1 - i:2 - i].rearrange("e w -> w e"),
                                allow_slow_non_contiguous=True).then_inc(s_krow, 16)

        def columns(e):
            e.wait_ge(s_rows, 32)
            for i in range(2):
                e.tensor_copy(K["srcF"][i][:], rows[i][:, :, 0])
                e.tensor_copy(K["dstF"][i][:], rows[i][:, :, 1])
                e.tensor_copy(K["srcU"][i][:], rows[i][:, :, 0])
                e.tensor_copy(K["dstU"][i][:], rows[i][:, :, 1])
            e.tensor_copy(K["ordU"][:], rows[0][:, :, 2])
            e.drain()

        def segments(e, t, part):
            if part == 1:
                e.drain()
                e.wait_ge(s_krow, 32)
                e.memset(first[0:2, 0:1], 0.0)
                e.memset(first[0:2, E:E + 1], 0.0)
                e.tensor_tensor(first[0:2, 1:E], keyI[0:2, 1:E], keyI[0:2, 0:E - 1], ALU.is_equal)
                e.drain()
            if part == 2:
                e.drain()
                counts = keyI[0:2, :].bitcast(F32)
                e.tensor_tensor_scan(counts, first[0:2, 0:E], one[0:2, 0:1].broadcast_to([2, E]), 0.0,
                                     ALU.mult, ALU.add).then_inc(s_cnt, 1)
                e.drain()

        def turn_rows(e, t, part):
            if part == 0:
                e.wait_ge(s_cnt, 1)
                e.dma_start(S["seg"], first[0:2, :]).then_inc(s_line, 16)
                e.dma_start(S["cnt"], keyI[0:2, :].bitcast(F32)).then_inc(s_line, 16)
                e.wait_ge(s_line, 32)
                for i in range(2):
                    e.dma_start(same[i][:], S["seg"][i, 1:E + 1].rearrange("(t p) -> p t", p=R),
                                allow_slow_non_contiguous=True).then_inc(s_seg, 16)
                    e.dma_start(cntC[i][:], S["cnt"][i].rearrange("(t p) -> p t", p=R),
                                allow_slow_non_contiguous=True).then_inc(s_seg, 16)

        def node_rows(e):
            e.drain()
            e.wait_ge(s_seg, 64)
            for i in range(2):
                e.tensor_copy(payN[i][:, :, 1], cntC[i][:])
                e.tensor_scalar(payN[i][:, :, 0], pos[:], 1.0, None, ALU.add)
                e.tensor_scalar(atF[:], (K["dstF"][0] if i == 0 else K["srcF"][1])[:], 2.0, float(i),
                                ALU.mult, ALU.add)
                e.drain()
                e.scalar_tensor_tensor(out=atF[:], in0=same[i][:], scalar=float(FAR), in1=atF[:],
                                       op0=ALU.mult, op1=ALU.add)
                e.drain()
                e.tensor_copy(at[i][:], atF[:])
                e.drain()
            e.tensor_copy(tmp[0][:], atF[:]).then_inc(s_at, 1)
            e.drain()

        def scatter_nodes(i):
            def at_point(e, t, part):
                if part == 0:
                    e.wait_ge(s_at, 1)
                    e.wait_ge(s_zero, 16)
                g = t * POINTS + part
                use = g + i * (TILES // W)
                e.tensor_copy(idxE[:], at[i][:, bass.ds(g * W, W)])
                e.tensor_copy(payB[:], payN[i][:, bass.ds(g * W, W), :]).then_inc(s_cN, 1)
                wait(e, s_cN, use + 1)
                for k in range(W):
                    e.indirect_dma_start(S["nodes"], bass.IndirectOffsetOnAxis(ap=idxE[:, k:k + 1], axis=0),
                                         payB[:, k, :], None, bounds_check=2 * N - 1,
                                         oob_is_err=False).then_inc(s_scN, 16)
                wait(e, s_scN, use * (16 * W) + 16 * W)
            return at_point

        wide_nodes = S["nodes"].rearrange("(n two) w -> n (two w)", two=2)

        def look_up(q):
            idx, name = looks[q]

            def at_point(e, t, part):
                g = t * POINTS + part
                use = g + q * (TILES // W)
                e.tensor_copy(idxE[:], idx[:, bass.ds(g * W, W)]).then_inc(s_cG, 1)
                wait(e, s_cG, use + 1)
                for k in range(W):
                    e.indirect_dma_start(gotB[:, k, :], None, wide_nodes,
                                         bass.IndirectOffsetOnAxis(ap=idxE[:, k:k + 1], axis=0))\
                        .then_inc(s_got, 16)
                wait(e, s_got, use * (16 * W) + 16 * W)
                e.tensor_copy(info[name][:, bass.ds(g * W, W), :], gotB[:]).then_inc(s_copied, 1)
                wait(e, s_copied, use + 1)
            return at_point

        def row_map(e, a, b, scale, shift, out):
            e.tensor_tensor(tmp[0][:], a, b, ALU.subtract)
            e.tensor_scalar(tmp[1][:], a, 0.0, None, ALU.is_gt)
            e.drain()
            e.scalar_tensor_tensor(out=tmp[2][:], in0=tmp[0][:], scalar=scale, in1=tmp[1][:],
                                   op0=ALU.add, op1=ALU.mult)
            e.drain()
            e.scalar_tensor_tensor(out=tmp[3][:], in0=tmp[2][:], scalar=shift, in1=b,
                                   op0=ALU.add, op1=ALU.add)
            e.drain()
            e.tensor_copy(out[:], tmp[3][:])
            e.drain()

        def map1(e, n, out):
            row_map(e, info[n][:, :, 0], info[n][:, :, 2], -float(E), float(E - 1), out)

        def map2(e, n, out):
            row_map(e, info[n][:, :, 2], info[n][:, :, 0], float(E), -1.0, out)

        def maps(e, t, part):
            e.drain()
            if part == 0:
                e.wait_ge(s_copied, 4 * TILES // W)
                map1(e, "src0", K["m1s"])
                map2(e, "src0", K["m2s"])
                e.reciprocal(K["inv2"][:], info["src1"][:, :, 3])
                e.tensor_scalar(deg[0][:], info["src0"][:, :, 1], 1.0, None, ALU.add)
                e.tensor_scalar(deg[1][:], info["dst0"][:, :, 1], 1.0, None, ALU.add).then_inc(s_pw, 1)
            if part == 1:
                map1(e, "dst1", K["m1d"])
                map2(e, "dst1", K["m2d"])
                map2(e, "dst0", K["ownA"])
                map1(e, "src1", K["ownB"])
            if part == 2:
                e.scalar_tensor_tensor(out=tmp[0][:], in0=same[0][:], scalar=float(FAR), in1=K["dstF"][0][:],
                                       op0=ALU.mult, op1=ALU.add)
                e.tensor_scalar(tmp[1][:], info["src1"][:, :, 0], 0.0, None, ALU.is_gt)
                e.drain()
                e.tensor_copy(K["outA"][:], tmp[0][:])
                e.tensor_tensor(tmp[2][:], tmp[1][:], same[1][:], ALU.max)
                e.drain()
                e.scalar_tensor_tensor(out=tmp[3][:], in0=tmp[2][:], scalar=float(FAR), in1=K["srcF"][1][:],
                                       op0=ALU.mult, op1=ALU.add)
                e.drain()
                e.tensor_copy(K["outB"][:], tmp[3][:])
                e.wait_ge(s_pd, 1)
                e.tensor_tensor(K["norm3"][:], dinv[0][:], dinv[1][:], ALU.mult)
                e.tensor_tensor(K["self3"][:], dinv[1][:], dinv[1][:], ALU.mult)
            e.drain()

        def degrees(e, t, part):
            if part == 0:
                e.wait_ge(s_pw, 1)
                e.tensor_tensor(dinv[0][:], deg[0][:], half[:], ALU.pow)
                e.tensor_tensor(dinv[1][:], deg[1][:], half[:], ALU.pow).then_inc(s_pd, 1)

        rank_turns = TILES // TR
        lines = [
            (1, {"sync": sync_first, "gpsimd": pool_first}, {"vector": rank_keys(0)}),
            (rank_turns, {"vector": rank_turn}, {"vector": rank_done(0), "sync": next_keys}),
            (1, {}, {"vector": rank_keys(1)}),
            (rank_turns, {"vector": rank_turn, "gpsimd": scatter_edges(0, TR, (1,))}, {"vector": rank_done(1)}),
            (SCATTER_TURNS, {"gpsimd": scatter_edges(1, W, tuple(range(POINTS)))}, {}),
            (1, {"sync": load_tables}, {"vector": columns}),
            (1, {"vector": segments}, {}),
            (1, {"sync": turn_rows}, {"vector": node_rows})]
        lines += [(SCATTER_TURNS, {"gpsimd": scatter_nodes(i)}, {}) for i in range(2)]
        lines += [(SCATTER_TURNS, {"gpsimd": look_up(q)}, {}) for q in range(4)]
        lines += [(1, {"vector": maps, "gpsimd": degrees}, {})]
        return tuple(lines)
    return stages


def att_weights(nc, K, A):
    with ExitStack() as ctx:
        sb, ps, sem = scopes(nc, ctx, "att")
        We = sb("We", [64, D])
        att = {n: sb(n, [P, D]) for n in ("src", "dst", "edge")}
        prod = sb("prod", [P, DB, D])
        s_ld = sem("s_ld")
        block = ctx.enter_context(nc.Block())
        drams = {"src": A["L1_gnn_att_src"], "dst": A["L1_gnn_att_dst"], "edge": A["L1_gnn_att_edge"]}

        @block.sync
        def _(e):
            e.dma_start(We[:], A["L1_gnn_W_e"]).then_inc(s_ld, 16)
            for n in att:
                e.dma_start(att[n][:], drams[n].rearrange("h c -> (h c)").unsqueeze(0).broadcast_to([P, D]))\
                    .then_inc(s_ld, 16)

        @block.vector
        def _(e):
            e.wait_ge(s_ld, 64)
            for n, out in (("src", K["WAs"]), ("dst", K["WAd"])):
                e.drain()
                e.tensor_tensor(prod[:], K["W"][:, :, :], att[n][:].unsqueeze(1).broadcast_to([P, DB, D]), ALU.mult)
                e.drain()
                e.tensor_reduce(out[:], prod[:].rearrange("p k (h c) -> p k h c", h=8), AX.X, ALU.add)
            e.drain()
            e.tensor_tensor(prod[0:64, 0, :], We[:], att["edge"][0:64, :], ALU.mult)
            e.drain()
            e.tensor_reduce(K["WAe"][:], prod[0:64, 0, :].rearrange("p (h c) -> p h c", h=8), AX.X, ALU.add)

        @block.gpsimd
        def _(e):
            def keep(t, base, pattern, cm):
                e.drain()
                e.affine_select(out=t, in_=t, compare_op=ALU.is_ge, fill=0.0, base=base, pattern=pattern,
                                channel_multiplier=cm)
            for t, w in ((K["rep0"], 64), (K["rep1"], 32)):
                e.memset(t[:], 1.0)
                keep(t[:], 0, [[1, D]], -w)
                keep(t[:], w - 1, [[-1, D]], w)
            e.memset(K["sum0"][:], 1.0)
            keep(K["sum0"][:], 0, [[P, DB], [-64, 4]], 1)
            keep(K["sum0"][:], 63, [[-P, DB], [64, 4]], -1)



LANES = 2


def pipeline(e, pairs, parts, part):
    steps = [(base,) + part(base, msg) for base, msg in parts]
    steps[0][1](steps[0][0])
    for n, (base, load, rest, head) in enumerate(steps):
        with e.Fori(base, base + pairs - 1) as i:
            head(i)
            load(i + 1)
            rest(i)
        head(base + pairs - 1)
        if n + 1 < len(steps):
            steps[n + 1][1](steps[n + 1][0])
        rest(base + pairs - 1)


def nothing(i):
    pass


def with_next(e, base, pairs, msg, front, rest):
    if not msg:
        with e.Fori(base, base + pairs) as i:
            rest(i, lambda: None)
        return
    front(base)
    with e.Fori(base, base + pairs - 1) as i:
        rest(i, lambda: front(i + 1))
    rest(base + pairs - 1, lambda: None)


def before(e, s, i):
    if not isinstance(i, int) or i > 0:
        wait(e, s, i)


def gather(e, table, idx, idxb, buf, n, s_idx, t, s_row):
    e.tensor_copy(idxb[:], idx[:, bass.ds(n * J, J)]).then_inc(s_idx, 1)
    wait(e, s_idx, t)
    for j in range(J):
        e.indirect_dma_start(buf[:, j, :], None, table, bass.IndirectOffsetOnAxis(ap=idxb[:, j:j + 1], axis=0))\
            .then_inc(s_row, 16)


def edge_scan(e, seg, n, src, agg, carry, blocks):
    for k in range(blocks):
        e.tensor_tensor_scan(agg[:, k, :], seg[:, bass.ds(n * C, C)], src[:, k, 0:C], carry[:, k:k + 1],
                             ALU.mult, ALU.add)
    e.drain()
    return e.tensor_copy(carry[:, 0:blocks], agg[:, :, C - 1])


def times_columns(e, rows, col, n, width):
    return e.tensor_tensor(rows[:], rows[:], col[:, bass.ds(n * J, J)].unsqueeze(2).broadcast_to([R, J, width]),
                           ALU.mult)


def value_chunk(S, n):
    return S["V"][bass.ds(n, 1)].rearrange("o p k c -> p (o k) c")


def lane_scopes(nc, ctx, name):
    sb, ps, sem = scopes(nc, ctx, name)
    lanes = range(LANES)
    return ((lambda n, s, d=F32: [sb(f"{n}{u}", s, d) for u in lanes]),
            (lambda n, s, d=F32: [ps(f"{n}{u}", s, d) for u in lanes]),
            (lambda n: [sem(f"{n}{u}") for u in lanes]), sb, sem)


def scores0(nc, K, A, S, alpha):
    with ExitStack() as ctx:
        sb, ps, sem, _, _ = lane_scopes(nc, ctx, "sc0")
        ms, ow = sb("ms", [R, J, D]), sb("ow", [R, J, D])
        idxm, idxo = sb("idxm", [R, J], U32), sb("idxo", [R, J], U32)
        msT, owT, qT, vT, prod = (sb(n, [P, DB, C]) for n in ("msT", "owT", "qT", "vT", "prod"))
        pA, pB = ps("pA", [P, DB, 512]), ps("pB", [P, DB, 512])
        s_im, s_io, s_rm, s_ro, s_T, s_Tc, s_q, s_qc, s_k, s_v, s_pr, s_vc, s_al, s_alc, s_st = (
            sem(n) for n in ("s_im", "s_io", "s_rm", "s_ro", "s_T", "s_Tc", "s_q", "s_qc", "s_k", "s_v",
                             "s_pr", "s_vc", "s_al", "s_alc", "s_st"))
        block = ctx.enter_context(nc.Block())
        pairs = K["E"] // C // LANES
        lanes = range(LANES)

        @block.sync
        def _(e):
            with e.Fori(0, pairs) as i:
                for u in lanes:
                    wait(e, s_vc[u], i + 1)
                    e.dma_start(value_chunk(S, i * LANES + u), vT[u][:]).then_inc(s_st[u], 16)
            for u in lanes:
                e.wait_ge(s_st[u], 16 * pairs + 1)

        @block.gpsimd
        def _(e):
            for u in lanes:
                e.sem_inc(s_st[u], 1)

            def load(i):
                for u in lanes:
                    before(e, s_T[u], i)
                    n = i * LANES + u
                    gather(e, A["x"], K["srcU"][0], idxm[u], ms[u], n, s_im[u], i + 1, s_rm[u])
                    gather(e, A["x"], K["dstU"][0], idxo[u], ow[u], n, s_io[u], i + 1, s_ro[u])
            pipeline(e, pairs, ((0, True),), lambda base, msg: (load, nothing, nothing))

        @block.tensor
        def _(e):
            for u in lanes:
                e.sem_inc(s_alc[u], 1)
            with e.Fori(0, pairs) as i:
                for u in lanes:
                    e.wait_ge(s_rm[u], i * (16 * J) + 16 * J)
                    e.wait_ge(s_ro[u], i * (16 * J) + 16 * J)
                    e.wait_ge(s_alc[u], i + 1)
                    transposes(e, K, pA[u], ms[u], DB)
                    transposes(e, K, pB[u], ow[u], DB).then_inc(s_T[u], 1)
                for u in lanes:
                    e.wait_ge(s_Tc[u], i + 1)
                    for m in range(DB):
                        mm = product_T(e, pA[u][:, m, 0:C], K["Wq"], m, owT[u], DB)
                    mm.then_inc(s_q[u], 1)
                    for m in range(DB):
                        mm = product_T(e, pB[u][:, m, 0:C], K["Wk"], m, msT[u], DB)
                    mm.then_inc(s_k[u], 1)
                for u in lanes:
                    e.wait_ge(s_qc[u], i + 1)
                    for m in range(DB):
                        mm = product_T(e, pA[u][:, m, 0:C], K["Wv"], m, msT[u], DB)
                    mm.then_inc(s_v[u], 1)
                for u in lanes:
                    e.wait_ge(s_pr[u], i + 1)
                    for m in range(DB):
                        mm = e.matmul(pB[u][0:4, 0, 0:C], K["sum0"][:, m, :], prod[u][:, m, :], start=m == 0,
                                      stop=m == DB - 1)
                    mm.then_inc(s_al[u], 1)
                    e.wait_ge(s_vc[u], i + 1)

        @block.scalar
        def _(e):
            with e.Fori(0, pairs) as i:
                for u in lanes:
                    e.wait_ge(s_T[u], i + 1)
                    e.activation(msT[u][:], pA[u][:, :, 0:C], ACT.Copy)
                    e.activation(owT[u][:], pB[u][:, :, 0:C], ACT.Copy).then_inc(s_Tc[u], 1)
                for u in lanes:
                    e.wait_ge(s_q[u], i + 1)
                    for m in range(DB):
                        a = e.activation(qT[u][:, m, :], pA[u][:, m, 0:C], ACT.Identity, bias=K["bq"][:, m:m + 1])
                    a.then_inc(s_qc[u], 1)
                for u in lanes:
                    e.wait_ge(s_v[u], i + 1)
                    e.wait_ge(s_st[u], i * 16 + 1)
                    for m in range(DB):
                        a = e.activation(vT[u][:, m, :], pA[u][:, m, 0:C], ACT.Identity, bias=K["bv"][:, m:m + 1])
                    a.then_inc(s_vc[u], 1)

        @block.vector
        def _(e):
            with e.Fori(0, pairs) as i:
                for u in lanes:
                    wait(e, s_qc[u], i + 1)
                    e.wait_ge(s_k[u], i + 1)
                    for m in range(DB):
                        v = e.scalar_tensor_tensor(out=prod[u][:, m, :], in0=pB[u][:, m, 0:C],
                                                   scalar=K["bk"][:, m:m + 1], in1=qT[u][:, m, :],
                                                   op0=ALU.add, op1=ALU.mult)
                    v.then_inc(s_pr[u], 1)
                for u in lanes:
                    wait(e, s_al[u], i + 1)
                    e.tensor_scalar(alpha[0:4, bass.ds((i * LANES + u) * C, C)], pB[u][0:4, 0, 0:C], 0.125, None,
                                    ALU.mult).then_inc(s_alc[u], 1)


def scores1(nc, K, A, S, alpha, adst):
    with ExitStack() as ctx:
        sb, ps, sem, _, _ = lane_scopes(nc, ctx, "sc1")
        ms, ow, ea = sb("ms", [R, J, D]), sb("ow", [R, J, D]), sb("ea", [R, J, 64])
        idxm, idxe = sb("idxm", [R, J], U32), sb("idxe", [R, J], U32)
        msT, owT, vT = (sb(n, [P, DB, C]) for n in ("msT", "owT", "vT"))
        eaT = sb("eaT", [64, C])
        pA, pB = ps("pA", [P, DB, 512]), ps("pB", [P, DB, 512])
        s_im, s_ie, s_rm, s_re, s_lin, s_T, s_Tc, s_To, s_Toc, s_al, s_v, s_vc, s_alc, s_st = (
            sem(n) for n in ("s_im", "s_ie", "s_rm", "s_re", "s_lin", "s_T", "s_Tc", "s_To", "s_Toc", "s_al",
                             "s_v", "s_vc", "s_alc", "s_st"))
        block = ctx.enter_context(nc.Block())
        pairs = K["E"] // C // LANES
        lanes = range(LANES)

        @block.sync
        def _(e):
            def load(i):
                for u in lanes:
                    before(e, s_To[u], i)
                    e.dma_start(ow[u][:], rows_of(S["X1"], i * LANES + u)).then_inc(s_lin[u], 16)

            def store(i):
                for u in lanes:
                    wait(e, s_vc[u], i + 1)
                    e.dma_start(value_chunk(S, i * LANES + u), vT[u][:]).then_inc(s_st[u], 16)
            pipeline(e, pairs, ((0, True),), lambda base, msg: (load, store, nothing))
            for u in lanes:
                e.wait_ge(s_st[u], 16 * pairs + 1)

        @block.gpsimd
        def _(e):
            for u in lanes:
                e.sem_inc(s_st[u], 1)

            def load(i):
                for u in lanes:
                    before(e, s_T[u], i)
                    n = i * LANES + u
                    gather(e, S["X1"], K["m1s"], idxm[u], ms[u], n, s_im[u], i + 1, s_rm[u])
                    gather(e, A["edge_attr_64"], K["ordU"], idxe[u], ea[u], n, s_ie[u], i + 1, s_re[u])
            pipeline(e, pairs, ((0, True),), lambda base, msg: (load, nothing, nothing))

        @block.tensor
        def _(e):
            for u in lanes:
                e.sem_inc(s_alc[u], 1)
            with e.Fori(0, pairs) as i:
                for u in lanes:
                    e.wait_ge(s_rm[u], i * (16 * J) + 16 * J)
                    e.wait_ge(s_re[u], i * (16 * J) + 16 * J)
                    e.wait_ge(s_alc[u], i + 1)
                    transposes(e, K, pA[u], ms[u], DB)
                    transposes(e, K, pB[u], ea[u], 1, 64).then_inc(s_T[u], 1)
                for u in lanes:
                    e.wait_ge(s_lin[u], i * 16 + 16)
                    e.wait_ge(s_Tc[u], i + 1)
                    transposes(e, K, pB[u], ow[u], DB).then_inc(s_To[u], 1)
                    for m in range(DB):
                        mm = product_T(e, pA[u][:, m, 0:C], K["W"], m, msT[u], DB)
                    mm.then_inc(s_v[u], 1)
                for u in lanes:
                    e.wait_ge(s_Toc[u], i + 1)
                    for k in range(DB):
                        e.matmul(pB[u][0:8, 0, 0:C], K["WAs"][:, k, :], msT[u][:, k, :], start=k == 0, stop=False)
                    e.matmul(pB[u][0:8, 0, 0:C], K["WAe"][:, :], eaT[u][:, :], start=False, stop=True)
                    for k in range(DB):
                        mm = e.matmul(pB[u][0:8, 1, 0:C], K["WAd"][:, k, :], owT[u][:, k, :], start=k == 0,
                                      stop=k == DB - 1)
                    mm.then_inc(s_al[u], 1)
                    e.wait_ge(s_vc[u], i + 1)

        @block.scalar
        def _(e):
            with e.Fori(0, pairs) as i:
                for u in lanes:
                    e.wait_ge(s_T[u], i + 1)
                    e.activation(msT[u][:], pA[u][:, :, 0:C], ACT.Copy)
                    e.activation(eaT[u][:], pB[u][0:64, 0, 0:C], ACT.Copy).then_inc(s_Tc[u], 1)
                for u in lanes:
                    e.wait_ge(s_To[u], i + 1)
                    e.activation(owT[u][:], pB[u][:, :, 0:C], ACT.Copy).then_inc(s_Toc[u], 1)
                for u in lanes:
                    e.wait_ge(s_v[u], i + 1)
                    e.wait_ge(s_st[u], i * 16 + 1)
                    e.activation(vT[u][:], pA[u][:, :, 0:C], ACT.Copy).then_inc(s_vc[u], 1)

        @block.vector
        def _(e):
            with e.Fori(0, pairs) as i:
                for u in lanes:
                    wait(e, s_al[u], i + 1)
                    here = bass.ds((i * LANES + u) * C, C)
                    e.tensor_copy(alpha[0:8, here], pB[u][0:8, 0, 0:C])
                    e.tensor_copy(adst[0:8, here], pB[u][0:8, 1, 0:C]).then_inc(s_alc[u], 1)


def softmax(nc, K, name, H, seg, alpha, adst):
    E = K["E"]
    with ExitStack() as ctx:
        sb, ps, sem = scopes(nc, ctx, name)
        far, m = sb("far", [8, E + 1]), sb("m", [8, E])
        s_sub, s_exp = sem("s_sub"), sem("s_exp")
        block = ctx.enter_context(nc.Block())
        al, fr, mm, sg = alpha[0:H, :], far[0:H, :], m[0:H, :], seg[0:H, :]

        def last_of_segment(e):
            e.tensor_tensor_scan(mm[:, ::-1], fr[:, E:0:-1], mm[:, ::-1], 0.0 - BIG, ALU.add, ALU.max)

        @block.vector
        def _(e):
            e.tensor_scalar(fr, sg, 1.0, BIG, ALU.subtract, ALU.mult)
            if adst is not None:
                ad = adst[0:H, :]
                e.tensor_tensor(mm, sg[:, 1:E + 1], ad, ALU.mult)
                e.drain()
                e.tensor_tensor(mm, ad, mm, ALU.subtract)
                e.drain()
                e.tensor_tensor_scan(ad[:, ::-1], sg[:, E:0:-1], mm[:, ::-1], 0.0, ALU.mult, ALU.add)
                e.drain()
                e.tensor_tensor(al, al, ad, ALU.add)
                e.drain()
                e.scalar_tensor_tensor(out=al, in0=al, scalar=0.2, in1=al, op0=ALU.mult, op1=ALU.max)
            e.drain()
            e.tensor_tensor_scan(mm, fr[:, 0:E], al, 0.0 - BIG, ALU.add, ALU.max)
            e.drain()
            last_of_segment(e)
            e.drain()
            e.tensor_tensor(al, al, mm, ALU.subtract).then_inc(s_sub, 1)
            e.wait_ge(s_exp, 1)
            e.tensor_tensor_scan(mm, sg[:, 0:E], al, 0.0, ALU.mult, ALU.add)
            e.drain()
            last_of_segment(e)
            e.drain()
            e.tensor_scalar(mm, mm, 1e-16, None, ALU.add)
            e.drain()
            e.reciprocal(mm, mm)
            e.drain()
            e.tensor_tensor(al, al, mm, ALU.mult)

        @block.scalar
        def _(e):
            e.wait_ge(s_sub, 1)
            e.activation(al, al, ACT.Exp).then_inc(s_exp, 1)


def layer0_rows(nc, K, A, S, seg, attn):
    with ExitStack() as ctx:
        sb, ps, sem, sb1, sem1 = lane_scopes(nc, ctx, "l0")
        ow, xb, y, v, x1 = (sb(n, [R, J, D]) for n in ("ow", "xb", "y", "v", "x1"))
        idxb = sb("idxb", [R, J], U32)
        owT, vT, agg = (sb(n, [P, DB, C]) for n in ("owT", "vT", "agg"))
        carry = sb1("carry", [P, DB])
        pT, pE = ps("pT", [P, DB, 512]), ps("pE", [P, DB, 512])
        pR = [p[:, :, :].rearrange("p a (b d) -> p (a b) d", d=D) for p in pE]
        L = [ln_buffers(lambda n, s, u=u: sb1(f"{n}{u}", s), lambda n, u=u: sem1(f"{n}{u}"), "l0")
             for u in range(LANES)]
        s_idx, s_row, s_lin, s_T, s_Tc, s_ex, s_ag, s_r, s_u, s_g, s_xb, s_t, s_x1, s_st = (
            sem(n) for n in ("s_idx", "s_row", "s_lin", "s_T", "s_Tc", "s_ex", "s_ag", "s_r", "s_u",
                             "s_g", "s_xb", "s_t", "s_x1", "s_st"))
        block = ctx.enter_context(nc.Block())
        pairs = K["E"] // C // LANES
        lanes = range(LANES)
        parts = ((0, True), (pairs, False))

        @block.sync
        def _(e):
            def store(i):
                for u in lanes:
                    wait(e, s_x1[u], i + 1)
                    e.dma_start(rows_of(S["X1"], i * LANES + u), x1[u][:]).then_inc(s_st[u], 16)

            def load(i):
                for u in lanes:
                    before(e, s_ag[u], i)
                    e.dma_start(vT[u][:], value_chunk(S, i * LANES + u)).then_inc(s_lin[u], 16)
            def part(base, msg):
                return load if msg else nothing, store, nothing
            pipeline(e, pairs, parts, part)
            for u in lanes:
                e.wait_ge(s_st[u], 32 * pairs + 1)

        @block.gpsimd
        def _(e):
            for u in lanes:
                e.sem_inc(s_st[u], 1)
            def part(base, msg):
                def load(i):
                    for u in lanes:
                        before(e, s_T[u], i)
                        before(e, s_xb[u], i)
                        gather(e, A["x"], K["dstU"][0] if msg else K["srcU"][1], idxb[u], ow[u],
                               (i - base) * LANES + u, s_idx[u], i + 1, s_row[u])

                def head(i):
                    for u in lanes:
                        wait(e, s_row[u], i * (16 * J) + 16 * J)
                        e.tensor_tensor(xb[u][:], ow[u][:], wide(K["beta0"][:, :]), ALU.add).then_inc(s_xb[u], 1)

                def rest(i):
                    for half in (1, 2):
                        for u in lanes:
                            ln_pool(e, K, L[u], 2 * i + half)
                return load, rest, head
            pipeline(e, pairs, parts, part)

        @block.tensor
        def _(e):
            for base, msg in parts:
                with e.Fori(base, base + pairs) as i:
                    for u in lanes:
                        wait(e, s_u[u], i + 1)
                        if msg:
                            for m in range(DB):
                                mm = e.matmul(pE[u][:, m, 0:C], K["rep0"][:, m * P:(m + 1) * P],
                                              attn[0:4, bass.ds((i * LANES + u) * C, C)], start=True, stop=True)
                            mm.then_inc(s_ex[u], 1)
                        e.wait_ge(s_row[u], i * (16 * J) + 16 * J)
                        transposes(e, K, pT[u], ow[u], DB).then_inc(s_T[u], 1)
                    for u in lanes:
                        if msg:
                            e.wait_ge(s_ag[u], i + 1)
                        e.wait_ge(s_Tc[u], i + 1)
                        product_rows(e, pR[u], K["Wskip"], owT[u], DB, agg[u] if msg else None, K["ident"])\
                            .then_inc(s_r[u], 1)

        @block.scalar
        def _(e):
            with e.Fori(0, 2 * pairs) as i:
                for u in lanes:
                    e.wait_ge(s_T[u], i + 1)
                    e.activation(owT[u][:], pT[u][:, :, 0:C], ACT.Copy).then_inc(s_Tc[u], 1)
                for u in lanes:
                    e.wait_ge(s_u[u], i + 2)
                    e.activation(v[u][:], y[u][:], ACT.Gelu).then_inc(s_g[u], 1)

        @block.vector
        def _(e):
            e.memset(carry[:], 0.0)
            for u in lanes:
                e.sem_inc(s_u[u], 1)
            for base, msg in parts:
                def sums(i):
                    e.drain()
                    for u in lanes:
                        wait(e, s_ex[u], i + 1)
                        e.wait_ge(s_lin[u], i * 16 + 16)
                        e.tensor_tensor(vT[u][:], vT[u][:], pE[u][:, :, 0:C], ALU.mult)
                        e.drain()
                        edge_scan(e, seg, i * LANES + u, vT[u], agg[u], carry, DB).then_inc(s_ag[u], 1)
                        e.drain()

                def rest(i, ahead):
                    e.drain()
                    for u in lanes:
                        e.wait_ge(s_r[u], i + 1)
                        e.tensor_tensor(y[u][:], pR[u][0:R, :, :], wide(K["bskip"][:, :]), ALU.add)\
                            .then_inc(s_u[u], 1)
                    for u in lanes:
                        e.wait_ge(s_g[u], i + 1)
                        ln_stats(e, L[u], 2 * i + 1, v[u])
                    ahead()
                    for u in lanes:
                        wait(e, s_xb[u], i + 1)
                        ln_affine(e, L[u], 2 * i + 1, v[u], K["gamma0"], xb[u], y[u]).then_inc(s_t[u], 1)
                    for u in lanes:
                        e.wait_ge(s_t[u], i + 1)
                        ln_stats(e, L[u], 2 * i + 2, y[u])
                    for u in lanes:
                        wait(e, s_st[u], i * 16 + 1)
                        ln_scale(e, L[u], 2 * i + 2, y[u], x1[u]).then_inc(s_x1[u], 1)
                with_next(e, base, pairs, msg, sums, rest)


def layer1_rows(nc, K, A, S, seg, attn):
    with ExitStack() as ctx:
        sb, ps, sem, sb1, sem1 = lane_scopes(nc, ctx, "l1")
        x1, xb, y, v, x2, h = (sb(n, [R, J, D]) for n in ("x1", "xb", "y", "v", "x2", "h"))
        b_in = sb1("b_in", [R, D])
        x2T, vT, agg = (sb(n, [P, DB, C]) for n in ("x2T", "vT", "agg"))
        carry = sb1("carry", [P, DB])
        pT = ps("pT", [P, DB, 512])
        pA = [p[:, :, :].rearrange("p a (b d) -> p (a b) d", d=D) for p in pT]
        pR = ps("pR", [P, J, D])
        L = [ln_buffers(lambda n, s, u=u: sb1(f"{n}{u}", s), lambda n, u=u: sem1(f"{n}{u}"), "l1")
             for u in range(LANES)]
        s_b = sem1("s_b")
        s_lin, s_v, s_ex, s_ag, s_r, s_y, s_xb, s_ya, s_t, s_x2, s_T, s_Tc, s_h, s_hc, s_st, s_sth = (
            sem(n) for n in ("s_lin", "s_v", "s_ex", "s_ag", "s_r", "s_y", "s_xb", "s_ya", "s_t", "s_x2",
                             "s_T", "s_Tc", "s_h", "s_hc", "s_st", "s_sth"))
        block = ctx.enter_context(nc.Block())
        pairs = K["E"] // C // LANES
        lanes = range(LANES)

        @block.sync
        def _(e):
            e.dma_start(b_in[:], A["L2_gnn_b_in"].unsqueeze(0).broadcast_to([R, D])).then_inc(s_b, 16)

            def load(i, msg):
                for u in lanes:
                    before(e, s_xb[u], i)
                    e.dma_start(x1[u][:], rows_of(S["X1"], i * LANES + u)).then_inc(s_lin[u], 16)
                    if msg:
                        before(e, s_ag[u], i)
                        e.dma_start(vT[u][:], value_chunk(S, i * LANES + u)).then_inc(s_v[u], 16)

            def store(i):
                for u in lanes:
                    wait(e, s_x2[u], i + 1)
                    e.dma_start(rows_of(S["X2"], i * LANES + u), x2[u][:]).then_inc(s_st[u], 16)
                for u in lanes:
                    wait(e, s_hc[u], i + 2)
                    e.dma_start(rows_of(S["H"][0], i * LANES + u), h[u][:]).then_inc(s_sth[u], 16)
            load(0, True)
            for first, count, msg in ((0, pairs - 1, True), (pairs - 1, 1, False), (pairs, pairs - 1, False)):
                with e.Fori(first, first + count) as i:
                    load(i + 1, msg)
                    store(i)
            store(2 * pairs - 1)
            for u in lanes:
                e.wait_ge(s_st[u], 32 * pairs + 1)
                e.wait_ge(s_sth[u], 32 * pairs + 1)

        @block.gpsimd
        def _(e):
            for u in lanes:
                e.sem_inc(s_st[u], 1)
                e.sem_inc(s_sth[u], 1)

            def with_bias(i):
                for u in lanes:
                    before(e, s_t[u], i)
                    wait(e, s_lin[u], i * 16 + 16)
                    e.tensor_tensor(y[u][:], x1[u][:], wide(K["bias1"][:, :]), ALU.add).then_inc(s_y[u], 1)

            def with_beta(i):
                for u in lanes:
                    e.tensor_tensor(xb[u][:], x1[u][:], wide(K["beta1"][:, :]), ALU.add).then_inc(s_xb[u], 1)

            def pair(i, more):
                for u in lanes:
                    ln_pool(e, K, L[u], 2 * i + 1)
                if more:
                    with_bias(i + 1)
                for u in lanes:
                    ln_pool(e, K, L[u], 2 * i + 2)
                if more:
                    with_beta(i + 1)
            with_bias(0)
            with_beta(0)
            with e.Fori(0, 2 * pairs - 1) as i:
                pair(i, True)
            pair(2 * pairs - 1, False)

        @block.tensor
        def _(e):
            def expand(i):
                for u in lanes:
                    before(e, s_Tc[u], i)
                    for m in range(DB):
                        mm = e.matmul(pT[u][:, m, 0:C], K["rep1"][:, m * P:(m + 1) * P],
                                      attn[0:8, bass.ds((i * LANES + u) * C, C)], start=True, stop=True)
                    mm.then_inc(s_ex[u], 1)

            def turn_sums(i, u):
                wait(e, s_ag[u], i + 1)
                agg_rows(e, pA[u], agg[u], K["ident"]).then_inc(s_r[u], 1)

            def pair(i, more):
                for u in lanes:
                    e.wait_ge(s_x2[u], i + 1)
                    transposes(e, K, pT[u], x2[u], DB).then_inc(s_T[u], 1)
                if more:
                    expand(i + 1)
                for u in lanes:
                    wait(e, s_hc[u], i + 1)
                    e.wait_ge(s_Tc[u], i + 1)
                    product_rows(e, pR[u], K["W_in"], x2T[u], DB).then_inc(s_h[u], 1)
                    if more:
                        turn_sums(i + 1, u)
            expand(0)
            for u in lanes:
                turn_sums(0, u)
            with e.Fori(0, pairs - 1) as i:
                pair(i, True)
            with e.Fori(pairs - 1, 2 * pairs) as i:
                pair(i, False)

        @block.scalar
        def _(e):
            with e.Fori(0, 2 * pairs) as i:
                for u in lanes:
                    e.wait_ge(s_T[u], i + 1)
                    e.activation(x2T[u][:], pT[u][:, :, 0:C], ACT.Copy).then_inc(s_Tc[u], 1)

        @block.vector
        def _(e):
            e.memset(carry[:], 0.0)
            for u in lanes:
                e.sem_inc(s_hc[u], 1)
            e.wait_ge(s_b, 16)

            def hidden(i):
                for u in lanes:
                    wait(e, s_sth[u], i * 16 + 1)
                    e.wait_ge(s_h[u], i + 1)
                    e.tensor_tensor(h[u][:], pR[u][0:R, :, :], wide(b_in[:, :]), ALU.add).then_inc(s_hc[u], 1)

            for base, count, msg in ((0, 1, True), (1, pairs - 1, True), (pairs, 1, False),
                                     (pairs + 1, pairs - 1, False)):
                with e.Fori(base, base + count) as i:
                    e.drain()
                    if msg:
                        for u in lanes:
                            wait(e, s_ex[u], i + 1)
                            e.wait_ge(s_v[u], i * 16 + 16)
                            e.tensor_tensor(vT[u][:], vT[u][:], pT[u][:, :, 0:C], ALU.mult)
                            e.drain()
                            edge_scan(e, seg, i * LANES + u, vT[u], agg[u], carry, DB).then_inc(s_ag[u], 1)
                            e.drain()
                        for u in lanes:
                            wait(e, s_r[u], i + 1)
                            e.wait_ge(s_y[u], i + 1)
                            e.tensor_tensor(y[u][:], y[u][:], pA[u][0:R, :, :], ALU.add)
                        e.drain()
                    for u in lanes:
                        wait(e, s_y[u], i + 1)
                        ln_stats(e, L[u], 2 * i + 1, y[u])
                    if count > 1:
                        hidden(i - 1)
                    for u in lanes:
                        wait(e, s_xb[u], i + 1)
                        ln_affine(e, L[u], 2 * i + 1, y[u], K["gamma1"], xb[u], v[u]).then_inc(s_t[u], 1)
                    for u in lanes:
                        e.wait_ge(s_t[u], i + 1)
                        ln_stats(e, L[u], 2 * i + 2, v[u])
                    for u in lanes:
                        wait(e, s_st[u], i * 16 + 1)
                        ln_scale(e, L[u], 2 * i + 2, v[u], x2[u]).then_inc(s_x2[u], 1)
                if count > 1:
                    hidden(base + count - 1)


def layer2_rows(nc, K, A, S, seg, l):
    tail = l == 2
    with ExitStack() as ctx:
        sb, ps, sem, sb1, sem1 = lane_scopes(nc, ctx, f"l2{l}")
        ow, ms, h, x2, y, x3 = (sb(n, [R, J, D]) for n in ("ow", "ms", "h", "x2", "y", "x3"))
        bias = sb1("bias", [R, D])
        idxm, idxo = sb("idxm", [R, J], U32), sb("idxo", [R, J], U32)
        owT, agg, hT = (sb(n, [P, DB, C]) for n in ("owT", "agg", "hT"))
        carry = sb1("carry", [P, DB])
        pT, pM = ps("pT", [P, DB, 512]), ps("pM", [P, DB, 512])
        pR = [p[:, :, :].rearrange("p a (b d) -> p (a b) d", d=D) for p in pM]
        L = [ln_buffers(lambda n, s, u=u: sb1(f"{n}{u}", s), lambda n, u=u: sem1(f"{n}{u}"), "l2")
             for u in range(LANES)]
        s_b = sem1("s_b")
        s_im, s_io, s_own, s_ownG, s_x2, s_x2G, s_msg, s_w, s_T, s_M, s_Tc, s_ag, s_r = (
            sem(n) for n in ("s_im", "s_io", "s_own", "s_ownG", "s_x2", "s_x2G", "s_msg", "s_w", "s_T", "s_M",
                             "s_Tc", "s_ag", "s_r"))
        s_b1, s_h, s_hTc, s_o, s_ob, s_x3, s_st = (
            sem(n) for n in ("s_b1", "s_h", "s_hTc", "s_o", "s_ob", "s_x3", "s_st"))
        block = ctx.enter_context(nc.Block())
        pairs = K["E"] // C // LANES
        lanes = range(LANES)
        parts = ((0, False), (pairs, True))
        Wself, Wagg = K[f"Wself{l}"], K[f"Wagg{l}"]
        s_free = s_ob if tail else s_b1
        s_x2b = sem("s_x2b")

        def there(e, i, gathered, s_line, s_gather):
            if gathered:
                wait(e, s_gather, (i - pairs) * (16 * J) + 16 * J)
            else:
                wait(e, s_line, i * 16 + 16)

        @block.sync
        def _(e):
            e.dma_start(bias[:], A["L2_gnn_b_hid"][l].unsqueeze(0).broadcast_to([R, D])).then_inc(s_b, 16)
            def part(base, msg):
                def load(i):
                    for u in lanes:
                        n = i * LANES + u
                        if not (msg and l == 0):
                            before(e, s_T[u], i)
                            e.dma_start(ow[u][:], rows_of(S["H"][l], n)).then_inc(s_own[u], 16)
                        if tail and not msg:
                            wait(e, s_ob[u], i + 1)
                            e.dma_start(x2[u][:], rows_of(S["X2"], n)).then_inc(s_x2[u], 16)

                def store(i):
                    for u in lanes:
                        n = i * LANES + u
                        if tail:
                            wait(e, s_x3[u], i + 1)
                            e.dma_start(rows_of(S["X3"], n), x3[u][:]).then_inc(s_st[u], 16)
                        else:
                            wait(e, s_h[u], i + 1)
                            e.dma_start(rows_of(S["H"][l + 1], n), h[u][:]).then_inc(s_st[u], 16)
                return load, store, nothing
            pipeline(e, pairs, parts, part)
            for u in lanes:
                e.wait_ge(s_st[u], 32 * pairs + 1)

        @block.gpsimd
        def _(e):
            for u in lanes:
                e.sem_inc(s_st[u], 1)
            def part(base, msg):
                def load(i):
                    for u in lanes:
                        if not msg:
                            continue
                        n = (i - base) * LANES + u
                        before(e, s_M[u], i - base)
                        gather(e, S["H"][l], K["m1d"] if l == 0 else K["m2d"], idxm[u], ms[u], n, s_im[u],
                               i - base + 1, s_msg[u])
                        if l == 0:
                            before(e, s_T[u], i)
                            gather(e, S["H"][l], K["ownB"], idxo[u], ow[u], n, s_io[u], i - base + 1, s_ownG[u])
                        if tail:
                            wait(e, s_ob[u], i + 1)
                            gather(e, S["X2"], K["ownB"], idxo[u], x2[u], n, s_io[u], i - base + 1, s_x2G[u])

                def head(i):
                    if tail:
                        for u in lanes:
                            there(e, i, msg, s_x2[u], s_x2G[u])
                            e.tensor_tensor(x2[u][:], x2[u][:], wide(K["b_out"][:, :]), ALU.add)\
                                .then_inc(s_x2b[u], 1)

                def rest(i):
                    if tail:
                        for u in lanes:
                            ln_pool(e, K, L[u], i + 1)
                return load, rest, head
            pipeline(e, pairs, parts, part)

        @block.tensor
        def _(e):
            for base, msg in parts:
                with e.Fori(base, base + pairs) as i:
                    for u in lanes:
                        there(e, i, msg and l == 0, s_own[u], s_ownG[u])
                        transposes(e, K, pT[u], ow[u], DB).then_inc(s_T[u], 1)
                    if msg:
                        for u in lanes:
                            wait(e, s_w[u], i - base + 1)
                            wait(e, s_free[u], i + 1)
                            transposes(e, K, pM[u], ms[u], DB).then_inc(s_M[u], 1)
                    for u in lanes:
                        if msg:
                            wait(e, s_ag[u], i - base + 1)
                        else:
                            wait(e, s_free[u], i + 1)
                        e.wait_ge(s_Tc[u], i + 1)
                        if tail:
                            for m in range(DB):
                                mm = product_T(e, pM[u][:, m, 0:C], Wself, m, owT[u], DB, last=not msg)
                                if msg:
                                    mm = product_T(e, pM[u][:, m, 0:C], Wagg, m, agg[u], DB, first=False)
                            mm.then_inc(s_r[u], 1)
                            continue
                        terms = [(owT[u], Wself)] + ([(agg[u], Wagg)] if msg else [])
                        for j in range(J):
                            for a, (xT, w) in enumerate(terms):
                                for k in range(DB):
                                    mm = e.matmul(pR[u][0:R, j, :], xT[:, k, j * R:(j + 1) * R], w[:, k, :],
                                                  start=a == 0 and k == 0,
                                                  stop=a == len(terms) - 1 and k == DB - 1)
                        mm.then_inc(s_r[u], 1)
                    if tail:
                        for u in lanes:
                            e.wait_ge(s_hTc[u], i + 1)
                            product_rows(e, pR[u], K["W_out"], hT[u], DB).then_inc(s_o[u], 1)

        @block.scalar
        def _(e):
            with e.Fori(0, 2 * pairs) as i:
                for u in lanes:
                    e.wait_ge(s_T[u], i + 1)
                    e.activation(owT[u][:], pT[u][:, :, 0:C], ACT.Copy).then_inc(s_Tc[u], 1)
                for u in lanes:
                    if tail:
                        e.wait_ge(s_r[u], i + 1)
                        for m in range(DB):
                            a = e.activation(hT[u][:, m, :], pM[u][:, m, 0:C], ACT.Relu,
                                             bias=K["b_hid2"][:, m:m + 1])
                        a.then_inc(s_hTc[u], 1)
                    else:
                        e.wait_ge(s_st[u], i * 16 + 1)
                        e.wait_ge(s_b1[u], i + 2)
                        e.activation(h[u][:], y[u][:], ACT.Relu).then_inc(s_h[u], 1)

        @block.vector
        def _(e):
            e.memset(carry[:], 0.0)
            for u in lanes:
                e.sem_inc(s_b1[u], 1)
                e.sem_inc(s_ob[u], 1)
            e.wait_ge(s_b, 16)
            for base, msg in parts:
                def sums(i):
                    e.drain()
                    for u in lanes:
                        wait(e, s_msg[u], (i - base) * (16 * J) + 16 * J)
                        times_columns(e, ms[u], K["inv2"], (i - base) * LANES + u, D).then_inc(s_w[u], 1)
                    for u in lanes:
                        wait(e, s_M[u], i - base + 1)
                        edge_scan(e, seg, (i - base) * LANES + u, pM[u], agg[u], carry, DB)\
                            .then_inc(s_ag[u], 1)
                        e.drain()

                def rest(i, ahead):
                    e.drain()
                    if not tail:
                        for u in lanes:
                            wait(e, s_r[u], i + 1)
                            e.tensor_tensor(y[u][:], pR[u][0:R, :, :], wide(bias[:, :]), ALU.add)\
                                .then_inc(s_b1[u], 1)
                    if tail:
                        for u in lanes:
                            wait(e, s_x2b[u], i + 1)
                            wait(e, s_o[u], i + 1)
                            e.tensor_tensor(y[u][:], pR[u][0:R, :, :], x2[u][:], ALU.add).then_inc(s_ob[u], 1)
                        for u in lanes:
                            wait(e, s_ob[u], i + 2)
                            ln_stats(e, L[u], i + 1, y[u])
                        ahead()
                        for u in lanes:
                            wait(e, s_st[u], i * 16 + 1)
                            ln_scale(e, L[u], i + 1, y[u], x3[u]).then_inc(s_x3[u], 1)
                    else:
                        for u in lanes:
                            wait(e, s_h[u], i + 1)
                        ahead()
                with_next(e, base, pairs, msg, sums, rest)


def layer3_rows(nc, K, A, S, seg, l):
    with ExitStack() as ctx:
        sb, ps, sem, sb1, sem1 = lane_scopes(nc, ctx, f"l3{l}")
        w_in = [D, 2 * D, D][l]
        w_out = [2 * D, 2 * D, D][l]
        nb = w_in // P
        ow, ms = sb("ow", [R, J, w_in]), sb("ms", [R, J, w_in])
        y = sb("y", [R, J, w_out]) if l != 1 else None
        z = sb("z", [R, J, D]) if l else None
        x3 = sb("x3", [R, J, D]) if l == 2 else None
        bias = sb1("bias", [R, w_out])
        idxm, idxo, idxr = (sb(n, [R, J], U32) for n in ("idxm", "idxo", "idxr"))
        agg, tT = sb("agg", [P, nb, C]), sb("tT", [P, nb, C])
        gT = sb("gT", [P, 2 * DB, C]) if l == 1 else None
        carry = sb1("carry", [P, nb])
        pQ = ps("pQ", [P, 4, 512])
        pZ = [p[:, 2:4, :].rearrange("p a (b d) -> p (a b) d", d=D) for p in pQ]
        L = [ln_buffers(lambda n, s, u=u: sb1(f"{n}{u}", s), lambda n, u=u: sem1(f"{n}{u}"), "l3")
             for u in range(LANES)]
        s_b = sem1("s_b")
        s_im, s_io, s_ir, s_own, s_ownG, s_x3, s_x3G, s_msg, s_wo, s_wm, s_M, s_To, s_ag, s_tT = (
            sem(n) for n in ("s_im", "s_io", "s_ir", "s_own", "s_ownG", "s_x3", "s_x3G", "s_msg", "s_wo",
                             "s_wm", "s_M", "s_To", "s_ag", "s_tT"))
        s_r, s_b1, s_g, s_gT, s_z, s_zc, s_xa, s_st, s_sc, s_out = (
            sem(n) for n in ("s_r", "s_b1", "s_g", "s_gT", "s_z", "s_zc", "s_xa", "s_st", "s_sc",
                             "s_out"))
        block = ctx.enter_context(nc.Block())
        pairs = K["E"] // C // LANES
        lanes = range(LANES)
        parts = ((0, True), (pairs, False))
        src = [S["X3"], S["G"], S["Z"]][l]
        vec = [A["L3_gnn_b1"], A["L3_gnn_b2"], A["L3_gnn_b3"]][l]
        G = 16 * J
        s_free = s_zc if l == 1 else s_b1

        def there(e, i, gathered, s_line, s_gather, skipped):
            if gathered:
                wait(e, s_gather, i * G + G)
            else:
                wait(e, s_line, (i - skipped) * 16 + 16)

        def own_there(e, i, u, msg):
            there(e, i, l == 0 and msg, s_own[u], s_ownG[u], pairs if l == 0 else 0)

        @block.sync
        def _(e):
            e.dma_start(bias[:], vec.unsqueeze(0).broadcast_to([R, w_out])).then_inc(s_b, 16)
            def part(base, msg):
                def load(i):
                    for u in lanes:
                        n = i * LANES + u
                        if not (msg and l == 0):
                            if l == 2:
                                before(e, s_b1[u], i + 1)
                            else:
                                before(e, s_To[u], i)
                            e.dma_start(ow[u][:], rows_of(src, n)).then_inc(s_own[u], 16)
                        if l == 2 and not msg:
                            before(e, s_xa[u], i)
                            e.dma_start(x3[u][:], rows_of(S["X3"], n)).then_inc(s_x3[u], 16)

                def store(i):
                    for u in lanes:
                        n = i * LANES + u
                        if l == 0:
                            wait(e, s_g[u], i + 1)
                            e.dma_start(rows_of(S["G"], n), y[u][:]).then_inc(s_st[u], 16)
                        if l == 1:
                            wait(e, s_zc[u], i + 2)
                            e.dma_start(rows_of(S["Z"], n), z[u][:]).then_inc(s_st[u], 16)
                return load, store, nothing
            pipeline(e, pairs, parts, part)
            for u in lanes:
                if l < 2:
                    e.wait_ge(s_st[u], 32 * pairs + 1)
                else:
                    e.wait_ge(s_sc[u], 2 * pairs * G)

        @block.gpsimd
        def _(e):
            for u in lanes:
                e.sem_inc(s_st[u], 1)
            def part(base, msg):
                def load(i):
                    for u in lanes:
                        if not msg:
                            continue
                        n = i * LANES + u
                        before(e, s_M[u], i)
                        gather(e, src, K["m2s"] if l == 0 else K["m1s"], idxm[u], ms[u], n, s_im[u], i + 1,
                               s_msg[u])
                        if l == 0:
                            before(e, s_To[u], i)
                            gather(e, src, K["ownA"], idxo[u], ow[u], n, s_io[u], i + 1, s_ownG[u])
                        if l == 2:
                            before(e, s_xa[u], i)
                            gather(e, S["X3"], K["ownA"], idxo[u], x3[u], n, s_io[u], i + 1, s_x3G[u])

                def rest(i):
                    if l < 2:
                        return
                    for u in lanes:
                        col = K["outA"] if msg else K["outB"]
                        e.tensor_copy(idxr[u][:], col[:, bass.ds(((i - base) * LANES + u) * J, J)])\
                            .then_inc(s_ir[u], 1)
                        ln_pool(e, K, L[u], i + 1)
                    for u in lanes:
                        wait(e, s_ir[u], i + 1)
                        wait(e, s_out[u], i + 1)
                        for j in range(J):
                            e.indirect_dma_start(A["out"],
                                                 bass.IndirectOffsetOnAxis(ap=idxr[u][:, j:j + 1], axis=0),
                                                 z[u][:, j, :], None, bounds_check=K["N"] - 1, oob_is_err=False)\
                                .then_inc(s_sc[u], 16)
                    for u in lanes:
                        wait(e, s_sc[u], i * G + G)
                return load, rest, nothing
            pipeline(e, pairs, parts, part)

        @block.tensor
        def _(e):
            for base, msg in parts:
                with e.Fori(base, base + pairs) as i:
                    if msg:
                        for u in lanes:
                            wait(e, s_free[u], i + 1)
                            wait(e, s_wm[u], i + 1)
                            transposes(e, K, pQ[u], ms[u], nb).then_inc(s_M[u], 1)
                    if l == 2:
                        if msg:
                            for u in lanes:
                                wait(e, s_ag[u], i + 1)
                                agg_rows(e, pZ[u], agg[u], K["ident"]).then_inc(s_r[u], 1)
                    else:
                        for u in lanes:
                            if msg:
                                wait(e, s_ag[u], i + 1)
                                wait(e, s_wo[u], i + 1)
                            else:
                                wait(e, s_free[u], i + 1)
                                own_there(e, i, u, msg)
                            transposes(e, K, pQ[u], ow[u], nb).then_inc(s_To[u], 1)
                        w = K["W1"] if l == 0 else K["W2"]
                        for u in lanes:
                            e.wait_ge(s_tT[u], i + 1)
                            if l == 1:
                                for m in range(2 * DB):
                                    mm = product_T(e, pQ[u][:, m, 0:C], w, m, tT[u], nb)
                                mm.then_inc(s_r[u], 1)
                                continue
                            for j in range(J):
                                for k in range(nb):
                                    mm = e.matmul(pQ[u][0:R, j, :], tT[u][:, k, j * R:(j + 1) * R], w[:, k, :],
                                                  start=k == 0, stop=k == nb - 1)
                            mm.then_inc(s_r[u], 1)
                    if l == 1:
                        for u in lanes:
                            e.wait_ge(s_gT[u], i + 1)
                            product_rows(e, pZ[u], K["W3"], gT[u], 2 * DB).then_inc(s_z[u], 1)

        @block.scalar
        def _(e):
            with e.Fori(0, 2 * pairs) as i:
                for u in lanes:
                    if l == 1:
                        e.wait_ge(s_r[u], i + 1)
                        for m in range(2 * DB):
                            a = e.activation(gT[u][:, m, :], pQ[u][:, m, 0:C], ACT.Relu, bias=K["b2"][:, m:m + 1])
                        a.then_inc(s_gT[u], 1)
                    else:
                        e.wait_ge(s_b1[u], i + 2)
                        e.activation(y[u][:], y[u][:], ACT.Relu).then_inc(s_g[u], 1)

        @block.vector
        def _(e):
            e.memset(carry[:], 0.0)
            for u in lanes:
                e.sem_inc(s_b1[u], 1)
                e.sem_inc(s_zc[u], 1)
            e.wait_ge(s_b, 16)
            for base, msg in parts:
                def sums(i):
                    e.drain()
                    for u in lanes:
                        wait(e, s_msg[u], i * G + G)
                        times_columns(e, ms[u], K["norm3"], i * LANES + u, w_in).then_inc(s_wm[u], 1)
                        own_there(e, i, u, msg)
                        times_columns(e, ow[u], K["self3"], i * LANES + u, w_in).then_inc(s_wo[u], 1)
                    for u in lanes:
                        wait(e, s_M[u], i + 1)
                        edge_scan(e, seg, i * LANES + u, pQ[u], agg[u], carry, nb).then_inc(s_ag[u], 1)
                        e.drain()

                def rest(i, ahead):
                    e.drain()
                    if l < 2:
                        for u in lanes:
                            wait(e, s_To[u], i + 1)
                            if msg:
                                e.tensor_tensor(tT[u][:], pQ[u][:, 0:nb, 0:C], agg[u][:], ALU.add)\
                                    .then_inc(s_tT[u], 1)
                            else:
                                e.tensor_copy(tT[u][:], pQ[u][:, 0:nb, 0:C]).then_inc(s_tT[u], 1)
                        for u in lanes:
                            if l == 1:
                                continue
                            wait(e, s_st[u], i * 16 + 1)
                            wait(e, s_r[u], i + 1)
                            e.tensor_tensor(y[u][:], pQ[u][0:R, :, :],
                                            bias[:, :].unsqueeze(1).broadcast_to([R, J, w_out]), ALU.add)\
                                .then_inc(s_b1[u], 1)
                        if l == 1:
                            for u in lanes:
                                wait(e, s_st[u], i * 16 + 1)
                                wait(e, s_z[u], i + 1)
                                e.tensor_copy(z[u][:], pZ[u][0:R, :, :]).then_inc(s_zc[u], 1)
                        ahead()
                    else:
                        for u in lanes:
                            if msg:
                                wait(e, s_r[u], i + 1)
                                e.tensor_tensor(ow[u][:], ow[u][:], pZ[u][0:R, :, :], ALU.add)
                                e.drain()
                            else:
                                own_there(e, i, u, msg)
                            e.tensor_tensor(y[u][:], ow[u][:], wide(bias[:, :]), ALU.add).then_inc(s_b1[u], 1)
                        for u in lanes:
                            wait(e, s_g[u], i + 1)
                            there(e, i, msg, s_x3[u], s_x3G[u], pairs)
                            e.tensor_tensor(y[u][:], y[u][:], x3[u][:], ALU.add).then_inc(s_xa[u], 1)
                        for u in lanes:
                            wait(e, s_xa[u], i + 1)
                            ln_stats(e, L[u], i + 1, y[u])
                        ahead()
                        for u in lanes:
                            ln_scale(e, L[u], i + 1, y[u], z[u]).then_inc(s_out[u], 1)
                with_next(e, base, pairs, msg, sums, rest)


def build(nc, A):
    K = {}
    N, _ = A["x"].shape
    E = A["src"].shape[0]
    K["N"], K["E"] = N, E

    def scratch(name, shape, d=F32):
        return nc.dram_tensor(name, shape, d, kind="Internal").ap()
    S = dict(
        edges=[scratch(f"edges{i}", [E, 4], I32) for i in range(2)],
        seg=scratch("seg", [2, E + 1]), cnt=scratch("cnt", [2, E]),
        nodes=scratch("nodes", [2 * N, 2]),
        V=scratch("V", [E // C, P, DB, C]),
        X1=scratch("X1", [2 * E, D]), X2=scratch("X2", [2 * E, D]), X3=scratch("X3", [2 * E, D]),
        H=[scratch(f"H{i}", [2 * E, D]) for i in range(3)],
        G=scratch("G", [2 * E, 2 * D]), Z=scratch("Z", [2 * E, D]))
    with ExitStack() as ctx:
        K["sb"] = scopes(nc, ctx, "k")[0]
        for n in ("srcF", "dstF"):
            K[n] = [K["sb"](f"{n}{i}", [R, TILES]) for i in range(2)]
        for n in ("srcU", "dstU"):
            K[n] = [K["sb"](f"{n}{i}", [R, TILES], U32) for i in range(2)]
        for n in ("ordU", "m1s", "m2s", "m1d", "m2d", "ownA", "ownB", "outA", "outB"):
            K[n] = K["sb"](n, [R, TILES], U32)
        for n in ("inv2", "norm3", "self3"):
            K[n] = K["sb"](n, [R, TILES])
        K["WAs"], K["WAd"], K["WAe"] = K["sb"]("WAs", [P, DB, 8]), K["sb"]("WAd", [P, DB, 8]), K["sb"]("WAe", [64, 8])
        K["rep0"], K["rep1"], K["sum0"] = K["sb"]("rep0", [4, D]), K["sb"]("rep1", [8, D]), K["sb"]("sum0", [P, DB, 4])
        load_constants(nc, K, A)
        att_weights(nc, K, A)
        dense(nc, K, A, N, prepare(nc, K, A, S))
        with ExitStack() as c2:
            sb = scopes(nc, c2, "attn")[0]
            seg, alpha = sb("seg", [P, E + 1]), sb("alpha", [8, E])
            load_segments(nc, K, "seg_a", S, 0, seg)
            scores0(nc, K, A, S, alpha)
            softmax(nc, K, "sm0", 4, seg, alpha, None)
            layer0_rows(nc, K, A, S, seg, alpha)
            with ExitStack() as c3:
                adst = scopes(nc, c3, "attn1")[0]("adst", [8, E])
                scores1(nc, K, A, S, alpha, adst)
                softmax(nc, K, "sm1", 8, seg, alpha, adst)
            layer1_rows(nc, K, A, S, seg, alpha)
        with ExitStack() as c2:
            seg = scopes(nc, c2, "l2s")[0]("seg", [P, E + 1])
            load_segments(nc, K, "seg_b", S, 1, seg)
            for l in range(3):
                layer2_rows(nc, K, A, S, seg, l)
        with ExitStack() as c2:
            seg = scopes(nc, c2, "l3s")[0]("seg", [P, E + 1])
            load_segments(nc, K, "seg_c", S, 0, seg)
            for l in range(3):
                layer3_rows(nc, K, A, S, seg, l)


_INS = ['x', 'src', 'dst', 'edge_attr_64', 'L0_gnn_Wq', 'L0_gnn_bq', 'L0_gnn_Wk', 'L0_gnn_bk', 'L0_gnn_Wv',
        'L0_gnn_bv', 'L0_gnn_Wskip', 'L0_gnn_bskip', 'L0_gnn_gamma', 'L0_gnn_beta_ln', 'L1_gnn_W',
        'L1_gnn_W_e', 'L1_gnn_att_src', 'L1_gnn_att_dst', 'L1_gnn_att_edge', 'L1_gnn_bias', 'L1_gnn_gamma',
        'L1_gnn_beta', 'L2_gnn_W_in', 'L2_gnn_b_in', 'L2_gnn_W_agg', 'L2_gnn_W_self', 'L2_gnn_b_hid',
        'L2_gnn_W_out', 'L2_gnn_b_out', 'L3_gnn_W1', 'L3_gnn_b1', 'L3_gnn_W2', 'L3_gnn_b2', 'L3_gnn_W3',
        'L3_gnn_b3']


def kernel(**inputs):
    import numpy as _np
    import concourse.bacc as _bacc
    from concourse import mybir as _mybir
    from concourse.bass_utils import run_bass_kernel_spmd as _run

    nc = _bacc.Bacc("TRN2", target_bir_lowering=False, num_devices=1)
    arrays, args = {}, {}
    for name in _INS:
        a = _np.ascontiguousarray(inputs[name])
        arrays[f"in_{name}_dram"] = a
        args[name] = nc.dram_tensor(f"in_{name}_dram", a.shape, _mybir.dt.from_np(a.dtype), kind="ExternalInput").ap()
    out_shape = inputs['x'].shape
    args["out"] = nc.dram_tensor("out_0_dram", out_shape, _mybir.dt.float32, kind="ExternalOutput").ap()
    build(nc, args)
    r = _run(nc, [arrays], core_ids=[0])
    return r.results[0]["out_0_dram"]
```
